# Optimizing a Trainium2 kernel written in Bass

```python
import numpy as np
import jax
import jax.numpy as jnp

def _softmax(x, axis=-1):
    return jax.nn.softmax(x, axis=axis)

def _gelu(x):
    return jax.nn.gelu(x, approximate=True)

def _silu(x):
    return jax.nn.silu(x)

def _sigmoid(x):
    return jax.nn.sigmoid(x)

def _layernorm(x, axis=-1, eps=1e-05):
    m = jnp.mean(x, axis=axis, keepdims=True)
    v = jnp.var(x, axis=axis, keepdims=True)
    return (x - m) / jnp.sqrt(v + eps)

def _scatter_add(tgt, idx, src, axis=0):
    return tgt.at[idx].add(src)

def _segment_sum(src, seg, n):
    return jax.ops.segment_sum(src, seg, n)
kernel_name = 'mk_hybrid_d1_jaxref_r8_36182b'

def setup_inputs(seed: int=0):
    np.random.seed(seed)
    _w = jnp.asarray

    def _L0_attn_a_setup():
        import jax, jax.numpy as jnp
        import numpy as np
        import math
        B, T, D = (2, 512, 128)
        H = 16
        HEAD_DIM = D // H
        CHUNK = 64

        def chunked_attention(q, k, v, chunk_size, scale):
            Bq, Hq, Tq, hd = q.shape
            S = k.shape[2]
            nc = Tq // chunk_size
            q_chunks = q.reshape(Bq, Hq, nc, chunk_size, hd).transpose(2, 0, 1, 3, 4)
            starts = jnp.arange(nc, dtype=jnp.int32) * chunk_size
            k_pos = jnp.arange(S)

            def body(carry, xs):
                qc, start = xs
                scores = jnp.einsum('bhqd,bhkd->bhqk', qc, k) * scale
                q_pos = start + jnp.arange(chunk_size)
                causal_mask = k_pos[None, :] > q_pos[:, None]
                scores = jnp.where(causal_mask[None, None], -jnp.inf, scores)
                m = jnp.max(scores, axis=-1, keepdims=True)
                m = jnp.where(jnp.isinf(m), jnp.zeros_like(m), m)
                p = jax.nn.softmax(scores - m, axis=-1)
                oc = jnp.einsum('bhqk,bhkd->bhqd', p, v)
                return (carry, oc)
            _, outs = jax.lax.scan(body, None, (q_chunks, starts))
            return outs.transpose(1, 2, 0, 3, 4).reshape(Bq, Hq, Tq, hd)
        key = jax.random.key(seed)
        ks = jax.random.split(key, 9)
        s = 1.0 / math.sqrt(D)
        return {'x': jax.random.normal(ks[0], (B, T, D), dtype=jnp.float32), 'Wq': jax.random.normal(ks[1], (D, D), dtype=jnp.float32) * s, 'bq': jax.random.normal(ks[2], (D,), dtype=jnp.float32) * 0.01, 'Wk': jax.random.normal(ks[3], (D, D), dtype=jnp.float32) * s, 'bk': jax.random.normal(ks[4], (D,), dtype=jnp.float32) * 0.01, 'Wv': jax.random.normal(ks[5], (D, D), dtype=jnp.float32) * s, 'bv': jax.random.normal(ks[6], (D,), dtype=jnp.float32) * 0.01, 'Wo': jax.random.normal(ks[7], (D, D), dtype=jnp.float32) * s, 'bo': jax.random.normal(ks[8], (D,), dtype=jnp.float32) * 0.01}
    _L0_attn_a_in = _L0_attn_a_setup()

    def _L0_attn_b_setup():
        import jax, jax.numpy as jnp
        import numpy as np
        LANES = 4
        EPS = 1e-08

        def _rms_norm(z):
            return z * jax.lax.rsqrt(jnp.mean(z * z, axis=-1, keepdims=True) + EPS)

        def _combine(left, right, W):
            B, T, C = left.shape
            hd = C // LANES
            q = left.reshape(B, T, LANES, hd)
            k = right.reshape(B, T, LANES, hd)
            v = ((left + right) @ W).reshape(B, T, LANES, hd)
            scores = jnp.einsum('btld,btmd->btlm', q, k) * hd ** (-0.5)
            att = jax.nn.softmax(scores, axis=-1)
            z = jnp.einsum('btlm,btmd->btld', att, v)
            denom = (1.0 + jnp.arange(LANES, dtype=z.dtype))[None, None, :, None]
            z = _rms_norm(z) / denom
            return left + z.reshape(B, T, C)

        def _pscan2(x, W, identity):
            B, T, C = x.shape
            d = 1
            while d < T:
                ident = jnp.broadcast_to(identity.astype(x.dtype), (B, d, C))
                shifted = jnp.concatenate([ident, x[:, :-d]], axis=1)
                x = _combine(shifted, x, W)
                d *= 2
            return x

        def _reference_tuple_inner(x, W_up, W_v, W_proj, identity, W_scan_raw):
            U, _, Vt = jnp.linalg.svd(W_scan_raw, full_matrices=False)
            W = U @ Vt
            q = x @ W_up.T
            v = x @ W_v.T
            q = _pscan2(q, W, identity)
            Y = q * v @ W_proj.T
            return (Y, q)
        key = jax.random.key(seed)
        ks = jax.random.split(key, 6)
        B, T, C = (4, 256, 128)
        s = 0.02
        x = jax.random.normal(ks[0], (B, T, C), dtype=jnp.float32)
        W_up = jax.random.normal(ks[1], (C, C), dtype=jnp.float32) * s
        W_v = jax.random.normal(ks[2], (C, C), dtype=jnp.float32) * s
        W_proj = jax.random.normal(ks[3], (C, C), dtype=jnp.float32) * s
        identity = jax.random.uniform(ks[4], (C,), dtype=jnp.float32)
        W_scan_raw = jax.random.normal(ks[5], (C, C), dtype=jnp.float32) * s
        return {'x': x, 'W_up': W_up, 'W_v': W_v, 'W_proj': W_proj, 'identity': identity, 'W_scan_raw': W_scan_raw}
    _L0_attn_b_in = _L0_attn_b_setup()

    def _L0_ffn_setup():
        import jax, jax.numpy as jnp
        import numpy as np
        key = jax.random.key(seed)
        k1, k2, k3, k4 = jax.random.split(key, 4)
        B, T, M = (4, 256, 128)
        E, F = (16, 512)
        x = jax.random.normal(k1, (B, T, M), dtype=jnp.float32) * 0.02
        Wg = jax.random.normal(k2, (M, E), dtype=jnp.float32) * 0.02
        w1 = jax.random.normal(k3, (E, M, F), dtype=jnp.float32) * 0.02
        w2 = jax.random.normal(k4, (E, F, M), dtype=jnp.float32) * 0.02
        return {'x': x, 'Wg': Wg, 'w1': w1, 'w2': w2}
    _L0_ffn_in = _L0_ffn_setup()
    _d = {'L0_attn_a_x': _L0_attn_a_in['x'], 'L0_attn_a_Wq': _L0_attn_a_in['Wq'], 'L0_attn_a_bq': _L0_attn_a_in['bq'], 'L0_attn_a_Wk': _L0_attn_a_in['Wk'], 'L0_attn_a_bk': _L0_attn_a_in['bk'], 'L0_attn_a_Wv': _L0_attn_a_in['Wv'], 'L0_attn_a_bv': _L0_attn_a_in['bv'], 'L0_attn_a_Wo': _L0_attn_a_in['Wo'], 'L0_attn_a_bo': _L0_attn_a_in['bo'], 'L0_attn_b_W_up': _L0_attn_b_in['W_up'], 'L0_attn_b_W_v': _L0_attn_b_in['W_v'], 'L0_attn_b_W_proj': _L0_attn_b_in['W_proj'], 'L0_attn_b_identity': _L0_attn_b_in['identity'], 'L0_attn_b_W_scan_raw': _L0_attn_b_in['W_scan_raw'], 'L0_ffn_Wg': _L0_ffn_in['Wg'], 'L0_ffn_w1': _L0_ffn_in['w1'], 'L0_ffn_w2': _L0_ffn_in['w2']}
    _x0 = _d['L0_attn_a_x']
    _d['L0_attn_a_x'] = jax.random.normal(jax.random.fold_in(jax.random.key(seed), 1), (2, 2048, 128), dtype=_x0.dtype)
    del _x0
    return _d

def reference(L0_attn_a_x, L0_attn_a_Wq, L0_attn_a_bq, L0_attn_a_Wk, L0_attn_a_bk, L0_attn_a_Wv, L0_attn_a_bv, L0_attn_a_Wo, L0_attn_a_bo, L0_attn_b_W_up, L0_attn_b_W_v, L0_attn_b_W_proj, L0_attn_b_identity, L0_attn_b_W_scan_raw, L0_ffn_Wg, L0_ffn_w1, L0_ffn_w2):

    def _L0_attn_a_ref(x, Wq, bq, Wk, bk, Wv, bv, Wo, bo):
        import jax, jax.numpy as jnp
        import numpy as np
        import math
        B, T, D = (2, 512, 128)
        H = 16
        HEAD_DIM = D // H
        CHUNK = 64

        def chunked_attention(q, k, v, chunk_size, scale):
            Bq, Hq, Tq, hd = q.shape
            S = k.shape[2]
            nc = Tq // chunk_size
            q_chunks = q.reshape(Bq, Hq, nc, chunk_size, hd).transpose(2, 0, 1, 3, 4)
            starts = jnp.arange(nc, dtype=jnp.int32) * chunk_size
            k_pos = jnp.arange(S)

            def body(carry, xs):
                qc, start = xs
                scores = jnp.einsum('bhqd,bhkd->bhqk', qc, k) * scale
                q_pos = start + jnp.arange(chunk_size)
                causal_mask = k_pos[None, :] > q_pos[:, None]
                scores = jnp.where(causal_mask[None, None], -jnp.inf, scores)
                m = jnp.max(scores, axis=-1, keepdims=True)
                m = jnp.where(jnp.isinf(m), jnp.zeros_like(m), m)
                p = jax.nn.softmax(scores - m, axis=-1)
                oc = jnp.einsum('bhqk,bhkd->bhqd', p, v)
                return (carry, oc)
            _, outs = jax.lax.scan(body, None, (q_chunks, starts))
            return outs.transpose(1, 2, 0, 3, 4).reshape(Bq, Hq, Tq, hd)
        Bx, Tx, Dx = x.shape
        scale = 1.0 / math.sqrt(HEAD_DIM)

        def proj(W, b):
            y = x @ W.T + b
            return y.reshape(Bx, Tx, H, HEAD_DIM).transpose(0, 2, 1, 3)
        q = proj(Wq, bq)
        k = proj(Wk, bk)
        v = proj(Wv, bv)
        out = chunked_attention(q, k, v, CHUNK, scale)
        out = out.transpose(0, 2, 1, 3).reshape(Bx, Tx, Dx)
        return out @ Wo.T + bo

    def _L0_attn_b_ref(x, W_up, W_v, W_proj, identity, W_scan_raw):
        import jax, jax.numpy as jnp
        import numpy as np
        LANES = 4
        EPS = 1e-08

        def _rms_norm(z):
            return z * jax.lax.rsqrt(jnp.mean(z * z, axis=-1, keepdims=True) + EPS)

        def _combine(left, right, W):
            B, T, C = left.shape
            hd = C // LANES
            q = left.reshape(B, T, LANES, hd)
            k = right.reshape(B, T, LANES, hd)
            v = ((left + right) @ W).reshape(B, T, LANES, hd)
            scores = jnp.einsum('btld,btmd->btlm', q, k) * hd ** (-0.5)
            att = jax.nn.softmax(scores, axis=-1)
            z = jnp.einsum('btlm,btmd->btld', att, v)
            denom = (1.0 + jnp.arange(LANES, dtype=z.dtype))[None, None, :, None]
            z = _rms_norm(z) / denom
            return left + z.reshape(B, T, C)

        def _pscan2(x, W, identity):
            B, T, C = x.shape
            d = 1
            while d < T:
                ident = jnp.broadcast_to(identity.astype(x.dtype), (B, d, C))
                shifted = jnp.concatenate([ident, x[:, :-d]], axis=1)
                x = _combine(shifted, x, W)
                d *= 2
            return x

        def _reference_tuple_inner(x, W_up, W_v, W_proj, identity, W_scan_raw):
            U, _, Vt = jnp.linalg.svd(W_scan_raw, full_matrices=False)
            W = U @ Vt
            q = x @ W_up.T
            v = x @ W_v.T
            q = _pscan2(q, W, identity)
            Y = q * v @ W_proj.T
            return (Y, q)
        return _reference_tuple_inner(x, W_up, W_v, W_proj, identity, W_scan_raw)[0]

    def _L0_ffn_ref(x, Wg, w1, w2):
        import jax, jax.numpy as jnp
        import numpy as np
        d = x.shape[-1]
        xr = x.reshape(-1, d)
        S = xr.shape[0]
        E = Wg.shape[1]
        C = (S + E - 1) // E
        gate = jax.nn.softmax(xr @ Wg, axis=-1)
        idx = jnp.argmax(gate, axis=1)
        gates_s = jnp.take_along_axis(gate, idx[:, None], axis=1)[:, 0]
        onehot = jax.nn.one_hot(idx, E, dtype=jnp.int32)
        loc = jnp.sum((jnp.cumsum(onehot, axis=0) - 1) * onehot, axis=1)
        valid = loc < C
        loc_pad = jnp.minimum(loc, C)
        dispatched = jnp.zeros((E, C + 1, d), dtype=x.dtype).at[idx, loc_pad].set(xr)
        dispatched = dispatched[:, :C]
        h = jax.nn.relu(jnp.einsum('ecm,emf->ecf', dispatched, w1))
        expert_out = jnp.einsum('ecf,efm->ecm', h, w2)
        gathered = expert_out[idx, jnp.minimum(loc, C - 1)]
        combined = gathered * (gates_s * valid.astype(x.dtype))[:, None]
        return combined.reshape(x.shape)
    x = L0_attn_a_x
    x = x + _L0_attn_a_ref(_layernorm(x, axis=-1), L0_attn_a_Wq, L0_attn_a_bq, L0_attn_a_Wk, L0_attn_a_bk, L0_attn_a_Wv, L0_attn_a_bv, L0_attn_a_Wo, L0_attn_a_bo)
    x = x + _L0_ffn_ref(_layernorm(x, axis=-1), L0_ffn_Wg, L0_ffn_w1, L0_ffn_w2)
    x = x + _L0_attn_b_ref(_layernorm(x, axis=-1), L0_attn_b_W_up, L0_attn_b_W_v, L0_attn_b_W_proj, L0_attn_b_identity, L0_attn_b_W_scan_raw)
    x = x + _L0_ffn_ref(_layernorm(x, axis=-1), L0_ffn_Wg, L0_ffn_w1, L0_ffn_w2)
    return x

_drawn_inputs = setup_inputs


def setup_inputs(seed=0):
    import zlib

    import numpy as np

    out = dict(_drawn_inputs(seed))
    spreads = {}
    factors = {'L0_attn_a_bq': 8.0,
     'L0_attn_a_bk': 8.0,
     'L0_attn_a_bv': 4.523,
     'L0_attn_a_bo': 4.973,
     'L0_ffn_Wg': 4.555,
     'L0_ffn_w1': 5.394,
     'L0_ffn_w2': 4.448}
    for name, (base, spread) in spreads.items():
        noise = np.random.default_rng([zlib.crc32(name.encode()), seed]).standard_normal(out[name].shape)
        drawn = base * np.exp(spread * noise) if base else spread * noise
        out[name] = jnp.asarray(drawn.astype(out[name].dtype))
    for name, factor in factors.items():
        out[name] = (out[name] * factor).astype(out[name].dtype)
    return out
```

```python
import concourse.bass as bass
from concourse import mybir
from contextlib import ExitStack

fp32 = mybir.dt.float32
bf16 = mybir.dt.bfloat16
i32 = mybir.dt.int32
ALU = mybir.AluOpType
ACT = mybir.ActivationFunctionType
AX = mybir.AxisListType

P = 128
B, T, D = 2, 2048, 128
N = B * T
H = 16
HD = D // H
NT = N // P
EPS = 1e-5
MASKED = -1e30
LEAST = -3e38
NEWTON = (15 / 8, -10 / 8, 3 / 8)


class Steps:

    def __init__(self, engine, semaphore, base=0):
        self.engine, self.semaphore, self.base, self.n = engine, semaphore, base, 0

    def then(self, instruction):
        self.n += 1
        instruction.then_inc(self.semaphore, 1)
        self.engine.wait_ge(self.semaphore, self.base + self.n)


def stage_semaphores(nc, cx, prefix):
    taken = []
    cx.callback(nc.all_engine_barrier)
    cx.callback(nc.clear_and_free_semaphores, taken)

    def take(name):
        taken.append(nc.alloc_semaphore(name=prefix + name))
        return taken[-1]

    return take


def finish_stats(nc, steps, st, tmp, mean, var):
    mean_a, m2_a, mean_b, m2_b = st[:, :, 1], st[:, :, 2], st[:, :, 4], st[:, :, 5]
    s, d, m2, dd = (tmp[:, k, :] for k in range(4))
    nc.vector.tensor_tensor(s, mean_a, mean_b, ALU.add)
    nc.vector.tensor_tensor(m2, m2_a, m2_b, ALU.add)
    steps.then(nc.vector.tensor_tensor(d, mean_a, mean_b, ALU.subtract))
    steps.then(nc.vector.tensor_tensor(dd, d, d, ALU.mult))
    nc.vector.tensor_scalar(mean, s, 0.5, None, ALU.mult)
    steps.then(nc.vector.tensor_scalar(m2, m2, 1.0 / D, EPS, ALU.mult, ALU.add))
    steps.then(nc.vector.scalar_tensor_tensor(out=var, in0=dd, scalar=0.25, in1=m2, op0=ALU.mult, op1=ALU.add))


def project(nc, c, x, Wq, bq, Wk, bk, Wv, bv, Wo, bo, Wscan, q_parts, k_parts):
    CH = 512
    NCH = N // CH
    TC = CH // P
    NB = NT // B
    with ExitStack() as cx:
        def sb(name, shape, dt=fp32):
            return cx.enter_context(nc.sbuf_tensor(name, shape, dt))

        def ps(name, shape=(P, CH)):
            return cx.enter_context(nc.psum_tensor(name, list(shape), fp32))

        sem = stage_semaphores(nc, cx, "project_")

        W_nat = sb("W_nat", [P, 4, D])
        W_T = sb("W_T", [P, 3, D])
        bias_cols = sb("bias_cols", [P, 2])
        bv_rows = sb("bv_rows", [P, D])
        bo_rows = sb("bo_rows", [P, D])
        st = sb("st", [P, NT, 6])
        tmp = sb("tmp", [P, 4, NT])
        mean, var, std, rstd = (sb(n, [P, NT]) for n in ("mean", "var", "std", "rstd"))
        centred = [sb(f"centred{u}", [P, TC, D]) for u in range(2)]
        xn = [sb(f"xn{u}", [P, TC, D]) for u in range(2)]
        xnT = [sb(f"xnT{u}", [P, CH]) for u in range(2)]
        full = [sb(f"full{u}", [P, 2, CH]) for u in range(2)]
        rest = [sb(f"rest{u}", [P, 2, CH]) for u in range(2)]
        parts = [sb(f"parts{u}", [P, 2, 3, CH], bf16) for u in range(2)]
        squares = sb("squares", [P, D])
        norm = sb("norm", [P, 3])
        ones = sb("ones_f", [P, P])
        psT = [ps(f"psT{u}") for u in range(2)]
        psQK = [[ps(f"psQK{u}{a}") for a in range(2)] for u in range(2)]
        psV = [ps(f"psV{u}") for u in range(2)]

        x_loaded = [sem(f"x_loaded{b}") for b in range(B)]
        w_loaded, b_loaded, made = sem("w_loaded"), sem("b_loaded"), sem("made")
        wT_in_psum, wT_copied = sem("wT_in_psum"), sem("wT_copied")
        stats, stat_steps, std_done, rstd_done = sem("stats"), sem("stat_steps"), sem("std_done"), sem("rstd_done")
        centred_done, xn_ready = sem("centred_done"), sem("xn_ready")
        xT_in_psum, xT_copied, v_in_psum, v_done, full_done = (
            sem(n) for n in ("xT_in_psum", "xT_copied", "v_in_psum", "v_done", "full_done"))
        stored = [sem(f"stored{u}") for u in range(2)]
        qk_in_psum, rest_done, mid_done, lo_done = (
            sem(n) for n in ("qk_in_psum", "rest_done", "mid_done", "lo_done"))
        norm_act, norm_pe, norm_dve = sem("norm_act"), sem("norm_pe"), sem("norm_dve")
        resid_done = sem("resid_done")
        block = cx.enter_context(nc.Block())

        x_t = x.rearrange("(i p) d -> p i d", p=P)

        @block.sync
        def _(sp):
            for ch in range(NCH):
                sp.dma_start(c.X[:, ch * TC:(ch + 1) * TC, :], x_t[:, ch * TC:(ch + 1) * TC, :])\
                  .then_inc(x_loaded[ch // (NCH // B)], 16)
            for m, w in enumerate((Wq, Wk, Wv, Wo)):
                sp.dma_start(W_nat[:, m, :], w).then_inc(w_loaded, 16)
            sp.dma_start(c.S_nat[:], Wscan).then_inc(w_loaded, 16)
            for a, bias in enumerate((bq, bk)):
                sp.dma_start(bias_cols[:, a:a + 1], bias.rearrange("(p a) -> p a", a=1)).then_inc(b_loaded, 16)
            sp.dma_start(bv_rows[:], bv.rearrange("(a d) -> a d", a=1).broadcast_to([P, D])).then_inc(b_loaded, 16)
            sp.dma_start(bo_rows[:], bo.rearrange("(a d) -> a d", a=1).broadcast_to([P, D])).then_inc(b_loaded, 16)
            with sp.Fori(0, NCH // 2) as it:
                for u in range(2):
                    ch = it * 2 + u
                    sp.wait_ge(lo_done, ch * 2 + 2)
                    for a, dst in enumerate((q_parts, k_parts)):
                        sp.dma_start(dst.rearrange("a p t -> p a t")[:, :, bass.ds(ch * CH, CH)], parts[u][:, a, :, :])\
                          .then_inc(stored[u], 16)
            for u in range(2):
                sp.wait_ge(stored[u], 32 + 16 * NCH)

        @block.gpsimd
        def _(pool):
            for t, value in ((c.ident, 0.0), (c.ident_b, 0.0), (c.mask_b, 0.0), (c.mask_q, 0.0), (c.select, 0.0),
                             (ones, 1.0)):
                nc.gpsimd.memset(t[:], value).then_inc(made, 1)
            pool.wait_ge(made, 6)
            for m in (c.ident, c.ident_b):
                nc.gpsimd.affine_select(out=m[:], in_=m[:], compare_op=ALU.not_equal, fill=1.0, base=0,
                                        pattern=[[-1, P]], channel_multiplier=1).then_inc(made, 1)
            nc.gpsimd.affine_select(out=c.mask_b[:], in_=c.mask_b[:], compare_op=ALU.is_ge, fill=MASKED, base=0,
                                    pattern=[[-1, P]], channel_multiplier=1).then_inc(made, 1)
            nc.gpsimd.affine_select(out=c.mask_q[:], in_=c.mask_q[:], compare_op=ALU.is_ge, fill=MASKED, base=0,
                                    pattern=[[1, P]], channel_multiplier=-1).then_inc(made, 1)
            for g in range(4):
                pool.wait_ge(made, 10 + g)
                nc.gpsimd.affine_select(out=c.select[:], in_=c.select[:], compare_op=ALU.not_equal, fill=1.0,
                                        base=-32 * g, pattern=[[-1, HD + 1]], channel_multiplier=1).then_inc(made, 1)
            with pool.Fori(0, NCH // 2) as it:
                for u in range(2):
                    ch = it * 2 + u
                    pool.wait_ge(rstd_done, ch // (NCH // B) + 1)
                    sl = (slice(None), bass.ds(ch * TC, TC))
                    pool.wait_ge(xT_in_psum, ch + 1)
                    nc.gpsimd.tensor_tensor(centred[u][:], c.X[sl], mean[sl].unsqueeze(2).broadcast_to([P, TC, D]),
                                            ALU.subtract).then_inc(centred_done, 1)
                    pool.wait_ge(centred_done, ch + 1)
                    nc.gpsimd.tensor_tensor(xn[u][:], centred[u][:], rstd[sl].unsqueeze(2).broadcast_to([P, TC, D]),
                                            ALU.mult).then_inc(xn_ready, 1)
            pool.wait_ge(b_loaded, 64)
            pool.wait_ge(xn_ready, NCH)
            nc.gpsimd.tensor_tensor(c.X[:], c.X[:], bo_rows[:].unsqueeze(1).broadcast_to([P, NT, D]), ALU.add)\
              .then_inc(resid_done, 1)
            pool.wait_ge(resid_done, 1)

        @block.vector
        def _(dve):
            dve.sem_inc(v_done, 2)
            steps = Steps(dve, stat_steps)
            for b in range(B):
                half = slice(b * NB, (b + 1) * NB)
                dve.wait_ge(x_loaded[b], 16 * NCH // B)
                with dve.Fori(b * NB, (b + 1) * NB) as i:
                    nc.vector.bn_stats(st[:, bass.ds(i, 1), :], c.X[:, bass.ds(i, 1), :]).then_inc(stats, 1)
                dve.wait_ge(stats, (b + 1) * NB)
                finish_stats(nc, steps, st[:, half, :], tmp[:, :, half], mean[:, half], var[:, half])
                dve.wait_ge(std_done, b + 1)
                nc.vector.reciprocal(rstd[:, half], std[:, half]).then_inc(rstd_done, 1)
            dve.wait_ge(wT_in_psum, 1)
            nc.vector.tensor_copy(W_T[:].rearrange("p m d -> p (m d)"), psT[0][:, 0:3 * D]).then_inc(wT_copied, 1)
            nc.vector.tensor_copy(c.Wo_T[:], psT[0][:, 3 * D:]).then_inc(wT_copied, 1)
            dve.wait_ge(b_loaded, 64)
            with dve.Fori(0, NCH // 2) as it:
                for u in range(2):
                    ch = it * 2 + u
                    for a in range(2):
                        dve.wait_ge(full_done, ch * 2 + a + 5)
                        nc.vector.tensor_tensor(rest[u][:, a, :], full[u][:, a, :], parts[u][:, a, 0, :], ALU.subtract)\
                          .then_inc(rest_done, 1)
                        dve.wait_ge(rest_done, ch * 2 + a + 1)
                        nc.vector.tensor_copy(parts[u][:, a, 1, :], rest[u][:, a, :]).then_inc(mid_done, 1)
                        dve.wait_ge(mid_done, ch * 2 + a + 1)
                        nc.vector.tensor_tensor(parts[u][:, a, 2, :], rest[u][:, a, :], parts[u][:, a, 1, :],
                                                ALU.subtract).then_inc(lo_done, 1)
                    dve.wait_ge(v_in_psum, ch + 3)
                    nc.vector.tensor_tensor(c.V[:, :, bass.ds(ch, 1), :, :].rearrange("p h c i d -> p (c i) h d"),
                                            psV[u][:].rearrange("p (i h d) -> p i h d", i=TC, h=H),
                                            bv_rows[:].rearrange("p (h d) -> p h d", h=H).unsqueeze(1)
                                            .broadcast_to([P, TC, H, HD]), ALU.add).then_inc(v_done, 1)
            dve.wait_ge(norm_act, 2)
            nc.vector.reciprocal(norm[:, 2:3], norm[:, 1:2]).then_inc(norm_dve, 1)
            dve.wait_ge(norm_dve, 1)
            nc.vector.tensor_scalar(c.S[:, 0, :], c.S_nat[:], norm[:, 2:3], None, ALU.mult).then_inc(norm_dve, 1)
            dve.wait_ge(norm_pe, 2)
            nc.vector.tensor_copy(c.S[:, 1, :], psT[0][:, 0:D]).then_inc(norm_dve, 1)
            dve.wait_ge(norm_dve, 3)

        @block.scalar
        def _(act):
            act.sem_inc(xT_copied, 2)
            act.sem_inc(full_done, 4)
            act.wait_ge(w_loaded, 80)
            nc.scalar.activation(squares[:], c.S_nat[:], ACT.Square, accum_out=norm[:, 0:1]).then_inc(norm_act, 1)
            act.wait_ge(norm_pe, 1)
            nc.scalar.activation(norm[:, 1:2], psQK[0][0][:, 0:1], ACT.Sqrt).then_inc(norm_act, 1)
            for b in range(B):
                half = slice(b * NB, (b + 1) * NB)
                act.wait_ge(stat_steps, 4 * (b + 1))
                nc.scalar.activation(std[:, half], var[:, half], ACT.Sqrt).then_inc(std_done, 1)
            act.wait_ge(b_loaded, 64)
            with act.Fori(0, NCH // 2) as it:
                for u in range(2):
                    ch = it * 2 + u
                    act.wait_ge(xT_in_psum, ch + 3)
                    act.wait_ge(v_in_psum, ch + 1)
                    nc.scalar.activation(xnT[u][:], psT[u][:], ACT.Copy).then_inc(xT_copied, 1)
                    act.wait_ge(stored[u], it * 32 + 32)
                    for a in range(2):
                        act.wait_ge(qk_in_psum, ch * 2 + a + 1)
                        nc.scalar.activation(parts[u][:, a, 0, :], psQK[u][a][:], ACT.Identity,
                                             bias=bias_cols[:, a:a + 1])
                        nc.scalar.activation(full[u][:, a, :], psQK[u][a][:], ACT.Identity,
                                             bias=bias_cols[:, a:a + 1]).then_inc(full_done, 1)

        @block.tensor
        def _(pe):
            pe.sem_inc(xT_in_psum, 2)
            pe.sem_inc(v_in_psum, 2)
            for u in range(2):
                pe.sem_inc(stored[u], 32)
            pe.wait_ge(made, 8)
            pe.wait_ge(w_loaded, 80)
            for m in range(4):
                last = nc.tensor.transpose(psT[0][:, m * D:(m + 1) * D], W_nat[:, m, :], c.ident[:])
            last.then_inc(wT_in_psum, 1)
            pe.wait_ge(norm_act, 1)
            nc.tensor.matmul(psQK[0][0][:, 0:1], ones[:], norm[:, 0:1], start=True, stop=True).then_inc(norm_pe, 1)
            pe.wait_ge(norm_act, 2)
            pe.wait_ge(wT_copied, 2)
            with pe.Fori(0, NCH // 2) as it:
                for u in range(2):
                    ch = it * 2 + u
                    pe.wait_ge(xn_ready, ch + 1)
                    pe.wait_ge(xT_copied, ch + 1)
                    for i in range(TC):
                        last = nc.tensor.transpose(psT[u][:, i * P:(i + 1) * P], xn[u][:, i, :], c.ident[:])
                    last.then_inc(xT_in_psum, 1)
                    pe.wait_ge(xT_copied, ch + 3)
                    pe.wait_ge(full_done, ch * 2 + 2)
                    for a in range(2):
                        nc.tensor.matmul(psQK[u][a][:], W_T[:, a, :], xnT[u][:], start=True, stop=True)\
                          .then_inc(qk_in_psum, 1)
                    pe.wait_ge(v_done, ch + 1)
                    for i in range(TC):
                        last = nc.tensor.matmul(psV[u][:, i * D:(i + 1) * D], xnT[u][:, i * P:(i + 1) * P],
                                                W_T[:, 2, :], start=True, stop=True)
                    last.then_inc(v_in_psum, 1)
            pe.wait_ge(norm_dve, 2)
            pe.wait_ge(xT_copied, NCH + 2)
            nc.tensor.transpose(psT[0][:, 0:D], c.S[:, 0, :], c.ident[:]).then_inc(norm_pe, 1)


def constants(nc, cx, c):
    def sb(name, shape, dt=fp32):
        return cx.enter_context(nc.sbuf_tensor(name, shape, dt))
    c.ident = sb("ident", [P, P])
    c.ident_b = sb("ident_b", [P, P], bf16)
    c.S = sb("S_pair", [P, 2, D])


def attention_tensors(nc, cx, c):
    def sb(name, shape, dt=fp32):
        return cx.enter_context(nc.sbuf_tensor(name, shape, dt))
    c.mask_b = sb("mask_b", [P, P], bf16)
    c.mask_q = sb("mask_q", [P, P], bf16)
    c.select = sb("select", [P, HD + 1])
    c.X = sb("X", [P, NT, D])
    c.V = sb("V", [P, H, 8, 4, HD])
    c.Wo_T = sb("Wo_T", [P, D])
    c.A_out = sb("A_out", [P, NT // B, B * H, HD])
    c.S_nat = sb("S_nat", [P, D])


def attend(nc, c, q_parts, k_parts, max_dram):
    NH = B * H
    NQ = T // P
    G = 4
    QW = T // G
    SCALE = HD ** -0.5
    R = 3
    ROWS = P
    MROW = P - 2
    STEPS = [(g, kt) for g in range(G) for kt in range(4 * g + 4)]
    NS = len(STEPS)
    NBATCH = NS // 4
    GROUP_END = {g: sum(4 * f + 4 for f in range(g + 1)) // 4 - 1 for g in range(G)}
    MAXES = [(i, ck) for i in range(NQ) for ck in range(i // 4 + 1)]
    FIRST_MAXES = sum(i // 4 + 1 for i in range(NQ // 2))
    assert len(MAXES) == NS and FIRST_MAXES == 12

    with ExitStack() as cx:
        def sb(name, shape, dt=fp32):
            return cx.enter_context(nc.sbuf_tensor(name, shape, dt))

        def ps(name, shape=(P, 512), dt=fp32):
            return cx.enter_context(nc.psum_tensor(name, list(shape), dt))

        sem = stage_semaphores(nc, cx, "attend_")

        Q = [sb(f"Qs{r}", [ROWS, T], bf16) for r in range(R)]
        K = [sb(f"Ks{r}", [ROWS, T], bf16) for r in range(R)]
        Vp = [sb(f"Vp{r}", [P, NQ, 32]) for r in range(R)]
        probs = sb("probs", [P, 8, QW])
        probs0 = sb("probs0", [P, 4, QW])
        chunk_max = [sb(f"chunk_max{r}", [P, NQ, 4]) for r in range(R)]
        neg_max = [sb(f"neg_max{r}", [P, 2, NQ // 2]) for r in range(R)]
        neg_max_b = [sb(f"neg_max_b{r}", [P, 2, 2, NQ // 2], bf16) for r in range(R)]
        max_rows = [sb(f"max_rows{f}", [NQ, P], bf16) for f in range(2)]
        O_sb = [sb(f"O_sb{u}", [P, QW]) for u in range(2)]
        inv = sb("inv", [P, NQ])
        ones_row = sb("ones_row", [2, T], bf16)
        A = sb("A_newton", [P, D])
        A_b = sb("A_b", [P, D])
        Z = sb("Z_newton", [P, D])
        Y = sb("Y_newton", [P, D])
        a_ident = sb("a_ident", [P, D])
        b_tile = sb("b_tile", [P, D])
        ps_max = [ps(f"ps_max{u}") for u in range(R)]
        ps_s = [ps(f"ps_s{u}") for u in range(R)]
        ps_o = ps("ps_o")
        ps_misc = ps("ps_misc")
        comb3 = ps_misc[:, 0:16 * NQ].rearrange("p (i w) -> p i w", w=16)
        newton_ps = ps_misc[:, 256:512]
        rows_ps = ps_misc[0:NQ, 256:256 + P // 2].bitcast(bf16)

        stacks_loaded = [sem(f"stacks_loaded{r}") for r in range(R)]
        max_rows_loaded = [[sem(f"max_rows_loaded{r}{f}") for f in range(2)] for r in range(R)]
        max_rows_stored = [sem(f"max_rows_stored{f}") for f in range(2)]
        ones_loaded, made, v_staged = sem("ones_loaded"), sem("made_b"), sem("v_staged")
        max_scored, max_reduced = sem("max_scored"), sem("max_reduced")
        neg_max_steps = sem("neg_max_steps")
        rows_in_psum = sem("rows_in_psum")
        scored, exp_done, pv_done, o_copied = sem("scored"), sem("exp_done"), sem("pv_done"), sem("o_copied")
        combined, inv_done = sem("combined"), sem("inv_done")
        misc_read = sem("misc_read")
        newton_mm, newton_pool = sem("newton_mm"), sem("newton_pool")
        block = cx.enter_context(nc.Block())

        def sections(engine, section):
            section(-1, -1, 2, False, True)
            section(0, 0, 0, True, True)
            with engine.Fori(0, (NH - 2) // R) as it:
                for u in range(R):
                    section(it * R + (u + 1), it + (u + 1) // R, (u + 1) % R, True, True)
            section(NH - 1, (NH - 1) // R, (NH - 1) % R, True, False)

        def following(j, r):
            return (j + 1, 0) if r == R - 1 else (j, r + 1)

        def preceding(j, r):
            return (j - 1, R - 1) if r == 0 else (j, r - 1)

        def wait(engine, semaphore, value):
            if not isinstance(value, int) or value > 0:
                engine.wait_ge(semaphore, value)

        def reads(s, name, nxt=True):
            if not isinstance(s, int) or s > 0:
                order = ["rows1", "A", "comb", "Y", "rows0", "X", "end"]
                if not nxt:
                    order.remove("rows0")
                return s * 6 + order.index(name)
            return ["rows0 of head 0", "rows1", "A", "Y", "rows0", "X", "end"].index(name) if s == 0 else 0

        @block.sync
        def _(sp):
            def load(s, j, r):
                rows, cols = bass.ds(s % H * HD, HD), bass.ds(s // H * T, T)
                for stack, parts, order in ((Q[r], q_parts, (0, 0, 0, 1, 1, 2)), (K[r], k_parts, (0, 1, 2, 0, 1, 0))):
                    for row, a in enumerate(order):
                        sp.dma_start(stack[row * HD:(row + 1) * HD, :], parts[a, rows, cols])\
                          .then_inc(stacks_loaded[r], 16)

            def place_max_rows(s, j, r, f):
                if f:
                    sp.wait_ge(misc_read, reads(s, "rows1") + 1)
                else:
                    sp.wait_ge(misc_read, reads(s - 1, "rows0") + 1)
                sp.dma_start(max_dram[f], max_rows[f][:])\
                  .then_inc(max_rows_stored[f], 16)
                sp.wait_ge(max_rows_stored[f], s * 16 + 16)
                sp.dma_start(Q[r][MROW:, f * T // 2:(f + 1) * T // 2],
                             max_dram[f].rearrange("(a i) q -> a (i q)", a=2)).then_inc(max_rows_loaded[r][f], 16)

            def section(s, j, r):
                place_max_rows(s, j, r, 1)
                if not isinstance(s, int) or s < NH - 2:
                    sp.wait_ge(scored, s * NS)
                    load(s + 2, *following(*following(j, r)))
                if not isinstance(s, int) or s < NH - 1:
                    place_max_rows(s + 1, *following(j, r), 0)

            sp.wait_ge(made, 14)
            load(0, 0, 0)
            load(1, 0, 1)
            for r in range(R):
                sp.dma_start(K[r][MROW:, :], ones_row[:]).then_inc(ones_loaded, 16)
            place_max_rows(0, 0, 0, 0)
            place_max_rows(0, 0, 0, 1)
            load(2, 0, 2)
            place_max_rows(1, 0, 1, 0)
            with sp.Fori(0, (NH - 2) // R - 1) as it:
                for u in range(R):
                    section(it * R + (u + 1), it + (u + 1) // R, (u + 1) % R)
            for s in range(NH - 1 - R, NH):
                section(s, s // R, s % R)

        @block.gpsimd
        def _(pool):
            n = 0
            for t, value in [(t, 0.0) for t in Vp] + [(t, LEAST) for t in chunk_max] + [(probs0, 0.0), (ones_row, 1.0)] \
                    + [(t, 0.0) for t in Q + K]:
                nc.gpsimd.memset(t[:], value).then_inc(made, 1)
                n += 1
            pool.wait_ge(made, n)
            for t in Vp:
                nc.gpsimd.memset(t[:, :, HD:HD + 1], 1.0).then_inc(made, 1)
            nc.gpsimd.memset(b_tile[:], NEWTON[1])
            nc.gpsimd.tensor_scalar(a_ident[:], c.ident[:], NEWTON[0], None, ALU.mult).then_inc(made, 1)
            pool.wait_ge(made, n + R + 1)

            def section(s, j, r, exp, nxt):
                if nxt:
                    h, b = (s + 1) % H, (s + 1) // H
                    wait(pool, pv_done, (s - 1) * NBATCH + 1)
                    nc.gpsimd.tensor_copy(Vp[(r + 1) % R][:, :, 0:HD], c.V[:, bass.ds(h, 1), bass.ds(b * 4, 4), :, :]
                                          .rearrange("p h c i d -> p (h c i) d")).then_inc(v_staged, 1)
                if exp:
                    pool.wait_ge(misc_read, reads(s, "A") + 1)
                    nc.gpsimd.tensor_tensor(A_b[:], A[:], b_tile[:], ALU.mult).then_inc(newton_pool, 1)
                    pool.wait_ge(newton_pool, s * 2 + 1)
                    nc.gpsimd.tensor_tensor(Z[:], A_b[:], a_ident[:], ALU.add).then_inc(newton_pool, 1)

            sections(pool, section)

        @block.vector
        def _(dve):
            dve.wait_ge(made, 18)

            def negate_maxima(s, r, f):
                half = neg_max_b[r][:, f]
                nc.vector.tensor_reduce(neg_max[r][:, f, :], chunk_max[r][:, f * NQ // 2:(f + 1) * NQ // 2, :],
                                        axis=AX.X, op=ALU.max, negate=True).then_inc(neg_max_steps, 1)
                dve.wait_ge(neg_max_steps, s * 6 + (3 * f + 1))
                nc.vector.tensor_copy(half[:, 0, :], neg_max[r][:, f, :]).then_inc(neg_max_steps, 1)
                dve.wait_ge(neg_max_steps, s * 6 + (3 * f + 2))
                nc.vector.tensor_tensor(half[:, 1, :], neg_max[r][:, f, :], half[:, 0, :], ALU.subtract)\
                  .then_inc(neg_max_steps, 1)

            def normalise(s):
                dve.wait_ge(combined, s * G)
                nc.vector.reciprocal(inv[:], comb3[:, :, HD]).then_inc(inv_done, 1)
                dve.wait_ge(inv_done, s)
                nc.vector.tensor_tensor(c.A_out[:, :, bass.ds(s - 1, 1), :].rearrange("p i s d -> p i (s d)"),
                                        comb3[:, :, 0:HD], inv[:].unsqueeze(2).broadcast_to([P, NQ, HD]), ALU.mult)\
                  .then_inc(misc_read, 1)

            def newton(s):
                dve.wait_ge(newton_mm, s * 3 + 2)
                dve.wait_ge(newton_pool, s * 2 + 2)
                nc.vector.scalar_tensor_tensor(out=Y[:], in0=newton_ps[:, 0:D], scalar=NEWTON[2], in1=Z[:],
                                               op0=ALU.mult, op1=ALU.add).then_inc(misc_read, 1)

            def section(s, j, r, exp, nxt):
                first = isinstance(s, int) and s <= 0
                r1 = (r + 1) % R
                for k, (i, ck) in enumerate(MAXES if nxt else []):
                    dve.wait_ge(max_scored, (s + 1) * NS + (k + 1))
                    scores, out = ps_max[(k + r1) % R], chunk_max[r1][:, i, ck:ck + 1]
                    w = QW if ck < i // 4 else (i % 4 + 1) * P
                    nc.vector.tensor_reduce(out, scores[:, 0:w], axis=AX.X, op=ALU.max).then_inc(max_reduced, 1)
                    if k == FIRST_MAXES - 1:
                        dve.wait_ge(max_reduced, (s + 1) * NS + (k + 1))
                        negate_maxima(s + 1, r1, 0)
                        if exp and not first:
                            normalise(s)
                    if k == 15 and exp:
                        newton(s)
                if nxt:
                    dve.wait_ge(max_reduced, (s + 1) * NS + NS)
                    negate_maxima(s + 1, r1, 1)
                else:
                    normalise(s)
                    newton(s)

            sections(dve, section)
            normalise(NH)
            dve.wait_ge(misc_read, reads(NH - 1, "end", False) + 1)

        @block.scalar
        def _(act):
            act.wait_ge(made, 14)

            def copy_rows(s, j, r, f):
                act.wait_ge(rows_in_psum, s * 2 + (f + 1))
                wait(act, max_rows_stored[f], s * 16)
                nc.scalar.activation(max_rows[f][:], rows_ps, ACT.Copy).then_inc(misc_read, 1)

            def copy_group(s, g):
                batches = s * NBATCH + (GROUP_END[g] + 1)
                act.wait_ge(pv_done, batches)
                wait(act, combined, s * G + (g - 1))
                nc.scalar.activation(O_sb[g % 2][:], ps_o[:], ACT.Copy).then_inc(o_copied, 1)

            def section(s, j, r, exp, nxt):
                if not exp:
                    copy_rows(0, 0, 0, 0)
                    return
                first = isinstance(s, int) and s == 0
                for n in range(NBATCH):
                    wait(act, pv_done, {0: s * NBATCH - (NBATCH - 1), 1: s * NBATCH, 2: s * NBATCH}.get(n, s * NBATCH + (n - 1)))
                    for q in range(4):
                        k = 4 * n + q
                        g, kt = STEPS[k]
                        q0 = max(0, kt - 4 * g) * P
                        dst = (probs0[:, q, q0:] if n == 0 else probs[:, n % 2 * 4 + q, q0:])
                        act.wait_ge(scored, s * NS + (k + 1))
                        nc.scalar.activation(dst, ps_s[(k + r) % R][:, q0:], ACT.Exp, scale=SCALE).then_inc(exp_done, 1)
                    if n == 0:
                        copy_rows(s, j, r, 1)
                        if not first:
                            copy_group(s - 1, G - 1)
                    if n == 1:
                        act.wait_ge(newton_mm, s * 3 + 1)
                        nc.scalar.activation(A[:], newton_ps[:, 0:D], ACT.Copy).then_inc(misc_read, 1)
                    for g in range(G - 1):
                        if n == GROUP_END[g] + 1:
                            copy_group(s, g)
                    if n == 4 and nxt:
                        copy_rows(s + 1, *following(j, r), 0)
                    if n == 6:
                        act.wait_ge(newton_mm, s * 3 + 3)
                        nc.scalar.activation(c.S[:].rearrange("p a d -> p (a d)"), newton_ps, ACT.Copy)\
                          .then_inc(misc_read, 1)

            sections(act, section)
            copy_group(NH - 1, G - 1)

        @block.tensor
        def _(pe):
            pe.wait_ge(made, 18)

            def score(s, j, r, k):
                g, kt = STEPS[k]
                q0 = max(0, kt - 4 * g) * P
                if k == 0:
                    pe.wait_ge(max_rows_loaded[r][0], j * 16 + 16)
                if k == 12:
                    pe.wait_ge(max_rows_loaded[r][1], j * 16 + 16)
                wait(pe, exp_done, s * NS + (k - 2))
                diagonal = kt >= 4 * g
                last = nc.tensor.matmul(ps_s[(k + r) % R][:, q0:], K[r][:, kt * P:(kt + 1) * P],
                                        Q[r][:, g * QW + q0:(g + 1) * QW], start=True, stop=not diagonal)
                if diagonal:
                    last = nc.tensor.matmul(ps_s[(k + r) % R][:, q0:q0 + P], c.mask_b[:], c.ident_b[:], start=False, stop=True)
                last.then_inc(scored, 1)

            def score_for_max(s, j, r, k):
                i, ck = MAXES[k]
                w = QW if ck < i // 4 else (i % 4 + 1) * P
                if k == 0:
                    pe.wait_ge(stacks_loaded[r], j * 192 + 192)
                wait(pe, max_reduced, s * NS + (k - 2))
                diagonal = ck == i // 4
                last = nc.tensor.matmul(ps_max[(k + r) % R][:, 0:w], Q[r][0:MROW, i * P:(i + 1) * P],
                                        K[r][0:MROW, ck * QW:ck * QW + w], start=True, stop=not diagonal)
                if diagonal:
                    last = nc.tensor.matmul(ps_max[(k + r) % R][:, w - P:w], c.mask_q[:], c.ident_b[:], start=False,
                                            stop=True)
                last.then_inc(max_scored, 1)

            def products(s, r, n):
                pe.wait_ge(exp_done, s * NS + 4 * (n + 1))
                if n == 0:
                    pe.wait_ge(v_staged, s + 1)
                g = STEPS[4 * n][0]
                if STEPS[4 * n][1] == 0:
                    wait(pe, o_copied, s * G + g)
                for q in range(4):
                    kt = STEPS[4 * n + q][1]
                    q0 = max(0, kt - 4 * g) * P if n else 0
                    src = probs[:, n % 2 * 4 + q, q0:] if n else probs0[:, q, :]
                    last = nc.tensor.matmul(ps_o[32 * q:32 * q + 32, q0:], Vp[r][:, kt, :], src,
                                            start=kt < 4, stop=kt >= 4 * g)
                last.then_inc(pv_done, 1)

            def combine(s, g):
                pe.wait_ge(o_copied, s * G + (g + 1))
                for t in range(4):
                    last = nc.tensor.matmul(comb3[:, 4 * g + t, 0:HD + 1], O_sb[g % 2][:, t * P:(t + 1) * P], c.select[:],
                                            start=True, stop=True)
                last.then_inc(combined, 1)

            def turn_rows(s, r, f):
                pe.wait_ge(neg_max_steps, s * 6 + 3 * (f + 1))
                nc.tensor.transpose(rows_ps, neg_max_b[r][:, f].rearrange("p a i -> p (a i)"), c.ident_b[:])\
                  .then_inc(rows_in_psum, 1)

            def between(s, j, r, n, exp, nxt):
                first = isinstance(s, int) and s == 0
                j1, r1 = following(j, r)

                def misc(name):
                    wait(pe, misc_read, reads(s, name, nxt))

                if not exp:
                    if n == 4:
                        turn_rows(0, 0, 0)
                    return
                if n == 0:
                    misc("rows1")
                    turn_rows(s, r, 1)
                    if not first:
                        products(s - 1, (r - 1) % R, NBATCH - 1)
                else:
                    products(s, r, n - 1)
                if n == 1:
                    misc("A")
                    nc.tensor.matmul(newton_ps[:, 0:D], c.S[:, 0, :], c.S[:, 0, :], start=True, stop=True)\
                      .then_inc(newton_mm, 1)
                if n == 2 and not first:
                    misc("comb")
                    combine(s - 1, G - 1)
                if n == 3:
                    misc("Y")
                    combine(s, 0)
                    nc.tensor.matmul(newton_ps[:, 0:D], A[:], A[:], start=True, stop=True).then_inc(newton_mm, 1)
                if n == 4 and nxt:
                    misc("rows0")
                    turn_rows(s + 1, r1, 0)
                if n == 5:
                    misc("X")
                    combine(s, 1)
                if n == 6:
                    nc.tensor.matmul(newton_ps[:, 0:D], c.S[:, 1, :], Y[:], start=True, stop=True)
                    nc.tensor.matmul(newton_ps[:, D:], Y[:], c.S[:, 1, :], start=True, stop=True).then_inc(newton_mm, 1)
                if n == 8:
                    misc("end")
                    combine(s, 2)

            def section(s, j, r, exp, nxt):
                j1, r1 = following(j, r)
                for n in range(NBATCH):
                    for k in range(4 * n, 4 * n + 4):
                        if exp:
                            score(s, j, r, k)
                        if nxt:
                            score_for_max(s + 1, j1, r1, k)
                        if k == 4 * n + 1:
                            between(s, j, r, n, exp, nxt)

            pe.wait_ge(ones_loaded, 16 * R)
            sections(pe, section)
            products(NH - 1, (NH - 1) % R, NBATCH - 1)
            combine(NH - 1, G - 1)


def project_out(nc, c, dst):
    TC = 4
    NCH = NT // TC
    with ExitStack() as cx:
        sem = stage_semaphores(nc, cx, "project_out_")

        aT = [cx.enter_context(nc.sbuf_tensor(f"aT{u}", [P, TC * P], fp32)) for u in range(2)]
        y = [cx.enter_context(nc.sbuf_tensor(f"y_out{u}", [P, TC, D], fp32)) for u in range(2)]
        psT = [cx.enter_context(nc.psum_tensor(f"ps_aT{u}", [P, TC * P], fp32)) for u in range(2)]
        psY = [cx.enter_context(nc.psum_tensor(f"ps_y{u}", [P, TC * D], fp32)) for u in range(2)]
        aT_in_psum, aT_copied, y_in_psum, y_done = (sem(n) for n in ("aT_in_psum", "aT_copied", "y_in_psum", "y_done"))
        y_stored = [sem(f"y_stored{u}") for u in range(2)]
        block = cx.enter_context(nc.Block())
        dst_t = dst.rearrange("(i p) d -> p i d", p=P)

        @block.tensor
        def _(pe):
            def turn(ch):
                if ch >= 2:
                    pe.wait_ge(aT_copied, ch - 1)
                for t in range(ch * TC, (ch + 1) * TC):
                    b, i = divmod(t, NT // B)
                    last = nc.tensor.transpose(psT[ch % 2][:, t % TC * P:(t % TC + 1) * P],
                                               c.A_out[:, i, b * H:(b + 1) * H, :].rearrange("p h d -> p (h d)"), c.ident[:])
                last.then_inc(aT_in_psum, 1)

            turn(0)
            for ch in range(NCH):
                if ch + 1 < NCH:
                    turn(ch + 1)
                pe.wait_ge(aT_copied, ch + 1)
                if ch >= 2:
                    pe.wait_ge(y_done, ch - 1)
                for i in range(TC):
                    last = nc.tensor.matmul(psY[ch % 2][:, i * D:(i + 1) * D], aT[ch % 2][:, i * P:(i + 1) * P], c.Wo_T[:],
                                            start=True, stop=True)
                last.then_inc(y_in_psum, 1)

        @block.scalar
        def _(act):
            for ch in range(NCH):
                act.wait_ge(aT_in_psum, ch + 1)
                if ch >= 2:
                    act.wait_ge(y_in_psum, ch - 1)
                nc.scalar.activation(aT[ch % 2][:], psT[ch % 2][:], ACT.Copy).then_inc(aT_copied, 1)

        @block.vector
        def _(dve):
            for ch in range(NCH):
                dve.wait_ge(y_in_psum, ch + 1)
                if ch >= 2:
                    dve.wait_ge(y_stored[ch % 2], ch // 2 * 16)
                nc.vector.tensor_tensor(y[ch % 2][:].rearrange("p i d -> p (i d)"), psY[ch % 2][:],
                                        c.X[:, ch * TC:(ch + 1) * TC, :].rearrange("p i d -> p (i d)"), ALU.add)\
                  .then_inc(y_done, 1)

        @block.sync
        def _(sp):
            for ch in range(NCH):
                sp.wait_ge(y_done, ch + 1)
                sp.dma_start(dst_t[:, ch * TC:(ch + 1) * TC, :], y[ch % 2][:]).then_inc(y_stored[ch % 2], 16)
            for u in range(2):
                sp.wait_ge(y_stored[u], NCH // 2 * 16)


E_ = 16
F = 512
CAP = (N + E_ - 1) // E_
ROW = D + 2
RANK_STEP, COUNT_STEP = 9, 11


def moe(nc, c, name, x, Wg, w1, w2, dispatched, routed):
    J = NT
    TC = 4
    NCH = J // TC
    S2 = CAP // P
    FT = F // P
    with ExitStack() as cx:
        def sb(n, shape, dt=fp32):
            return cx.enter_context(nc.sbuf_tensor(f"{name}_{n}", shape, dt))

        def ps(n, shape):
            return cx.enter_context(nc.psum_tensor(f"{name}_{n}", shape, fp32))

        sem = stage_semaphores(nc, cx, f"{name}_")

        X = sb("x", [P, J, D])
        Wg_sb = sb("Wg", [P, E_])
        st = sb("st", [P, J, 6])
        tmp = sb("tmp", [P, 4, J])
        mean, var, std, rstd = (sb(n, [P, J]) for n in ("mean", "var", "std", "rstd"))
        xs = [sb(f"xs{u}", [P, TC, D]) for u in range(2)]
        xsT = [sb(f"xsT{u}", [P, TC * P]) for u in range(2)]
        rows = sb("rows", [P, J, ROW])
        logits = sb("logits", [P, J, E_])
        best = sb("best", [P, J])
        work = sb("work", [P, J, E_])
        expd = sb("expd", [P, J, E_])
        weight = sb("weight", [P, J, E_])
        rank = sb("rank", [P, J])
        onehot = sb("onehot", [P, E_, J])
        restart = sb("restart", [P, E_, J])
        count = sb("count", [P, E_, J])
        place = sb("place", [P, E_, J])
        token = sb("token", [P, J])
        small = sb("small", [P, 8, J])
        slot_i = sb("slot_i", [P, J], i32)
        before = sb("before", [P, P])
        blank = sb("blank", [P, J, ROW])
        w1_sb = [sb(f"w1_{u}", [P, F]) for u in range(2)]
        w2_sb = [sb(f"w2_{u}", [P, FT, D]) for u in range(2)]
        d_sb = [sb(f"d{u}", [P, S2, ROW]) for u in range(2)]
        dT = [sb(f"dT{u}", [P, CAP]) for u in range(2)]
        hT = [sb(f"hT{u}", [P, FT, CAP]) for u in range(2)]
        y = [sb(f"y{u}", [P, S2, D]) for u in range(2)]
        to_row = [sb(f"to_row{u}", [P, S2], i32) for u in range(2)]
        psD = [ps(f"psD{u}", [P, 512]) for u in range(2)]
        psH = [ps(f"psH{u}", [P, 1024]) for u in range(2)]
        psY = [ps(f"psY{u}", [P, 512]) for u in range(2)]

        x_loaded, wg_loaded, made, blanked, blank_made = (sem(n) for n in ("x_loaded", "wg_loaded", "made", "blanked", "blank_made"))
        stats, steps_done, std_done = sem("stats"), sem("steps"), sem("std_done")
        xs_in_psum, xsT_copied, logits_in_psum, logits_copied = (
            sem(n) for n in ("xs_in_psum", "xsT_copied", "logits_in_psum", "logits_copied"))
        xs_ready, rows_copied, exp_done, base_in_psum = sem("xs_ready"), sem("rows_copied"), sem("exp_done"), sem("base")
        slots_ready, scattered = sem("slots_ready"), sem("scattered")
        e_loaded = [sem(f"e_loaded{u}") for u in range(2)]
        d_in_psum, d_copied, h_in_psum, h_act, h_dve, y_in_psum, y_done, ids_done = (
            sem(n) for n in ("d_in_psum", "d_copied", "h_in_psum", "h_act", "h_dve", "y_in_psum", "y_done", "ids_done"))
        y_sent = [sem(f"y_sent{u}") for u in range(2)]
        block = cx.enter_context(nc.Block())

        def experts(engine, expert):
            for u in range(2):
                expert(u, 0, u, True, False)
            with engine.Fori(1, E_ // 2 - 1) as i:
                for u in range(2):
                    expert(i * 2 + u, i, u, False, False)
            for u in range(2):
                expert(E_ - 2 + u, E_ // 2 - 1, u, False, True)

        @block.sync
        def _(sp):
            xv = x.rearrange("(p j) d -> p j d", j=J)
            for k in range(4):
                sl = slice(k * J // 4, (k + 1) * J // 4)
                sp.dma_start(X[:, sl, :], xv[:, sl, :]).then_inc(x_loaded, 16)
            sp.dma_start(Wg_sb[:], Wg).then_inc(wg_loaded, 16)
            sp.wait_ge(blank_made, 2)
            sp.dma_start(dispatched[0:N, :].rearrange("(p j) w -> p j w", j=J), blank[:]).then_inc(blanked, 16)
            sp.dma_start(routed[0:N, :].rearrange("(p j) w -> p j w", j=J), blank[:, :, 0:D]).then_inc(blanked, 16)

            def load_weights(e, u):
                sp.dma_start(w1_sb[u][:], w1[bass.ds(e, 1), :, :].rearrange("e m f -> m (e f)")).then_inc(e_loaded[u], 16)
                sp.dma_start(w2_sb[u][:], w2[bass.ds(e, 1), :, :].rearrange("e (f p) m -> p (e f) m", p=P))\
                  .then_inc(e_loaded[u], 16)

            def load_rows(e, u):
                sp.dma_start(d_sb[u][:], dispatched[bass.ds(e * CAP, CAP), :].rearrange("(s p) w -> p s w", p=P))\
                  .then_inc(e_loaded[u], 16)

            for u in range(2):
                load_weights(u, u)
            sp.wait_ge(scattered, 16 * J)
            for u in range(2):
                load_rows(u, u)

            def expert(e, i, u, first, last):
                if not last:
                    sp.wait_ge(y_done, (e + 1) * S2)
                    load_weights(e + 2, u)
                    load_rows(e + 2, u)

            experts(sp, expert)

        @block.gpsimd
        def _(pool):
            nc.gpsimd.memset(blank[:], 0.0).then_inc(blank_made, 1)
            nc.gpsimd.memset(restart[:], 1.0).then_inc(made, 1)
            nc.gpsimd.memset(before[:], 1.0).then_inc(made, 1)
            nc.gpsimd.iota(weight[:], pattern=[[0, J], [-1, E_]], base=E_, channel_multiplier=0,
                           allow_small_or_imprecise_dtypes=True).then_inc(made, 1)
            nc.gpsimd.iota(token[:], pattern=[[1, J]], base=0, channel_multiplier=J,
                           allow_small_or_imprecise_dtypes=True).then_inc(made, 1)
            pool.wait_ge(blank_made, 1)
            pool.wait_ge(made, 4)
            nc.gpsimd.iota(blank[:, :, D:D + 1], pattern=[[1, J]], base=N, channel_multiplier=J,
                           allow_small_or_imprecise_dtypes=True).then_inc(blank_made, 1)
            nc.gpsimd.memset(restart[:, :, 0:1], 0.0).then_inc(made, 1)
            nc.gpsimd.affine_select(out=before[:], in_=before[:], compare_op=ALU.is_gt, fill=0.0, base=0,
                                    pattern=[[1, P]], channel_multiplier=-1).then_inc(made, 1)
            with pool.Fori(0, NCH // 2) as it:
                for u in range(2):
                    ch = it * 2 + u
                    pool.wait_ge(xs_ready, (ch + 1) * TC)
                    nc.gpsimd.tensor_copy(rows[:, bass.ds(ch * TC, TC), 0:D], xs[u][:]).then_inc(rows_copied, 1)
            pool.wait_ge(rows_copied, NCH + 2)
            pool.wait_ge(slots_ready, 3)
            pool.wait_ge(blanked, 32)
            for j in range(J):
                pool.indirect_dma_start(dispatched, bass.IndirectOffsetOnAxis(ap=slot_i[:, j:j + 1], axis=0),
                                        rows[:, j, :], None).then_inc(scattered, 16)

            for e in range(E_):
                pool.wait_ge(ids_done, e + 1)
                for s in range(S2):
                    pool.wait_ge(y_done, e * S2 + s + 1)
                    pool.indirect_dma_start(routed, bass.IndirectOffsetOnAxis(ap=to_row[e % 2][:, s:s + 1], axis=0),
                                            y[e % 2][:, s, :], None).then_inc(y_sent[e % 2], 16)
            for u in range(2):
                pool.wait_ge(y_sent[u], E_ // 2 * S2 * 16)

        @block.vector
        def _(dve):
            dve.sem_inc(logits_copied, 2)
            steps = Steps(dve, steps_done)
            dve.wait_ge(x_loaded, 64)
            with dve.Fori(0, J) as j:
                nc.vector.bn_stats(st[:, bass.ds(j, 1), :], X[:, bass.ds(j, 1), :]).then_inc(stats, 1)
            dve.wait_ge(stats, J)
            finish_stats(nc, steps, st, tmp, mean[:], var[:])
            dve.wait_ge(std_done, 1)
            steps.then(nc.vector.reciprocal(rstd[:], std[:]))
            with dve.Fori(0, NCH // 2) as it:
                for u in range(2):
                    ch = it * 2 + u
                    dve.wait_ge(xs_in_psum, ch + 1)
                    dve.wait_ge(rows_copied, ch + 1)
                    for i in range(TC):
                        j = ch * TC + i
                        nc.vector.tensor_scalar(xs[u][:, i, :], X[:, bass.ds(j, 1), :].rearrange("p o d -> p (o d)"),
                                                mean[:, bass.ds(j, 1)], rstd[:, bass.ds(j, 1)], ALU.subtract, ALU.mult)\
                          .then_inc(xs_ready, 1)
                    dve.wait_ge(logits_in_psum, ch + 3)
                    nc.vector.tensor_copy(logits[:, bass.ds(ch * TC, TC), :].rearrange("p j e -> p (j e)"),
                                          psD[u][:, 0:TC * E_]).then_inc(logits_copied, 1)
            dve.wait_ge(logits_copied, NCH + 2)
            dve.wait_ge(made, 6)
            per_token = [P, J, E_]
            steps.then(nc.vector.tensor_reduce(best[:], logits[:], axis=AX.X, op=ALU.max))
            best_b = best[:].unsqueeze(2).broadcast_to(per_token)
            steps.then(nc.vector.tensor_tensor(work[:], logits[:], best_b, ALU.is_equal))
            nc.vector.tensor_tensor(expd[:], logits[:], best_b, ALU.subtract).then_inc(slots_ready, 1)
            steps.then(nc.vector.tensor_tensor(work[:], work[:], weight[:], ALU.mult))
            steps.then(nc.vector.tensor_reduce(rank[:], work[:], axis=AX.X, op=ALU.max))
            steps.then(nc.vector.tensor_tensor(onehot[:].rearrange("p e j -> p j e"), weight[:],
                                               rank[:].unsqueeze(2).broadcast_to(per_token), ALU.is_equal))
            steps.then(nc.vector.tensor_tensor_scan(out=count[:].rearrange("p e j -> p (e j)"),
                                                    data0=restart[:].rearrange("p e j -> p (e j)"),
                                                    data1=onehot[:].rearrange("p e j -> p (e j)"), initial=0.0,
                                                    op0=ALU.mult, op1=ALU.add))
            after_count = steps.n
            assert after_count == COUNT_STEP
            dve.wait_ge(base_in_psum, 1)
            steps.then(nc.vector.tensor_tensor(place[:], count[:], psD[0][:, 0:E_].unsqueeze(2).broadcast_to([P, E_, J]),
                                               ALU.add))
            steps.then(nc.vector.tensor_tensor(place[:], place[:], onehot[:], ALU.mult))
            loc1, valid, first_slot, slot, trash, diff, dest, total = (small[:, k, :] for k in range(8))
            steps.then(nc.vector.tensor_reduce(loc1, place[:].rearrange("p e j -> p j e"), axis=AX.X, op=ALU.add))
            nc.vector.tensor_scalar(valid, loc1, float(CAP), None, ALU.is_le)
            nc.vector.tensor_scalar(trash, token[:], float(N), None, ALU.add)
            steps.then(nc.vector.tensor_scalar(first_slot, rank[:], -float(CAP), float(E_ * CAP - 1), ALU.mult, ALU.add))
            steps.then(nc.vector.tensor_tensor(slot, first_slot, loc1, ALU.add))
            steps.then(nc.vector.tensor_tensor(diff, slot, trash, ALU.subtract))
            steps.then(nc.vector.tensor_tensor(slot, diff, valid, ALU.mult))
            steps.then(nc.vector.tensor_tensor(dest, slot, trash, ALU.add))
            nc.vector.tensor_copy(slot_i[:], dest).then_inc(slots_ready, 1)
            nc.vector.tensor_copy(rows[:, :, D], token[:])
            dve.wait_ge(exp_done, 1)
            steps.then(nc.vector.tensor_reduce(total, work[:], axis=AX.X, op=ALU.add))
            nc.vector.reciprocal(rows[:, :, D + 1], total).then_inc(slots_ready, 1)

            def expert(e, i, u, first, last):
                dve.wait_ge(e_loaded[u], i * 48 + 48)
                if not first:
                    dve.wait_ge(y_sent[u], i * 32)
                nc.vector.tensor_copy(to_row[u][:], d_sb[u][:, :, D]).then_inc(ids_done, 1)
                dve.wait_ge(h_in_psum, e * 2 + 2)
                nc.vector.tensor_scalar(hT[u][:, FT // 2:, :].rearrange("p f s -> p (f s)"), psH[u][:, F:], 0.0, None,
                                        ALU.max).then_inc(h_dve, 1)
                dve.wait_ge(y_in_psum, e + 1)
                for s in range(S2):
                    nc.vector.tensor_scalar(y[u][:, s, :], psY[u][:, s * D:(s + 1) * D], d_sb[u][:, s, D + 1:D + 2], None,
                                            ALU.mult).then_inc(y_done, 1)

            experts(dve, expert)

        @block.scalar
        def _(act):
            act.sem_inc(xsT_copied, 2)
            act.wait_ge(steps_done, 4)
            nc.scalar.activation(std[:], var[:], ACT.Sqrt).then_inc(std_done, 1)
            with act.Fori(0, NCH // 2) as it:
                for u in range(2):
                    ch = it * 2 + u
                    act.wait_ge(xs_in_psum, ch + 3)
                    act.wait_ge(logits_in_psum, ch + 1)
                    nc.scalar.activation(xsT[u][:], psH[u][:, 0:TC * P], ACT.Copy).then_inc(xsT_copied, 1)
            act.wait_ge(slots_ready, 1)
            act.wait_ge(steps_done, RANK_STEP)
            nc.scalar.activation(work[:], expd[:], ACT.Exp).then_inc(exp_done, 1)

            def expert(e, i, u, first, last):
                act.wait_ge(d_in_psum, e + 1)
                nc.scalar.activation(dT[u][:], psD[u][:, 0:CAP], ACT.Copy).then_inc(d_copied, 1)
                act.wait_ge(h_in_psum, e * 2 + 1)
                nc.scalar.activation(hT[u][:, 0:FT // 2, :].rearrange("p f s -> p (f s)"), psH[u][:, 0:F], ACT.Relu)\
                   .then_inc(h_act, 1)

            experts(act, expert)

        @block.tensor
        def _(pe):
            pe.sem_inc(xs_in_psum, 2)
            pe.sem_inc(logits_in_psum, 2)
            pe.sem_inc(rows_copied, 2)
            pe.wait_ge(wg_loaded, 16)
            with pe.Fori(0, NCH // 2) as it:
                for u in range(2):
                    ch = it * 2 + u
                    pe.wait_ge(xs_ready, (ch + 1) * TC)
                    pe.wait_ge(xsT_copied, ch + 1)
                    for i in range(TC):
                        last = nc.tensor.transpose(psH[u][:, i * P:(i + 1) * P], xs[u][:, i, :], c.ident[:])
                    last.then_inc(xs_in_psum, 1)
                    pe.wait_ge(xsT_copied, ch + 3)
                    pe.wait_ge(logits_copied, ch + 1)
                    for i in range(TC):
                        last = nc.tensor.matmul(psD[u][:, i * E_:(i + 1) * E_], xsT[u][:, i * P:(i + 1) * P], Wg_sb[:],
                                                start=True, stop=True)
                    last.then_inc(logits_in_psum, 1)
            pe.wait_ge(steps_done, COUNT_STEP)
            pe.wait_ge(made, 6)
            nc.tensor.matmul(psD[0][:, 0:E_], before[:], count[:, :, J - 1], start=True, stop=True).then_inc(base_in_psum, 1)
            pe.wait_ge(steps_done, COUNT_STEP + 1)

            def up(e, i, u):
                pe.wait_ge(e_loaded[u], i * 48 + 48)
                for s in range(S2):
                    last = nc.tensor.transpose(psD[u][:, s * P:(s + 1) * P], d_sb[u][:, s, 0:D], c.ident[:])
                last.then_inc(d_in_psum, 1)
                pe.wait_ge(d_copied, e + 1)
                for f in range(FT):
                    last = nc.tensor.matmul(psH[u][:, f * CAP:(f + 1) * CAP], w1_sb[u][:, f * P:(f + 1) * P], dT[u][:],
                                            start=True, stop=True)
                    if f % 2:
                        last.then_inc(h_in_psum, 1)

            def down(e, i, u):
                pe.wait_ge(h_act, e + 1)
                pe.wait_ge(h_dve, e + 1)
                for s in range(S2):
                    for f in range(FT):
                        last = nc.tensor.matmul(psY[u][:, s * D:(s + 1) * D], hT[u][:, f, s * P:(s + 1) * P],
                                                w2_sb[u][:, f, :], start=f == 0, stop=f == FT - 1)
                last.then_inc(y_in_psum, 1)

            up(0, 0, 0)

            def expert(e, i, u, first, last):
                if not (last and u):
                    up(e + 1, i + 1 if u else i, 1 - u)
                down(e, i, u)

            experts(pe, expert)


LANES = 4
W_LANE = D // LANES
SC = 4
CW = N // SC // P
SHIFTS = [1 << k for k in range(T.bit_length() - 1)]
PAD = SHIFTS[-1]
RMS_EPS = 1e-8


def scan_tensors(nc, cx, c):
    def sb(name, shape, dt=fp32):
        return cx.enter_context(nc.sbuf_tensor(name, shape, dt))
    c.X2 = sb("X2", [P, SC, CW, D])
    c.q = sb("q", [P, SC, CW, D])
    c.v2 = sb("v2", [P, SC, CW, D])
    c.Wproj_T = sb("Wproj_T", [P, D])
    c.L = [sb(f"L{ch}", [P, CW, D]) for ch in range(SC)]
    c.U = [sb(f"U{u}", [P, CW, D]) for u in range(2)]
    c.UT = [sb(f"UT{u}", [P, CW * P]) for u in range(2)]


def token_rows(t, ch):
    return t.rearrange("(c p j) d -> p c j d", c=SC, j=CW)[:, bass.ds(ch, 1), :, :].rearrange("p c j d -> p (c j) d")


def padded_rows(t, ch, shift=0):
    first = ch // (SC // B) * (PAD + T) + PAD + ch % (SC // B) * (CW * P) - shift
    return t[first:first + CW * P, :].rearrange("(p j) d -> p j d", j=CW)


def scan_inputs(nc, c, x1, routed, W_up, W_v, W_proj, identity, scanned):
    with ExitStack() as cx:
        def sb(name, shape, dt=fp32):
            return cx.enter_context(nc.sbuf_tensor(name, shape, dt))

        def ps(name):
            return cx.enter_context(nc.psum_tensor(name, [P, CW * P], fp32))

        sem = stage_semaphores(nc, cx, "scan_inputs_")

        W_nat = sb("Wb_nat", [P, 3, D])
        W_T = sb("Wb_T", [P, 2, D])
        st = sb("st_b", [P, NT, 6])
        tmp = sb("tmp_b", [P, 4, NT])
        mean, var, std, rstd = (sb(n, [P, NT]) for n in ("mean_b", "var_b", "std_b", "rstd_b"))
        ident_row = sb("ident_row", [P, D])
        psT, psQ, psV = ps("psT_b"), ps("psQ_b"), ps("psV_b")

        loaded = [sem(f"loaded{ch}") for ch in range(SC)]
        w_loaded, identity_loaded, padded, q_stored = sem("w_loaded"), sem("identity_loaded"), sem("padded"), sem("q_stored")
        summed, stats, stat_steps, std_done, rstd_done = (
            sem(n) for n in ("summed", "stats", "stat_steps", "std_done", "rstd_done"))
        wT_in_psum, wT_copied = sem("wT_in_psum"), sem("wT_copied")
        xn_ready, xT_in_psum, xT_copied, q_in_psum, v_in_psum, q_copied, v_copied = (
            sem(n) for n in ("xn_ready", "xT_in_psum", "xT_copied", "q_in_psum", "v_in_psum", "q_copied", "v_copied"))
        block = cx.enter_context(nc.Block())

        @block.sync
        def _(sp):
            for ch in range(SC):
                sp.dma_start(c.X2[:, ch], token_rows(x1, ch)).then_inc(loaded[ch], 16)
                sp.dma_start(c.L[ch][:], token_rows(routed, ch)).then_inc(loaded[ch], 16)
            for m, w in enumerate((W_up, W_v, W_proj)):
                sp.dma_start(W_nat[:, m, :], w).then_inc(w_loaded, 16)
            sp.dma_start(ident_row[:], identity.rearrange("(a d) -> a d", a=1).broadcast_to([P, D]))\
              .then_inc(identity_loaded, 16)
            sp.wait_ge(identity_loaded, 16)
            for t in scanned:
                for b in range(B):
                    pads = t[b * (PAD + T):b * (PAD + T) + PAD, :].rearrange("(p j) d -> p j d", j=PAD // P)
                    sp.dma_start(pads, ident_row[:].unsqueeze(1).broadcast_to([P, PAD // P, D])).then_inc(padded, 16)
            for ch in range(SC):
                sp.wait_ge(q_copied, ch + 1)
                sp.dma_start(padded_rows(scanned[0], ch), c.q[:, ch]).then_inc(q_stored, 16)
            sp.wait_ge(padded, 16 * B * len(scanned))
            sp.wait_ge(q_stored, 16 * SC)

        @block.gpsimd
        def _(pool):
            for ch in range(SC):
                pool.wait_ge(loaded[ch], 32)
                nc.gpsimd.tensor_tensor(c.X2[:, ch], c.X2[:, ch], c.L[ch][:], ALU.add).then_inc(summed, 1)

        @block.vector
        def _(dve):
            dve.wait_ge(wT_in_psum, 1)
            nc.vector.tensor_copy(W_T[:].rearrange("p m d -> p (m d)"), psT[:, 0:2 * D]).then_inc(wT_copied, 1)
            nc.vector.tensor_copy(c.Wproj_T[:], psT[:, 2 * D:3 * D]).then_inc(wT_copied, 1)
            tiles = c.X2[:].rearrange("p c j d -> p (c j) d")
            with dve.Fori(0, SC) as ch:
                dve.wait_ge(summed, ch + 1)
                for j in range(CW):
                    i = ch * CW + j
                    nc.vector.bn_stats(st[:, bass.ds(i, 1), :], tiles[:, bass.ds(i, 1), :]).then_inc(stats, 1)
            dve.wait_ge(stats, NT)
            finish_stats(nc, Steps(dve, stat_steps), st, tmp, mean[:], var[:])
            dve.wait_ge(std_done, 1)
            nc.vector.reciprocal(rstd[:], std[:]).then_inc(rstd_done, 1)
            dve.wait_ge(rstd_done, 1)
            for ch in range(SC + 1):
                if ch < SC:
                    if ch >= 2:
                        dve.wait_ge(xT_in_psum, ch - 1)
                    for j in range(CW):
                        i = ch * CW + j
                        last = nc.vector.tensor_scalar(c.U[ch % 2][:, j, :], c.X2[:, ch, j, :], mean[:, i:i + 1],
                                                       rstd[:, i:i + 1], ALU.subtract, ALU.mult)
                    last.then_inc(xn_ready, 1)
                if ch > 0:
                    dve.wait_ge(v_in_psum, ch)
                    nc.vector.tensor_copy(c.v2[:, ch - 1].rearrange("p j d -> p (j d)"), psV[:]).then_inc(v_copied, 1)
            dve.wait_ge(v_copied, SC)

        @block.scalar
        def _(act):
            act.wait_ge(stat_steps, 4)
            nc.scalar.activation(std[:], var[:], ACT.Sqrt).then_inc(std_done, 1)
            for ch in range(SC):
                act.wait_ge(xT_in_psum, ch + 1)
                if ch >= 2:
                    act.wait_ge(v_in_psum, ch - 1)
                nc.scalar.activation(c.UT[ch % 2][:], psT[:], ACT.Copy).then_inc(xT_copied, 1)
                act.wait_ge(q_in_psum, ch + 1)
                nc.scalar.activation(c.q[:, ch].rearrange("p j d -> p (j d)"), psQ[:], ACT.Copy).then_inc(q_copied, 1)

        @block.tensor
        def _(pe):
            pe.wait_ge(w_loaded, 48)
            for m in range(3):
                last = nc.tensor.transpose(psT[:, m * D:(m + 1) * D], W_nat[:, m, :], c.ident[:])
            last.then_inc(wT_in_psum, 1)
            pe.wait_ge(wT_copied, 2)
            for ch in range(SC):
                pe.wait_ge(xn_ready, ch + 1)
                if ch >= 1:
                    pe.wait_ge(xT_copied, ch)
                for j in range(CW):
                    last = nc.tensor.transpose(psT[:, j * P:(j + 1) * P], c.U[ch % 2][:, j, :], c.ident[:])
                last.then_inc(xT_in_psum, 1)
                pe.wait_ge(xT_copied, ch + 1)
                for m, (dst, read, ready) in enumerate(((psQ, q_copied, q_in_psum), (psV, v_copied, v_in_psum))):
                    if ch >= 1:
                        pe.wait_ge(read, ch)
                    for j in range(CW):
                        last = nc.tensor.matmul(dst[:, j * D:(j + 1) * D], c.UT[ch % 2][:, j * P:(j + 1) * P], W_T[:, m, :],
                                                start=True, stop=True)
                    last.then_inc(ready, 1)


def scan(nc, c, scanned):
    LA, LW, CE = LANES, W_LANE, CW * D
    NS = len(SHIFTS)
    G = NS * SC
    ROWS = CW * LA
    HEAD = 7
    with ExitStack() as cx:
        def sb(name, shape, dt=fp32):
            return cx.enter_context(nc.sbuf_tensor(name, shape, dt))

        def ps(name):
            return cx.enter_context(nc.psum_tensor(name, [P, CE], fp32))

        sem = stage_semaphores(nc, cx, "scan_")

        lane_products = [sb(f"lane_products{u}", [P, LA, ROWS, LW]) for u in range(2)]
        weighted = sb("weighted", [P, LA, ROWS, LW])
        v_sb = [sb(f"v_sb{u}", [P, CE]) for u in range(2)]
        z_normed = sb("z_normed", [P, CW, D])
        squares = sb("z_squares", [P, ROWS, LW])
        scores = sb("scores", [P, LA * CW, LA])
        best = sb("best_score", [P, LA * CW])
        shifted = sb("shifted_scores", [P, LA * CW, LA])
        expd = sb("exp_scores", [P, LA * CW, LA])
        total = sb("total", [P, LA * CW])
        share = sb("share", [P, LA * CW])
        att = [sb(f"att{u}", [P, LA, ROWS]) for u in range(2)]
        ss, log_ms, rs, rs_lane = (sb(n, [P, LA * CW]) for n in ("ss", "log_ms", "rs", "rs_lane"))
        lane_inv = sb("lane_inv", [P, LA, CW])
        eps = sb("rms_eps", [P, 1])
        psU, psZ = ps("psU"), ps("psZ")
        psV = [ps(f"psV_s{u}") for u in range(2)]

        l_loaded = [sem(f"l_loaded{ch}") for ch in range(SC)]
        x_stored = [sem(f"x_stored{ch}") for ch in range(SC)]
        made = sem("made_s")
        u_done, p1_pool, p2_pool, x_new = (sem(n) for n in ("u_done", "p1_pool", "p2_pool", "x_new"))
        u_in_psum, uT_copied, v_in_psum, v_copied, z_in_psum = (
            sem(n) for n in ("u_in_psum", "uT_copied", "v_in_psum", "v_copied", "z_in_psum"))
        head_steps, p2_dve, ss_done, rs_steps, z_done = (
            sem(n) for n in ("head_steps", "p2_dve", "ss_done", "rs_steps", "z_done"))
        exp_done, squared, rs_log, rs_done = sem("exp_done"), sem("squared"), sem("rs_log"), sem("rs_done")
        block = cx.enter_context(nc.Block())

        def chunks(engine, section, lag):
            for ch in range(SC):
                section(ch, 0, ch, True)
            with engine.Fori(1, NS) as s:
                for ch in range(SC):
                    section(s * SC + ch, s, ch, True)
            for k in range(lag):
                section(G + k, NS, k, False)

        def wait(engine, semaphore, value):
            if not isinstance(value, int) or value > 0:
                engine.wait_ge(semaphore, value)

        def reached(g, lag):
            return not isinstance(g, int) or 0 <= g - lag < G

        @block.sync
        def _(sp):
            for ch in range(SC):
                sp.dma_start(c.L[ch][:], padded_rows(scanned[0], ch, SHIFTS[0])).then_inc(l_loaded[ch], 16)
            for s in range(NS - 1):
                for ch in range(SC):
                    sp.wait_ge(x_new, s * SC + ch + 1)
                    sp.dma_start(padded_rows(scanned[(s + 1) % 2], ch), c.q[:, ch]).then_inc(x_stored[ch], 16)
                    sp.wait_ge(x_stored[ch], 16 * (s + 1))
                    sp.dma_start(c.L[ch][:], padded_rows(scanned[(s + 1) % 2], ch, SHIFTS[s + 1]))\
                      .then_inc(l_loaded[ch], 16)

        def lane_product(engine, ch, l, out):
            return engine.tensor_tensor(
                out[:, l].rearrange("p (j m) d -> p j m d", m=LA),
                c.L[ch][:, :, l * LW:(l + 1) * LW].unsqueeze(2).broadcast_to([P, CW, LA, LW]),
                c.q[:, ch].rearrange("p j (m d) -> p j m d", m=LA), ALU.mult)

        @block.gpsimd
        def _(pool):
            for l in range(LA):
                nc.gpsimd.memset(lane_inv[:, l, :], 1.0 / (l + 1)).then_inc(made, 1)
            nc.gpsimd.memset(eps[:], RMS_EPS).then_inc(made, 1)

            def section(g, s, ch, head):
                u = ch % 2
                if head:
                    pool.wait_ge(l_loaded[ch], s * 16 + 16)
                    wait(pool, x_new, g - 3)
                    wait(pool, u_in_psum, g - 1)
                    nc.gpsimd.tensor_tensor(c.U[u][:], c.L[ch][:], c.q[:, ch], ALU.add).then_inc(u_done, 1)
                    wait(pool, head_steps, (g - 2) * HEAD + 2)
                    lane_product(nc.gpsimd, ch, 2, lane_products[u])
                    lane_product(nc.gpsimd, ch, 3, lane_products[u]).then_inc(p1_pool, 1)
                if reached(g, 1):
                    pool.wait_ge(head_steps, (g - 1) * HEAD + HEAD)
                    pool.wait_ge(v_copied, g)
                    wait(pool, z_in_psum, g - 1)
                    nc.gpsimd.tensor_tensor(weighted[:, 3], att[1 - u][:, 3].unsqueeze(2).broadcast_to([P, ROWS, LW]),
                                            v_sb[1 - u][:].rearrange("p (r d) -> p r d", d=LW), ALU.mult)\
                      .then_inc(p2_pool, 1)
                if reached(g, 2):
                    pool.wait_ge(z_done, g - 1)
                    nc.gpsimd.tensor_tensor(c.q[:, (ch - 2) % SC], c.L[(ch - 2) % SC][:], z_normed[:], ALU.add)\
                      .then_inc(x_new, 1)

            chunks(pool, section, 2)
            pool.wait_ge(x_new, G)

        @block.vector
        def _(dve):
            dve.wait_ge(made, LA + 1)

            def section(g, s, ch, head):
                u = ch % 2
                if head:
                    dve.wait_ge(l_loaded[ch], s * 16 + 16)
                    wait(dve, x_new, g - 3)
                    steps = Steps(dve, head_steps, g * HEAD)
                    lane_product(nc.vector, ch, 0, lane_products[u])
                    steps.then(lane_product(nc.vector, ch, 1, lane_products[u]))
                    dve.wait_ge(p1_pool, g + 1)
                    steps.then(nc.vector.tensor_reduce(scores[:].rearrange("p r m -> p (r m)"),
                                                       lane_products[u][:].rearrange("p l r d -> p (l r) d"),
                                                       axis=AX.X, op=ALU.add))
                    steps.then(nc.vector.tensor_reduce(best[:], scores[:], axis=AX.X, op=ALU.max))
                    steps.then(nc.vector.tensor_tensor(shifted[:], scores[:], best[:].unsqueeze(2)
                                                       .broadcast_to([P, LA * CW, LA]), ALU.subtract))
                if reached(g, 1):
                    dve.wait_ge(squared, g)
                    nc.vector.tensor_reduce(ss[:], squares[:], axis=AX.X, op=ALU.add).then_inc(ss_done, 1)
                if head:
                    dve.wait_ge(exp_done, g + 1)
                    steps.then(nc.vector.tensor_reduce(total[:], expd[:], axis=AX.X, op=ALU.add))
                    steps.then(nc.vector.reciprocal(share[:], total[:]))
                    steps.then(nc.vector.tensor_tensor(att[u][:].rearrange("p l (j m) -> p (l j) m", m=LA), expd[:],
                                                       share[:].unsqueeze(2).broadcast_to([P, LA * CW, LA]), ALU.mult))
                    assert steps.n == HEAD
                    dve.wait_ge(v_in_psum, g + 1)
                    dve.wait_ge(v_copied, g + 1)
                    wait(dve, z_in_psum, g)
                    nc.vector.tensor_tensor(weighted[:, 0:3], att[u][:, 0:3].unsqueeze(3).broadcast_to([P, 3, ROWS, LW]),
                                            psV[u][:].rearrange("p (r d) -> p r d", d=LW).unsqueeze(1)
                                            .broadcast_to([P, 3, ROWS, LW]), ALU.mult).then_inc(p2_dve, 1)
                if reached(g, 1):
                    dve.wait_ge(rs_done, g)
                    nc.vector.tensor_tensor(rs_lane[:], rs[:], lane_inv[:].rearrange("p l j -> p (l j)"), ALU.mult)\
                      .then_inc(rs_steps, 1)
                    dve.wait_ge(rs_steps, g)
                    wait(dve, x_new, g - 1)
                    nc.vector.tensor_tensor(z_normed[:].rearrange("p j (l d) -> p l j d", l=LA),
                                            psZ[:].rearrange("p (l j d) -> p l j d", l=LA, d=LW),
                                            rs_lane[:].rearrange("p (l j) -> p l j", l=LA).unsqueeze(3)
                                            .broadcast_to([P, LA, CW, LW]), ALU.mult).then_inc(z_done, 1)

            chunks(dve, section, 1)

        @block.scalar
        def _(act):
            act.wait_ge(made, LA + 1)

            def section(g, s, ch, head):
                u = ch % 2
                if reached(g, 1):
                    act.wait_ge(head_steps, (g - 1) * HEAD + 4)
                    nc.scalar.activation(expd[:], shifted[:], ACT.Exp, scale=W_LANE ** -0.5).then_inc(exp_done, 1)
                if reached(g, 2):
                    act.wait_ge(z_in_psum, g - 1)
                    wait(act, ss_done, g - 2)
                    nc.scalar.activation(squares[:].rearrange("p r d -> p (r d)"), psZ[:], ACT.Square).then_inc(squared, 1)
                if head:
                    act.wait_ge(u_in_psum, g + 1)
                    wait(act, v_in_psum, g - 1)
                    nc.scalar.activation(c.UT[u][:], psU[:], ACT.Copy).then_inc(uT_copied, 1)
                if reached(g, 2):
                    act.wait_ge(ss_done, g - 1)
                    nc.scalar.activation(log_ms[:], ss[:], ACT.Ln, bias=eps[:], scale=1.0 / W_LANE).then_inc(rs_log, 1)
                    act.wait_ge(rs_log, g - 1)
                    nc.scalar.activation(rs[:], log_ms[:], ACT.Exp, scale=-0.5).then_inc(rs_done, 1)
                if head:
                    act.wait_ge(v_in_psum, g + 1)
                    wait(act, p2_pool, g - 1)
                    nc.scalar.activation(v_sb[u][:], psV[u][:], ACT.Copy).then_inc(v_copied, 1)

            chunks(act, section, 2)

        @block.tensor
        def _(pe):
            def section(g, s, ch, head):
                u = ch % 2
                if reached(g, 2):
                    pe.wait_ge(p2_dve, g - 1)
                    pe.wait_ge(p2_pool, g - 1)
                    wait(pe, z_done, g - 2)
                    for l in range(LA):
                        for m in range(LA):
                            last = nc.tensor.matmul(psZ[:, l * CW * LW:(l + 1) * CW * LW], c.ident[:],
                                                    weighted[:, l].rearrange("p (j m) d -> p j m d", m=LA)[:, :, m, :],
                                                    start=m == 0, stop=m == LA - 1)
                    last.then_inc(z_in_psum, 1)
                if head:
                    pe.wait_ge(u_done, g + 1)
                    wait(pe, uT_copied, g)
                    for j in range(CW):
                        last = nc.tensor.transpose(psU[:, j * P:(j + 1) * P], c.U[u][:, j, :], c.ident[:])
                    last.then_inc(u_in_psum, 1)
                    pe.wait_ge(uT_copied, g + 1)
                    wait(pe, p2_dve, g - 1)
                    wait(pe, v_copied, g - 1)
                    for j in range(CW):
                        last = nc.tensor.matmul(psV[u][:, j * D:(j + 1) * D], c.UT[u][:, j * P:(j + 1) * P], c.S[:, 0, :],
                                                start=True, stop=True)
                    last.then_inc(v_in_psum, 1)

            chunks(pe, section, 2)


def scan_outputs(nc, c, dst):
    with ExitStack() as cx:
        def ps(name):
            return cx.enter_context(nc.psum_tensor(name, [P, CW * P], fp32))

        sem = stage_semaphores(nc, cx, "scan_outputs_")

        psT = [ps(f"psT_o{u}") for u in range(2)]
        psY = [ps(f"psY_o{u}") for u in range(2)]
        gated, gT_in_psum, gT_copied, y_in_psum, y_done = (
            sem(n) for n in ("gated", "gT_in_psum", "gT_copied", "y_in_psum", "y_done"))
        y_stored = sem("y_stored")
        block = cx.enter_context(nc.Block())

        @block.gpsimd
        def _(pool):
            for ch in range(SC):
                if ch >= 2:
                    pool.wait_ge(gT_in_psum, ch - 1)
                nc.gpsimd.tensor_tensor(c.U[ch % 2][:], c.q[:, ch], c.v2[:, ch], ALU.mult).then_inc(gated, 1)

        @block.tensor
        def _(pe):
            for ch in range(SC):
                pe.wait_ge(gated, ch + 1)
                if ch >= 2:
                    pe.wait_ge(gT_copied, ch - 1)
                for j in range(CW):
                    last = nc.tensor.transpose(psT[ch % 2][:, j * P:(j + 1) * P], c.U[ch % 2][:, j, :], c.ident[:])
                last.then_inc(gT_in_psum, 1)
                pe.wait_ge(gT_copied, ch + 1)
                if ch >= 2:
                    pe.wait_ge(y_done, ch - 1)
                for j in range(CW):
                    last = nc.tensor.matmul(psY[ch % 2][:, j * D:(j + 1) * D], c.UT[ch % 2][:, j * P:(j + 1) * P],
                                            c.Wproj_T[:], start=True, stop=True)
                last.then_inc(y_in_psum, 1)

        @block.scalar
        def _(act):
            for ch in range(SC):
                act.wait_ge(gT_in_psum, ch + 1)
                if ch >= 2:
                    act.wait_ge(y_in_psum, ch - 1)
                nc.scalar.activation(c.UT[ch % 2][:], psT[ch % 2][:], ACT.Copy).then_inc(gT_copied, 1)

        @block.vector
        def _(dve):
            for ch in range(SC):
                dve.wait_ge(y_in_psum, ch + 1)
                nc.vector.tensor_tensor(c.X2[:, ch].rearrange("p j d -> p (j d)"), psY[ch % 2][:],
                                        c.X2[:, ch].rearrange("p j d -> p (j d)"), ALU.add).then_inc(y_done, 1)

        @block.sync
        def _(sp):
            for ch in range(SC):
                sp.wait_ge(y_done, ch + 1)
                sp.dma_start(token_rows(dst, ch), c.X2[:, ch]).then_inc(y_stored, 16)
            sp.wait_ge(y_stored, 16 * SC)


def final_sum(nc, x, routed, out):
    with ExitStack() as cx:
        x_sb = [cx.enter_context(nc.sbuf_tensor(f"x_last{ch}", [P, CW, D], fp32)) for ch in range(SC)]
        r_sb = [cx.enter_context(nc.sbuf_tensor(f"r_last{ch}", [P, CW, D], fp32)) for ch in range(SC)]
        sem = stage_semaphores(nc, cx, "final_sum_")
        loaded = [sem(f"loaded_last{ch}") for ch in range(SC)]
        summed, stored = sem("summed_last"), sem("stored_last")
        block = cx.enter_context(nc.Block())

        @block.sync
        def _(sp):
            for ch in range(SC):
                sp.dma_start(x_sb[ch][:], token_rows(x, ch)).then_inc(loaded[ch], 16)
                sp.dma_start(r_sb[ch][:], token_rows(routed, ch)).then_inc(loaded[ch], 16)
            for ch in range(SC):
                sp.wait_ge(summed, ch + 1)
                sp.dma_start(token_rows(out, ch), x_sb[ch][:]).then_inc(stored, 16)
            sp.wait_ge(stored, 16 * SC)

        @block.vector
        def _(dve):
            for ch in range(SC):
                dve.wait_ge(loaded[ch], 32)
                nc.vector.tensor_tensor(x_sb[ch][:], x_sb[ch][:], r_sb[ch][:], ALU.add).then_inc(summed, 1)


def hybrid_layer(nc, x, Wq, bq, Wk, bk, Wv, bv, Wo, bo, W_up, W_v, W_proj, identity, W_scan_raw, Wg, w1, w2, out):
    q_parts = nc.dram_tensor("q_parts", [3, P, N], bf16).ap()
    k_parts = nc.dram_tensor("k_parts", [3, P, N], bf16).ap()
    max_dram = nc.dram_tensor("max_rows_dram", [2, NT // B, P], bf16).ap()
    x1 = nc.dram_tensor("x1", [N, D], fp32).ap()
    x3 = nc.dram_tensor("x3", [N, D], fp32).ap()
    dispatched = [nc.dram_tensor(f"dispatched{k}", [2 * N, ROW], fp32).ap() for k in range(2)]
    routed = [nc.dram_tensor(f"routed{k}", [2 * N, D], fp32).ap() for k in range(2)]
    scanned = [nc.dram_tensor(f"scanned{k}", [B * (PAD + T), D], fp32).ap() for k in range(2)]

    class Shared:
        pass

    c = Shared()
    with ExitStack() as cx:
        constants(nc, cx, c)
        with ExitStack() as cx_attention:
            attention_tensors(nc, cx_attention, c)
            project(nc, c, x, Wq, bq, Wk, bk, Wv, bv, Wo, bo, W_scan_raw, q_parts, k_parts)
            attend(nc, c, q_parts, k_parts, max_dram)
            project_out(nc, c, x1)
        moe(nc, c, "m0", x1, Wg, w1, w2, dispatched[0], routed[0])
        with ExitStack() as cx_scan:
            scan_tensors(nc, cx_scan, c)
            scan_inputs(nc, c, x1, routed[0][0:N, :], W_up, W_v, W_proj, identity, scanned)
            scan(nc, c, scanned)
            scan_outputs(nc, c, x3)
        moe(nc, c, "m1", x3, Wg, w1, w2, dispatched[1], routed[1])
        final_sum(nc, x3, routed[1][0:N, :], out)


_INS = ["L0_attn_a_x", "L0_attn_a_Wq", "L0_attn_a_bq", "L0_attn_a_Wk", "L0_attn_a_bk", "L0_attn_a_Wv", "L0_attn_a_bv",
        "L0_attn_a_Wo", "L0_attn_a_bo", "L0_attn_b_W_up", "L0_attn_b_W_v", "L0_attn_b_W_proj", "L0_attn_b_identity",
        "L0_attn_b_W_scan_raw", "L0_ffn_Wg", "L0_ffn_w1", "L0_ffn_w2"]


def kernel(**inputs):
    import numpy as _np
    import concourse.bacc as _bacc
    from concourse import mybir as _mybir
    from concourse.bass_utils import run_bass_kernel_spmd as _run

    nc = _bacc.Bacc("TRN2", target_bir_lowering=False, num_devices=1)
    arrays, args = {}, []
    for name in _INS:
        a = _np.ascontiguousarray(inputs[name])
        if name == "L0_attn_a_x":
            a = a.reshape(N, D)
        arrays[f"in_{name}_dram"] = a
        args.append(nc.dram_tensor(f"in_{name}_dram", a.shape, _mybir.dt.from_np(a.dtype), kind="ExternalInput").ap())
    out = nc.dram_tensor("out_0_dram", (N, D), fp32, kind="ExternalOutput").ap()
    hybrid_layer(nc, *args, out)
    r = _run(nc, [arrays], core_ids=[0])
    return r.results[0]["out_0_dram"].reshape(B, T, D)
```

```python
import concourse.bass as bass
from concourse import mybir
from contextlib import ExitStack

fp32 = mybir.dt.float32
bf16 = mybir.dt.bfloat16
i32 = mybir.dt.int32
ALU = mybir.AluOpType
ACT = mybir.ActivationFunctionType
AX = mybir.AxisListType

P = 128
B, T, D = 2, 2048, 128
N = B * T
H = 16
HD = D // H
NT = N // P
EPS = 1e-5
MASKED = -1e30
LEAST = -3e38
NEWTON = (15 / 8, -10 / 8, 3 / 8)


class Steps:

    def __init__(self, engine, semaphore, base=0):
        self.engine, self.semaphore, self.base, self.n = engine, semaphore, base, 0

    def then(self, instruction):
        self.n += 1
        instruction.then_inc(self.semaphore, 1)
        self.engine.wait_ge(self.semaphore, self.base + self.n)


def stage_semaphores(nc, cx, prefix):
    taken = []
    cx.callback(nc.all_engine_barrier)
    cx.callback(nc.clear_and_free_semaphores, taken)

    def take(name):
        taken.append(nc.alloc_semaphore(name=prefix + name))
        return taken[-1]

    return take


def finish_stats(nc, steps, st, tmp, mean, var):
    mean_a, m2_a, mean_b, m2_b = st[:, :, 1], st[:, :, 2], st[:, :, 4], st[:, :, 5]
    s, d, m2, dd = (tmp[:, k, :] for k in range(4))
    nc.vector.tensor_tensor(s, mean_a, mean_b, ALU.add)
    nc.vector.tensor_tensor(m2, m2_a, m2_b, ALU.add)
    steps.then(nc.vector.tensor_tensor(d, mean_a, mean_b, ALU.subtract))
    steps.then(nc.vector.tensor_tensor(dd, d, d, ALU.mult))
    nc.vector.tensor_scalar(mean, s, 0.5, None, ALU.mult)
    steps.then(nc.vector.tensor_scalar(m2, m2, 1.0 / D, EPS, ALU.mult, ALU.add))
    steps.then(nc.vector.scalar_tensor_tensor(out=var, in0=dd, scalar=0.25, in1=m2, op0=ALU.mult, op1=ALU.add))


def project(nc, c, x, Wq, bq, Wk, bk, Wv, bv, Wo, bo, Wscan, q_parts, k_parts):
    CH = 512
    NCH = N // CH
    TC = CH // P
    NB = NT // B
    with ExitStack() as cx:
        def sb(name, shape, dt=fp32):
            return cx.enter_context(nc.sbuf_tensor(name, shape, dt))

        def ps(name, shape=(P, CH)):
            return cx.enter_context(nc.psum_tensor(name, list(shape), fp32))

        sem = stage_semaphores(nc, cx, "project_")

        W_nat = sb("W_nat", [P, 4, D])
        W_T = sb("W_T", [P, 3, D])
        bias_cols = sb("bias_cols", [P, 2])
        bv_rows = sb("bv_rows", [P, D])
        bo_rows = sb("bo_rows", [P, D])
        st = sb("st", [P, NT, 6])
        tmp = sb("tmp", [P, 4, NT])
        mean, var, std, rstd = (sb(n, [P, NT]) for n in ("mean", "var", "std", "rstd"))
        centred = [sb(f"centred{u}", [P, TC, D]) for u in range(2)]
        xn = [sb(f"xn{u}", [P, TC, D]) for u in range(2)]
        xnT = [sb(f"xnT{u}", [P, CH]) for u in range(2)]
        full = [sb(f"full{u}", [P, 2, CH]) for u in range(2)]
        rest = [sb(f"rest{u}", [P, 2, CH]) for u in range(2)]
        parts = [sb(f"parts{u}", [P, 2, 3, CH], bf16) for u in range(2)]
        squares = sb("squares", [P, D])
        norm = sb("norm", [P, 3])
        ones = sb("ones_f", [P, P])
        psT = [ps(f"psT{u}") for u in range(2)]
        psQK = [[ps(f"psQK{u}{a}") for a in range(2)] for u in range(2)]
        psV = [ps(f"psV{u}") for u in range(2)]

        x_loaded = [sem(f"x_loaded{b}") for b in range(B)]
        w_loaded, b_loaded, made = sem("w_loaded"), sem("b_loaded"), sem("made")
        wT_in_psum, wT_copied = sem("wT_in_psum"), sem("wT_copied")
        stats, stat_steps, std_done, rstd_done = sem("stats"), sem("stat_steps"), sem("std_done"), sem("rstd_done")
        centred_done, xn_ready = sem("centred_done"), sem("xn_ready")
        xT_in_psum, xT_copied, v_in_psum, v_done, full_done = (
            sem(n) for n in ("xT_in_psum", "xT_copied", "v_in_psum", "v_done", "full_done"))
        stored = [sem(f"stored{u}") for u in range(2)]
        qk_in_psum, rest_done, mid_done, lo_done = (
            sem(n) for n in ("qk_in_psum", "rest_done", "mid_done", "lo_done"))
        norm_act, norm_pe, norm_dve = sem("norm_act"), sem("norm_pe"), sem("norm_dve")
        resid_done = sem("resid_done")
        block = cx.enter_context(nc.Block())

        x_t = x.rearrange("(i p) d -> p i d", p=P)

        @block.sync
        def _(sp):
            for ch in range(NCH):
                sp.dma_start(c.X[:, ch * TC:(ch + 1) * TC, :], x_t[:, ch * TC:(ch + 1) * TC, :])\
                  .then_inc(x_loaded[ch // (NCH // B)], 16)
            for m, w in enumerate((Wq, Wk, Wv, Wo)):
                sp.dma_start(W_nat[:, m, :], w).then_inc(w_loaded, 16)
            sp.dma_start(c.S_nat[:], Wscan).then_inc(w_loaded, 16)
            for a, bias in enumerate((bq, bk)):
                sp.dma_start(bias_cols[:, a:a + 1], bias.rearrange("(p a) -> p a", a=1)).then_inc(b_loaded, 16)
            sp.dma_start(bv_rows[:], bv.rearrange("(a d) -> a d", a=1).broadcast_to([P, D])).then_inc(b_loaded, 16)
            sp.dma_start(bo_rows[:], bo.rearrange("(a d) -> a d", a=1).broadcast_to([P, D])).then_inc(b_loaded, 16)
            with sp.Fori(0, NCH // 2) as it:
                for u in range(2):
                    ch = it * 2 + u
                    sp.wait_ge(lo_done, ch * 2 + 2)
                    for a, dst in enumerate((q_parts, k_parts)):
                        sp.dma_start(dst.rearrange("a p t -> p a t")[:, :, bass.ds(ch * CH, CH)], parts[u][:, a, :, :])\
                          .then_inc(stored[u], 16)
            for u in range(2):
                sp.wait_ge(stored[u], 32 + 16 * NCH)

        @block.gpsimd
        def _(pool):
            for t, value in ((c.ident, 0.0), (c.ident_b, 0.0), (c.mask, 0.0), (c.select, 0.0),
                             (ones, 1.0)):
                nc.gpsimd.memset(t[:], value).then_inc(made, 1)
            pool.wait_ge(made, 5)
            for m in (c.ident, c.ident_b):
                nc.gpsimd.affine_select(out=m[:], in_=m[:], compare_op=ALU.not_equal, fill=1.0, base=0,
                                        pattern=[[-1, P]], channel_multiplier=1).then_inc(made, 1)
            nc.gpsimd.affine_select(out=c.mask[:, 3 * P:], in_=c.mask[:, 3 * P:], compare_op=ALU.is_ge,
                                    fill=MASKED, base=0, pattern=[[-1, P]], channel_multiplier=1).then_inc(made, 1)
            for g in range(4):
                pool.wait_ge(made, 8 + g)
                nc.gpsimd.affine_select(out=c.select[:], in_=c.select[:], compare_op=ALU.not_equal, fill=1.0,
                                        base=-32 * g, pattern=[[-1, HD + 1]], channel_multiplier=1).then_inc(made, 1)
            with pool.Fori(0, NCH // 2) as it:
                for u in range(2):
                    ch = it * 2 + u
                    pool.wait_ge(rstd_done, ch // (NCH // B) + 1)
                    sl = (slice(None), bass.ds(ch * TC, TC))
                    pool.wait_ge(xT_in_psum, ch + 1)
                    nc.gpsimd.tensor_tensor(centred[u][:], c.X[sl], mean[sl].unsqueeze(2).broadcast_to([P, TC, D]),
                                            ALU.subtract).then_inc(centred_done, 1)
                    pool.wait_ge(centred_done, ch + 1)
                    nc.gpsimd.tensor_tensor(xn[u][:], centred[u][:], rstd[sl].unsqueeze(2).broadcast_to([P, TC, D]),
                                            ALU.mult).then_inc(xn_ready, 1)
            pool.wait_ge(b_loaded, 64)
            pool.wait_ge(xn_ready, NCH)
            nc.gpsimd.tensor_tensor(c.X[:], c.X[:], bo_rows[:].unsqueeze(1).broadcast_to([P, NT, D]), ALU.add)\
              .then_inc(resid_done, 1)
            pool.wait_ge(resid_done, 1)

        @block.vector
        def _(dve):
            dve.sem_inc(v_done, 2)
            steps = Steps(dve, stat_steps)
            for b in range(B):
                half = slice(b * NB, (b + 1) * NB)
                dve.wait_ge(x_loaded[b], 16 * NCH // B)
                with dve.Fori(b * NB // 8, (b + 1) * NB // 8) as k:
                    for i in range(8):
                        nc.vector.bn_stats(st[:, bass.ds(k * 8 + i, 1), :], c.X[:, bass.ds(k * 8 + i, 1), :])\
                          .then_inc(stats, 1)
                dve.wait_ge(stats, (b + 1) * NB)
                finish_stats(nc, steps, st[:, half, :], tmp[:, :, half], mean[:, half], var[:, half])
                dve.wait_ge(std_done, b + 1)
                nc.vector.reciprocal(rstd[:, half], std[:, half]).then_inc(rstd_done, 1)
            dve.wait_ge(wT_in_psum, 1)
            nc.vector.tensor_copy(W_T[:].rearrange("p m d -> p (m d)"), psT[0][:, 0:3 * D]).then_inc(wT_copied, 1)
            nc.vector.tensor_copy(c.Wo_T[:], psT[0][:, 3 * D:]).then_inc(wT_copied, 1)
            dve.wait_ge(b_loaded, 64)
            with dve.Fori(0, NCH // 2) as it:
                for u in range(2):
                    ch = it * 2 + u
                    for a in range(2):
                        dve.wait_ge(full_done, ch * 2 + a + 5)
                        nc.vector.tensor_tensor(rest[u][:, a, :], full[u][:, a, :], parts[u][:, a, 0, :], ALU.subtract)\
                          .then_inc(rest_done, 1)
                        dve.wait_ge(rest_done, ch * 2 + a + 1)
                        nc.vector.tensor_copy(parts[u][:, a, 1, :], rest[u][:, a, :]).then_inc(mid_done, 1)
                        dve.wait_ge(mid_done, ch * 2 + a + 1)
                        nc.vector.tensor_tensor(parts[u][:, a, 2, :], rest[u][:, a, :], parts[u][:, a, 1, :],
                                                ALU.subtract).then_inc(lo_done, 1)
                    dve.wait_ge(v_in_psum, ch + 3)
                    nc.vector.tensor_tensor(c.V[:, :, bass.ds(ch, 1), :, :].rearrange("p h c i d -> p (c i) h d"),
                                            psV[u][:].rearrange("p (i h d) -> p i h d", i=TC, h=H),
                                            bv_rows[:].rearrange("p (h d) -> p h d", h=H).unsqueeze(1)
                                            .broadcast_to([P, TC, H, HD]), ALU.add).then_inc(v_done, 1)
            dve.wait_ge(norm_act, 2)
            nc.vector.reciprocal(norm[:, 2:3], norm[:, 1:2]).then_inc(norm_dve, 1)
            dve.wait_ge(norm_dve, 1)
            nc.vector.tensor_scalar(c.S[:, 0, :], c.S_nat[:], norm[:, 2:3], None, ALU.mult).then_inc(norm_dve, 1)
            dve.wait_ge(norm_pe, 2)
            nc.vector.tensor_copy(c.S[:, 1, :], psT[0][:, 0:D]).then_inc(norm_dve, 1)
            dve.wait_ge(norm_dve, 3)

        @block.scalar
        def _(act):
            act.sem_inc(xT_copied, 2)
            act.sem_inc(full_done, 4)
            act.wait_ge(w_loaded, 80)
            nc.scalar.activation(squares[:], c.S_nat[:], ACT.Square, accum_out=norm[:, 0:1]).then_inc(norm_act, 1)
            act.wait_ge(norm_pe, 1)
            nc.scalar.activation(norm[:, 1:2], psQK[0][0][:, 0:1], ACT.Sqrt).then_inc(norm_act, 1)
            for b in range(B):
                half = slice(b * NB, (b + 1) * NB)
                act.wait_ge(stat_steps, 4 * (b + 1))
                nc.scalar.activation(std[:, half], var[:, half], ACT.Sqrt).then_inc(std_done, 1)
            act.wait_ge(b_loaded, 64)
            with act.Fori(0, NCH // 2) as it:
                for u in range(2):
                    ch = it * 2 + u
                    act.wait_ge(xT_in_psum, ch + 3)
                    act.wait_ge(v_in_psum, ch + 1)
                    nc.scalar.activation(xnT[u][:], psT[u][:], ACT.Copy).then_inc(xT_copied, 1)
                    act.wait_ge(stored[u], it * 32 + 32)
                    for a in range(2):
                        act.wait_ge(qk_in_psum, ch * 2 + a + 1)
                        nc.scalar.activation(parts[u][:, a, 0, :], psQK[u][a][:], ACT.Identity,
                                             bias=bias_cols[:, a:a + 1])
                        nc.scalar.activation(full[u][:, a, :], psQK[u][a][:], ACT.Identity,
                                             bias=bias_cols[:, a:a + 1]).then_inc(full_done, 1)

        @block.tensor
        def _(pe):
            pe.sem_inc(xT_in_psum, 2)
            pe.sem_inc(v_in_psum, 2)
            for u in range(2):
                pe.sem_inc(stored[u], 32)
            pe.wait_ge(made, 7)
            pe.wait_ge(w_loaded, 80)
            for m in range(4):
                last = nc.tensor.transpose(psT[0][:, m * D:(m + 1) * D], W_nat[:, m, :], c.ident[:])
            last.then_inc(wT_in_psum, 1)
            pe.wait_ge(norm_act, 1)
            nc.tensor.matmul(psQK[0][0][:, 0:1], ones[:], norm[:, 0:1], start=True, stop=True).then_inc(norm_pe, 1)
            pe.wait_ge(norm_act, 2)
            pe.wait_ge(wT_copied, 2)
            with pe.Fori(0, NCH // 2) as it:
                for u in range(2):
                    ch = it * 2 + u
                    pe.wait_ge(xn_ready, ch + 1)
                    pe.wait_ge(xT_copied, ch + 1)
                    for i in range(TC):
                        last = nc.tensor.transpose(psT[u][:, i * P:(i + 1) * P], xn[u][:, i, :], c.ident[:])
                    last.then_inc(xT_in_psum, 1)
                    pe.wait_ge(xT_copied, ch + 3)
                    pe.wait_ge(full_done, ch * 2 + 2)
                    for a in range(2):
                        nc.tensor.matmul(psQK[u][a][:], W_T[:, a, :], xnT[u][:], start=True, stop=True)\
                          .then_inc(qk_in_psum, 1)
                    pe.wait_ge(v_done, ch + 1)
                    for i in range(TC):
                        last = nc.tensor.matmul(psV[u][:, i * D:(i + 1) * D], xnT[u][:, i * P:(i + 1) * P],
                                                W_T[:, 2, :], start=True, stop=True)
                    last.then_inc(v_in_psum, 1)
            pe.wait_ge(norm_dve, 2)
            pe.wait_ge(xT_copied, NCH + 2)
            nc.tensor.transpose(psT[0][:, 0:D], c.S[:, 0, :], c.ident[:]).then_inc(norm_pe, 1)


def constants(nc, cx, c):
    def sb(name, shape, dt=fp32):
        return cx.enter_context(nc.sbuf_tensor(name, shape, dt))
    c.ident = sb("ident", [P, P])
    c.ident_b = sb("ident_b", [P, P], bf16)
    c.X = sb("X", [P, NT, D])
    c.S = sb("S_pair", [P, 2, D])


def attention_tensors(nc, cx, c):
    def sb(name, shape, dt=fp32):
        return cx.enter_context(nc.sbuf_tensor(name, shape, dt))
    c.mask = sb("mask", [P, 4 * P])
    c.select = sb("select", [P, HD + 1])
    c.V = sb("V", [P, H, 8, 4, HD])
    c.Wo_T = sb("Wo_T", [P, D])
    c.A_out = sb("A_out", [P, NT // B, B * H, HD])
    c.S_nat = sb("S_nat", [P, D])


def attend(nc, c, q_parts, k_parts, max_dram):
    NH = B * H
    NQ = T // P
    G = 4
    QW = T // G
    SCALE = HD ** -0.5
    R = 3
    ROWS = P
    MROW = P - 2
    STEPS = [(g, kt) for g in range(G) for kt in range(4 * g + 4)]
    NS = len(STEPS)
    NBATCH = NS // 4
    MIDDLE = 2
    GROUP_END = {g: sum(4 * f + 4 for f in range(g + 1)) // 4 - 1 for g in range(G)}
    MAXES = [(i, ck) for a in range(4) for i, ck in ((a + 4, 0), (a, 0))]
    MAXES += [(i, 1) for i in range(7, 3, -1)]
    MAXES += [(i, ck) for i in range(NQ - 1, 7, -1) for ck in range(i // 4 + 1)]
    FIRST_MAXES = 12
    assert len(set(MAXES)) == NS and all(i < NQ // 2 for i, ck in MAXES[:FIRST_MAXES])

    with ExitStack() as cx:
        def sb(name, shape, dt=fp32):
            return cx.enter_context(nc.sbuf_tensor(name, shape, dt))

        def ps(name, shape=(P, 512), dt=fp32):
            return cx.enter_context(nc.psum_tensor(name, list(shape), dt))

        sem = stage_semaphores(nc, cx, "attend_")

        Q = [sb(f"Qs{r}", [ROWS, T], bf16) for r in range(R)]
        K = [sb(f"Ks{r}", [ROWS, T], bf16) for r in range(R)]
        Vp = [sb(f"Vp{r}", [P, NQ, 32]) for r in range(R)]
        probs = sb("probs", [P, 12, QW])
        probs0 = sb("probs0", [P, 4, QW])
        chunk_max = [sb(f"chunk_max{r}", [P, NQ, 4]) for r in range(R)]
        neg_max = [sb(f"neg_max{r}", [P, 2, NQ // 2]) for r in range(R)]
        neg_max_b = [sb(f"neg_max_b{r}", [P, 2, 2, NQ // 2], bf16) for r in range(R)]
        max_rows = [sb(f"max_rows{f}", [NQ, P], bf16) for f in range(2)]
        O_sb = [sb(f"O_sb{u}", [P, QW]) for u in range(2)]
        inv = sb("inv", [P, NQ])
        ones_row = sb("ones_row", [2, T], bf16)
        A = sb("A_newton", [P, D])
        A_b = sb("A_b", [P, D])
        Z = sb("Z_newton", [P, D])
        Y = sb("Y_newton", [P, D])
        a_ident = sb("a_ident", [P, D])
        b_tile = sb("b_tile", [P, D])
        ps_max = [ps(f"ps_max{u}") for u in range(R)]
        ps_s = [ps(f"ps_s{u}") for u in range(R)]
        ps_o = ps("ps_o")
        ps_misc = ps("ps_misc")
        comb3 = ps_misc[:, 0:16 * NQ].rearrange("p (i w) -> p i w", w=16)
        newton_ps = ps_misc[:, 256:512]
        rows_ps = ps_misc[0:NQ, 256:256 + P // 2].bitcast(bf16)

        stacks_loaded = [sem(f"stacks_loaded{r}") for r in range(R)]
        max_rows_loaded = [[sem(f"max_rows_loaded{r}{f}") for f in range(2)] for r in range(R)]
        max_rows_stored = [sem(f"max_rows_stored{f}") for f in range(2)]
        ones_loaded, made, v_staged = sem("ones_loaded"), sem("made_b"), sem("v_staged")
        max_scored, max_reduced = sem("max_scored"), sem("max_reduced")
        neg_max_steps = sem("neg_max_steps")
        rows_in_psum = sem("rows_in_psum")
        scored, exp_done, pv_done, o_copied = sem("scored"), sem("exp_done"), sem("pv_done"), sem("o_copied")
        combined, inv_done, masked = sem("combined"), sem("inv_done"), sem("masked")
        masks_begun, diagonals = sem("masks_begun"), sem("diagonals")
        misc_read = sem("misc_read")
        newton_mm, newton_pool = sem("newton_mm"), sem("newton_pool")
        block = cx.enter_context(nc.Block())

        def sections(engine, section):
            section(-1, -1, 2, False, True)
            section(0, 0, 0, True, True)
            with engine.Fori(0, (NH - 2) // R) as it:
                for u in range(R):
                    section(it * R + (u + 1), it + (u + 1) // R, (u + 1) % R, True, True)
            section(NH - 1, (NH - 1) // R, (NH - 1) % R, True, False)

        def following(j, r):
            return (j + 1, 0) if r == R - 1 else (j, r + 1)

        def preceding(j, r):
            return (j - 1, R - 1) if r == 0 else (j, r - 1)

        def wait(engine, semaphore, value):
            if not isinstance(value, int) or value > 0:
                engine.wait_ge(semaphore, value)

        def reads(s, name, nxt=True):
            if not isinstance(s, int) or s > 0:
                order = ["rows1", "A", "comb", "Y", "rows0", "X", "end"]
                if not nxt:
                    order.remove("rows0")
                return s * 6 + order.index(name)
            return ["rows0 of head 0", "rows1", "A", "Y", "rows0", "X", "end"].index(name) if s == 0 else 0

        @block.sync
        def _(sp):
            def load(s, j, r):
                rows, cols = bass.ds(s % H * HD, HD), bass.ds(s // H * T, T)
                for stack, parts, order in ((Q[r], q_parts, (0, 0, 0, 1, 1, 2)), (K[r], k_parts, (0, 1, 2, 0, 1, 0))):
                    for row, a in enumerate(order):
                        sp.dma_start(stack[row * HD:(row + 1) * HD, :], parts[a, rows, cols])\
                          .then_inc(stacks_loaded[r], 16)

            def place_max_rows(s, j, r, f):
                if f:
                    sp.wait_ge(misc_read, reads(s, "rows1") + 1)
                else:
                    sp.wait_ge(misc_read, reads(s - 1, "rows0") + 1)
                sp.dma_start(max_dram[f], max_rows[f][:])\
                  .then_inc(max_rows_stored[f], 16)
                sp.wait_ge(max_rows_stored[f], s * 16 + 16)
                sp.dma_start(Q[r][MROW:, f * T // 2:(f + 1) * T // 2],
                             max_dram[f].rearrange("(a i) q -> a (i q)", a=2)).then_inc(max_rows_loaded[r][f], 16)

            def section(s, j, r):
                place_max_rows(s, j, r, 1)
                if not isinstance(s, int) or s < NH - 2:
                    sp.wait_ge(scored, s * NS)
                    load(s + 2, *following(*following(j, r)))
                if not isinstance(s, int) or s < NH - 1:
                    place_max_rows(s + 1, *following(j, r), 0)

            sp.wait_ge(made, 14)
            load(0, 0, 0)
            load(1, 0, 1)
            for r in range(R):
                sp.dma_start(K[r][MROW:, :], ones_row[:]).then_inc(ones_loaded, 16)
            place_max_rows(0, 0, 0, 0)
            place_max_rows(0, 0, 0, 1)
            load(2, 0, 2)
            place_max_rows(1, 0, 1, 0)
            with sp.Fori(0, (NH - 2) // R - 1) as it:
                for u in range(R):
                    section(it * R + (u + 1), it + (u + 1) // R, (u + 1) % R)
            for s in range(NH - 1 - R, NH):
                section(s, s // R, s % R)

        @block.gpsimd
        def _(pool):
            n = 0
            for t, value in [(t, 0.0) for t in Vp] + [(t, LEAST) for t in chunk_max] + [(probs0, 0.0), (ones_row, 1.0)] \
                    + [(t, 0.0) for t in Q + K]:
                nc.gpsimd.memset(t[:], value).then_inc(made, 1)
                n += 1
            pool.wait_ge(made, n)
            for t in Vp:
                nc.gpsimd.memset(t[:, :, HD:HD + 1], 1.0).then_inc(made, 1)
            nc.gpsimd.memset(b_tile[:], NEWTON[1])
            nc.gpsimd.tensor_scalar(a_ident[:], c.ident[:], NEWTON[0], None, ALU.mult).then_inc(made, 1)
            pool.wait_ge(made, n + R + 1)

            def mask_probs(s, g):
                n = GROUP_END[g]
                for q in range(4):
                    pool.wait_ge(exp_done, s * NS + (4 * n + q + 1))
                    block = (probs[:, n % 3 * 4 + q, q * P:(q + 1) * P] if n else probs0[:, q, q * P:(q + 1) * P])
                    pool.sem_inc(masks_begun, 1)
                    nc.gpsimd.affine_select(out=block, in_=block, compare_op=ALU.is_ge, fill=0.0, base=0,
                                            pattern=[[1, P]], channel_multiplier=-1).then_inc(masked, 1)

            def section(s, j, r, exp, nxt):
                if nxt:
                    h, b = (s + 1) % H, (s + 1) // H
                    wait(pool, pv_done, (s - 1) * NBATCH + 1)
                    nc.gpsimd.tensor_copy(Vp[(r + 1) % R][:, :, 0:HD], c.V[:, bass.ds(h, 1), bass.ds(b * 4, 4), :, :]
                                          .rearrange("p h c i d -> p (h c i) d")).then_inc(v_staged, 1)
                if exp:
                    mask_probs(s, 0)
                    pool.wait_ge(misc_read, reads(s, "A") + 1)
                    nc.gpsimd.tensor_tensor(A_b[:], A[:], b_tile[:], ALU.mult).then_inc(newton_pool, 1)
                    pool.wait_ge(newton_pool, s * 2 + 1)
                    nc.gpsimd.tensor_tensor(Z[:], A_b[:], a_ident[:], ALU.add).then_inc(newton_pool, 1)
                    for g in range(1, G):
                        mask_probs(s, g)

            sections(pool, section)

        @block.vector
        def _(dve):
            dve.wait_ge(made, 18)

            def negate_maxima(s, r, f):
                half = neg_max_b[r][:, f]
                nc.vector.tensor_reduce(neg_max[r][:, f, :], chunk_max[r][:, f * NQ // 2:(f + 1) * NQ // 2, :],
                                        axis=AX.X, op=ALU.max, negate=True).then_inc(neg_max_steps, 1)
                dve.wait_ge(neg_max_steps, s * 6 + (3 * f + 1))
                nc.vector.tensor_copy(half[:, 0, :], neg_max[r][:, f, :]).then_inc(neg_max_steps, 1)
                dve.wait_ge(neg_max_steps, s * 6 + (3 * f + 2))
                nc.vector.tensor_tensor(half[:, 1, :], neg_max[r][:, f, :], half[:, 0, :], ALU.subtract)\
                  .then_inc(neg_max_steps, 1)

            def normalise(s):
                dve.wait_ge(combined, s * G)
                nc.vector.reciprocal(inv[:], comb3[:, :, HD]).then_inc(inv_done, 1)
                dve.wait_ge(inv_done, s)
                nc.vector.tensor_tensor(c.A_out[:, :, bass.ds(s - 1, 1), :].rearrange("p i s d -> p i (s d)"),
                                        comb3[:, :, 0:HD], inv[:].unsqueeze(2).broadcast_to([P, NQ, HD]), ALU.mult)\
                  .then_inc(misc_read, 1)

            def newton(s):
                dve.wait_ge(newton_mm, s * 3 + 2)
                dve.wait_ge(newton_pool, s * 2 + 2)
                nc.vector.scalar_tensor_tensor(out=Y[:], in0=newton_ps[:, 0:D], scalar=NEWTON[2], in1=Z[:],
                                               op0=ALU.mult, op1=ALU.add).then_inc(misc_read, 1)

            def section(s, j, r, exp, nxt):
                first = isinstance(s, int) and s <= 0
                r1 = (r + 1) % R
                for k, (i, ck) in enumerate(MAXES if nxt else []):
                    dve.wait_ge(max_scored, (s + 1) * NS + (k + 1))
                    scores, out = ps_max[(k + r1) % R], chunk_max[r1][:, i, ck:ck + 1]
                    if ck < i // 4:
                        nc.vector.tensor_reduce(out, scores[:], axis=AX.X, op=ALU.max).then_inc(max_reduced, 1)
                    else:
                        w = (i % 4 + 1) * P
                        dve.sem_inc(diagonals, 1)
                        nc.vector.tensor_tensor_reduce(out=scores[:, 0:w], in0=scores[:, 0:w], in1=c.mask[:, 4 * P - w:],
                                                       scale=1.0, scalar=LEAST, op0=ALU.add, op1=ALU.max,
                                                       accum_out=out).then_inc(max_reduced, 1)
                    if k == FIRST_MAXES - 1:
                        dve.wait_ge(max_reduced, (s + 1) * NS + (k + 1))
                        negate_maxima(s + 1, r1, 0)
                        if exp and not first:
                            normalise(s)
                    if k == 15 and exp:
                        newton(s)
                if nxt:
                    dve.wait_ge(max_reduced, (s + 1) * NS + NS)
                    negate_maxima(s + 1, r1, 1)
                else:
                    normalise(s)
                    newton(s)

            sections(dve, section)
            normalise(NH)
            dve.wait_ge(misc_read, reads(NH - 1, "end", False) + 1)

        @block.scalar
        def _(act):
            act.wait_ge(made, 14)

            def copy_rows(s, j, r, f):
                act.wait_ge(rows_in_psum, s * 2 + (f + 1))
                wait(act, max_rows_stored[f], s * 16)
                nc.scalar.activation(max_rows[f][:], rows_ps, ACT.Copy).then_inc(misc_read, 1)

            def copy_group(s, g):
                batches = s * NBATCH + (GROUP_END[g] + 1)
                act.wait_ge(pv_done, batches)
                wait(act, combined, s * G + (g - 1))
                nc.scalar.activation(O_sb[g % 2][:], ps_o[:], ACT.Copy).then_inc(o_copied, 1)

            def section(s, j, r, exp, nxt):
                if not exp:
                    copy_rows(0, 0, 0, 0)
                    return
                first = isinstance(s, int) and s == 0
                for n in range(NBATCH):
                    wait(act, pv_done, s * NBATCH + (1 - NBATCH if n == 0 else n - 3 if n <= 3 else n - 2))
                    for q in range(4):
                        k = 4 * n + q
                        g, kt = STEPS[k]
                        q0 = max(0, kt - 4 * g) * P
                        dst = (probs0[:, q, q0:] if n == 0 else probs[:, n % 3 * 4 + q, q0:])
                        act.wait_ge(scored, s * NS + (k + 1))
                        nc.scalar.activation(dst, ps_s[(k + r) % R][:, q0:], ACT.Exp, scale=SCALE).then_inc(exp_done, 1)
                    if n == 0:
                        copy_rows(s, j, r, 1)
                        if not first:
                            copy_group(s - 1, G - 1)
                    if n == 1:
                        act.wait_ge(newton_mm, s * 3 + 1)
                        nc.scalar.activation(A[:], newton_ps[:, 0:D], ACT.Copy).then_inc(misc_read, 1)
                    for g in range(G - 1):
                        if n == GROUP_END[g] + 1:
                            copy_group(s, g)
                    if n == 4 and nxt:
                        copy_rows(s + 1, *following(j, r), 0)
                    if n == 6:
                        act.wait_ge(newton_mm, s * 3 + 3)
                        nc.scalar.activation(c.S[:].rearrange("p a d -> p (a d)"), newton_ps, ACT.Copy)\
                          .then_inc(misc_read, 1)

            sections(act, section)
            copy_group(NH - 1, G - 1)

        @block.tensor
        def _(pe):
            pe.wait_ge(made, 18)

            def score(s, j, r, k):
                g, kt = STEPS[k]
                q0 = max(0, kt - 4 * g) * P
                if k == 0:
                    pe.wait_ge(max_rows_loaded[r][0], j * 16 + 16)
                if k == 12:
                    pe.wait_ge(max_rows_loaded[r][1], j * 16 + 16)
                wait(pe, exp_done, s * NS + (k - 2))
                nc.tensor.matmul(ps_s[(k + r) % R][:, q0:], K[r][:, kt * P:(kt + 1) * P],
                                 Q[r][:, g * QW + q0:(g + 1) * QW], start=True, stop=True).then_inc(scored, 1)

            def score_for_max(s, j, r, k):
                i, ck = MAXES[k]
                w = QW if ck < i // 4 else (i % 4 + 1) * P
                if k == 0:
                    pe.wait_ge(stacks_loaded[r], j * 192 + 192)
                wait(pe, max_reduced, s * NS + (k - 2))
                nc.tensor.matmul(ps_max[(k + r) % R][:, 0:w], Q[r][0:MROW, i * P:(i + 1) * P],
                                 K[r][0:MROW, ck * QW:ck * QW + w], start=True, stop=True).then_inc(max_scored, 1)

            def products(s, r, n):
                if n in GROUP_END.values():
                    pe.wait_ge(masked, s * 4 * G + 4 * (STEPS[4 * n][0] + 1))
                else:
                    pe.wait_ge(exp_done, s * NS + 4 * (n + 1))
                if n == 0:
                    pe.wait_ge(v_staged, s + 1)
                g = STEPS[4 * n][0]
                if STEPS[4 * n][1] == 0:
                    wait(pe, o_copied, s * G + g)
                for q in range(4):
                    kt = STEPS[4 * n + q][1]
                    q0 = max(0, kt - 4 * g) * P if n else 0
                    src = probs[:, n % 3 * 4 + q, q0:] if n else probs0[:, q, :]
                    last = nc.tensor.matmul(ps_o[32 * q:32 * q + 32, q0:], Vp[r][:, kt, :], src,
                                            start=kt < 4, stop=kt >= 4 * g)
                last.then_inc(pv_done, 1)

            def combine(s, g):
                pe.wait_ge(o_copied, s * G + (g + 1))
                for t in range(4):
                    last = nc.tensor.matmul(comb3[:, 4 * g + t, 0:HD + 1], O_sb[g % 2][:, t * P:(t + 1) * P], c.select[:],
                                            start=True, stop=True)
                last.then_inc(combined, 1)

            def turn_rows(s, r, f):
                pe.wait_ge(neg_max_steps, s * 6 + 3 * (f + 1))
                nc.tensor.transpose(rows_ps, neg_max_b[r][:, f].rearrange("p a i -> p (a i)"), c.ident_b[:])\
                  .then_inc(rows_in_psum, 1)

            def between(s, j, r, n, exp, nxt):
                first = isinstance(s, int) and s == 0
                j1, r1 = following(j, r)

                def misc(name):
                    wait(pe, misc_read, reads(s, name, nxt))

                if not exp:
                    if n == 4:
                        turn_rows(0, 0, 0)
                    return
                if n == 0:
                    misc("rows1")
                    turn_rows(s, r, 1)
                    if not first:
                        products(s - 1, (r - 1) % R, NBATCH - 1)
                else:
                    products(s, r, n - 1)
                if n == 1:
                    misc("A")
                    nc.tensor.matmul(newton_ps[:, 0:D], c.S[:, 0, :], c.S[:, 0, :], start=True, stop=True)\
                      .then_inc(newton_mm, 1)
                if n == 2 and not first:
                    misc("comb")
                    combine(s - 1, G - 1)
                if n == 3:
                    misc("Y")
                    combine(s, 0)
                    nc.tensor.matmul(newton_ps[:, 0:D], A[:], A[:], start=True, stop=True).then_inc(newton_mm, 1)
                if n == 4 and nxt:
                    misc("rows0")
                    turn_rows(s + 1, r1, 0)
                if n == 5:
                    misc("X")
                    combine(s, 1)
                if n == 6:
                    nc.tensor.matmul(newton_ps[:, 0:D], c.S[:, 1, :], Y[:], start=True, stop=True)
                    nc.tensor.matmul(newton_ps[:, D:], Y[:], c.S[:, 1, :], start=True, stop=True).then_inc(newton_mm, 1)
                if n == 8:
                    misc("end")
                    combine(s, 2)

            def section(s, j, r, exp, nxt):
                j1, r1 = following(j, r)
                for n in range(NBATCH):
                    for k in range(4 * n, 4 * n + 4):
                        if exp:
                            score(s, j, r, k)
                        if nxt:
                            score_for_max(s + 1, j1, r1, k)
                        if k == 4 * n + MIDDLE:
                            between(s, j, r, n, exp, nxt)

            pe.wait_ge(ones_loaded, 16 * R)
            sections(pe, section)
            products(NH - 1, (NH - 1) % R, NBATCH - 1)
            combine(NH - 1, G - 1)


def project_out(nc, c):
    TC = 4
    NCH = NT // TC
    with ExitStack() as cx:
        sem = stage_semaphores(nc, cx, "project_out_")

        aT = [cx.enter_context(nc.sbuf_tensor(f"aT{u}", [P, TC * P], fp32)) for u in range(2)]
        psT = [cx.enter_context(nc.psum_tensor(f"ps_aT{u}", [P, TC * P], fp32)) for u in range(2)]
        psY = [cx.enter_context(nc.psum_tensor(f"ps_y{u}", [P, TC * D], fp32)) for u in range(2)]
        aT_in_psum, aT_copied, y_in_psum, y_done = (sem(n) for n in ("aT_in_psum", "aT_copied", "y_in_psum", "y_done"))
        block = cx.enter_context(nc.Block())

        @block.tensor
        def _(pe):
            def turn(ch):
                if ch >= 2:
                    pe.wait_ge(aT_copied, ch - 1)
                for t in range(ch * TC, (ch + 1) * TC):
                    b, i = divmod(t, NT // B)
                    last = nc.tensor.transpose(psT[ch % 2][:, t % TC * P:(t % TC + 1) * P],
                                               c.A_out[:, i, b * H:(b + 1) * H, :].rearrange("p h d -> p (h d)"), c.ident[:])
                last.then_inc(aT_in_psum, 1)

            turn(0)
            for ch in range(NCH):
                if ch + 1 < NCH:
                    turn(ch + 1)
                pe.wait_ge(aT_copied, ch + 1)
                if ch >= 2:
                    pe.wait_ge(y_done, ch - 1)
                for i in range(TC):
                    last = nc.tensor.matmul(psY[ch % 2][:, i * D:(i + 1) * D], aT[ch % 2][:, i * P:(i + 1) * P], c.Wo_T[:],
                                            start=True, stop=True)
                last.then_inc(y_in_psum, 1)

        @block.scalar
        def _(act):
            for ch in range(NCH):
                act.wait_ge(aT_in_psum, ch + 1)
                if ch >= 2:
                    act.wait_ge(y_in_psum, ch - 1)
                nc.scalar.activation(aT[ch % 2][:], psT[ch % 2][:], ACT.Copy).then_inc(aT_copied, 1)

        @block.vector
        def _(dve):
            for ch in range(NCH):
                dve.wait_ge(y_in_psum, ch + 1)
                x = c.X[:, ch * TC:(ch + 1) * TC, :].rearrange("p i d -> p (i d)")
                nc.vector.tensor_tensor(x, psY[ch % 2][:], x, ALU.add).then_inc(y_done, 1)
            dve.wait_ge(y_done, NCH)


E_ = 16
F = 512
CAP = (N + E_ - 1) // E_
ROW = D + 2
RANK_STEP, ONEHOT_STEP = 9, 10


def moe(nc, c, name, Wg, w1, w2, dispatched, routed):
    J = NT
    TC = 4
    NCH = J // TC
    S2 = CAP // P
    FT = F // P
    with ExitStack() as cx:
        def sb(n, shape, dt=fp32):
            return cx.enter_context(nc.sbuf_tensor(f"{name}_{n}", shape, dt))

        def ps(n, shape):
            return cx.enter_context(nc.psum_tensor(f"{name}_{n}", shape, fp32))

        sem = stage_semaphores(nc, cx, f"{name}_")

        X = c.X
        Wg_sb = sb("Wg", [P, E_])
        st = sb("st", [P, J, 6])
        tmp = sb("tmp", [P, 4, J])
        mean, var, std, rstd = (sb(n, [P, J]) for n in ("mean", "var", "std", "rstd"))
        xs = [sb(f"xs{u}", [P, TC, D]) for u in range(2)]
        xsT = [sb(f"xsT{u}", [P, TC * P]) for u in range(2)]
        rows = sb("rows", [P, J, ROW])
        best = sb("best", [P, J])
        work = sb("work", [P, J, E_])
        expd = sb("expd", [P, J, E_])
        weight = sb("weight", [P, J, E_])
        rank = sb("rank", [P, J])
        onehot = sb("onehot", [P, J + 1, E_])
        restart = sb("restart", [P, E_, J])
        totals = sb("totals", [P, E_, J])
        earlier = sb("earlier", [P, E_, J])
        place = sb("place", [P, J, E_])
        token = sb("token", [P, J])
        small = sb("small", [P, 8, J])
        slot_i = sb("slot_i", [P, J], i32)
        up_to = sb("up_to", [P, P])
        ones = sb("ones", [P, P])
        blank = sb("blank", [P, J, ROW])
        w1_sb = sb("w1", [P, E_, F])
        w2_sb = sb("w2", [P, E_, FT, D])
        d_sb = blank
        dT = [sb(f"dT{u}", [P, CAP]) for u in range(2)]
        hT = [sb(f"hT{u}", [P, FT, CAP]) for u in range(2)]
        y = [sb(f"y{u}", [P, S2, D]) for u in range(2)]
        to_row = [sb(f"to_row{u}", [P, S2], i32) for u in range(2)]
        psD = [ps(f"psD{u}", [P, 512]) for u in range(2)]
        psH = [ps(f"psH{u}", [P, 1024]) for u in range(2)]
        psY = [ps(f"psY{u}", [P, 512]) for u in range(2)]
        logits, counts = (t[:].rearrange("p (j e) -> p j e", e=E_) for t in psY)

        wg_loaded, made, blanked, blank_made = (sem(n) for n in ("wg_loaded", "made", "blanked", "blank_made"))
        stats, steps_done, std_done = sem("stats"), sem("steps"), sem("std_done")
        xs_in_psum, xsT_copied, logits_in_psum = (sem(n) for n in ("xs_in_psum", "xsT_copied", "logits_in_psum"))
        xs_ready, rows_copied, exp_done, counts_in_psum, counted = (
            sem(n) for n in ("xs_ready", "rows_copied", "exp_done", "counts_in_psum", "counted"))
        slots_ready, scattered = sem("slots_ready"), sem("scattered")
        w_loaded, d_loaded = sem("w_loaded"), sem("d_loaded")
        d_in_psum, d_copied, h_in_psum, h_act, h_dve, y_in_psum, y_done, ids_done = (
            sem(n) for n in ("d_in_psum", "d_copied", "h_in_psum", "h_act", "h_dve", "y_in_psum", "y_done", "ids_done"))
        y_sent = [sem(f"y_sent{u}") for u in range(2)]
        block = cx.enter_context(nc.Block())

        @block.sync
        def _(sp):
            sp.dma_start(Wg_sb[:], Wg).then_inc(wg_loaded, 16)
            for e in range(0, E_, 2):
                sp.dma_start(w1_sb[:, e:e + 2, :], w1[e:e + 2, :, :].rearrange("e m f -> m e f")).then_inc(w_loaded, 16)
                sp.dma_start(w2_sb[:, e:e + 2, :, :].rearrange("p e f m -> p (e f) m"),
                             w2[e:e + 2, :, :].rearrange("e (f p) m -> p (e f) m", p=P)).then_inc(w_loaded, 16)
                if e == 0:
                    sp.wait_ge(blank_made, 2)
                    sp.dma_start(dispatched[0:N, :].rearrange("(p j) w -> p j w", j=J), blank[:]).then_inc(blanked, 16)
                    sp.dma_start(routed[0:N, :].rearrange("(p j) w -> p j w", j=J), blank[:, :, 0:D])\
                      .then_inc(blanked, 16)
            sp.wait_ge(scattered, 16 * J)
            for e in range(0, E_, 2):
                if e:
                    sp.wait_ge(d_loaded, e // 2 * 16)
                sp.dma_start(d_sb[:, e * S2:(e + 2) * S2, :],
                             dispatched[e * CAP:(e + 2) * CAP, :].rearrange("(s p) w -> p s w", p=P)).then_inc(d_loaded, 16)

        @block.gpsimd
        def _(pool):
            nc.gpsimd.memset(blank[:], 0.0).then_inc(blank_made, 1)
            nc.gpsimd.memset(restart[:], 1.0).then_inc(made, 1)
            nc.gpsimd.memset(up_to[:], 1.0).then_inc(made, 1)
            nc.gpsimd.memset(ones[:], 1.0).then_inc(made, 1)
            nc.gpsimd.memset(onehot[:, 0, :], 0.0).then_inc(made, 1)
            nc.gpsimd.iota(weight[:], pattern=[[0, J], [-1, E_]], base=E_, channel_multiplier=0,
                           allow_small_or_imprecise_dtypes=True).then_inc(made, 1)
            nc.gpsimd.iota(token[:], pattern=[[P, J]], base=0, channel_multiplier=1,
                           allow_small_or_imprecise_dtypes=True).then_inc(made, 1)
            pool.wait_ge(blank_made, 1)
            pool.wait_ge(made, 6)
            nc.gpsimd.iota(blank[:, :, D:D + 1], pattern=[[1, J]], base=N, channel_multiplier=J,
                           allow_small_or_imprecise_dtypes=True).then_inc(blank_made, 1)
            nc.gpsimd.memset(restart[:, :, 0:1], 0.0).then_inc(made, 1)
            nc.gpsimd.affine_select(out=up_to[:], in_=up_to[:], compare_op=ALU.is_ge, fill=0.0, base=0,
                                    pattern=[[1, P]], channel_multiplier=-1).then_inc(made, 1)
            with pool.Fori(0, NCH // 2) as it:
                for u in range(2):
                    ch = it * 2 + u
                    pool.wait_ge(xs_ready, (ch + 1) * TC)
                    nc.gpsimd.tensor_copy(rows[:, bass.ds(ch * TC, TC), 0:D], xs[u][:]).then_inc(rows_copied, 1)
            pool.wait_ge(rows_copied, NCH + 2)
            pool.wait_ge(slots_ready, 3)
            pool.wait_ge(blanked, 32)
            for j in range(J):
                pool.indirect_dma_start(dispatched, bass.IndirectOffsetOnAxis(ap=slot_i[:, j:j + 1], axis=0),
                                        rows[:, j, :], None).then_inc(scattered, 16)

            for e in range(E_):
                pool.wait_ge(ids_done, e + 1)
                for s in range(S2):
                    pool.wait_ge(y_done, e * S2 + s + 1)
                    pool.indirect_dma_start(routed, bass.IndirectOffsetOnAxis(ap=to_row[e % 2][:, s:s + 1], axis=0),
                                            y[e % 2][:, s, :], None).then_inc(y_sent[e % 2], 16)
            for u in range(2):
                pool.wait_ge(y_sent[u], E_ // 2 * S2 * 16)

        @block.vector
        def _(dve):
            steps = Steps(dve, steps_done)
            with dve.Fori(0, J // 8) as k:
                for j in range(8):
                    nc.vector.bn_stats(st[:, bass.ds(k * 8 + j, 1), :], X[:, bass.ds(k * 8 + j, 1), :]).then_inc(stats, 1)
            dve.wait_ge(stats, J)
            finish_stats(nc, steps, st, tmp, mean[:], var[:])
            dve.wait_ge(std_done, 1)
            steps.then(nc.vector.reciprocal(rstd[:], std[:]))
            with dve.Fori(0, NCH // 2) as it:
                for u in range(2):
                    ch = it * 2 + u
                    dve.wait_ge(xs_in_psum, ch + 1)
                    dve.wait_ge(rows_copied, ch + 1)
                    for i in range(TC):
                        j = ch * TC + i
                        nc.vector.tensor_scalar(xs[u][:, i, :], X[:, bass.ds(j, 1), :].rearrange("p o d -> p (o d)"),
                                                mean[:, bass.ds(j, 1)], rstd[:, bass.ds(j, 1)], ALU.subtract, ALU.mult)\
                          .then_inc(xs_ready, 1)
            dve.wait_ge(logits_in_psum, NCH + 2)
            dve.wait_ge(made, 8)
            per_token = [P, J, E_]
            steps.then(nc.vector.tensor_reduce(best[:], logits, axis=AX.X, op=ALU.max))
            best_b = best[:].unsqueeze(2).broadcast_to(per_token)
            steps.then(nc.vector.tensor_tensor(work[:], logits, best_b, ALU.is_equal))
            nc.vector.tensor_tensor(expd[:], logits, best_b, ALU.subtract).then_inc(slots_ready, 1)
            steps.then(nc.vector.tensor_tensor(work[:], work[:], weight[:], ALU.mult))
            steps.then(nc.vector.tensor_reduce(rank[:], work[:], axis=AX.X, op=ALU.max))
            steps.then(nc.vector.tensor_tensor(onehot[:, 1:, :], weight[:],
                                               rank[:].unsqueeze(2).broadcast_to(per_token), ALU.is_equal))
            assert steps.n == ONEHOT_STEP
            dve.wait_ge(counted, 1)
            steps.then(nc.vector.tensor_tensor_scan(out=earlier[:].rearrange("p e j -> p (e j)"),
                                                    data0=restart[:].rearrange("p e j -> p (e j)"),
                                                    data1=totals[:].rearrange("p e j -> p (e j)"), initial=0.0,
                                                    op0=ALU.mult, op1=ALU.add))
            steps.then(nc.vector.tensor_tensor(place[:], counts, earlier[:].rearrange("p e j -> p j e"), ALU.add))
            steps.then(nc.vector.tensor_tensor(place[:], place[:], onehot[:, 1:, :], ALU.mult))
            loc1, valid, first_slot, slot, trash, diff, dest, total = (small[:, k, :] for k in range(8))
            steps.then(nc.vector.tensor_reduce(loc1, place[:], axis=AX.X, op=ALU.add))
            nc.vector.tensor_scalar(valid, loc1, float(CAP), None, ALU.is_le)
            nc.vector.tensor_scalar(trash, token[:], float(N), None, ALU.add)
            steps.then(nc.vector.tensor_scalar(first_slot, rank[:], -float(CAP), float(E_ * CAP - 1), ALU.mult, ALU.add))
            steps.then(nc.vector.tensor_tensor(slot, first_slot, loc1, ALU.add))
            steps.then(nc.vector.tensor_tensor(diff, slot, trash, ALU.subtract))
            steps.then(nc.vector.tensor_tensor(slot, diff, valid, ALU.mult))
            steps.then(nc.vector.tensor_tensor(dest, slot, trash, ALU.add))
            nc.vector.tensor_copy(slot_i[:], dest).then_inc(slots_ready, 1)
            nc.vector.tensor_copy(rows[:, :, D], token[:])
            dve.wait_ge(exp_done, 1)
            steps.then(nc.vector.tensor_reduce(total, work[:], axis=AX.X, op=ALU.add))
            nc.vector.reciprocal(rows[:, :, D + 1], total).then_inc(slots_ready, 1)

            for e in range(E_):
                u = e % 2
                dve.wait_ge(d_loaded, (e // 2 + 1) * 16)
                if e >= 2:
                    dve.wait_ge(y_sent[u], e // 2 * 32)
                nc.vector.tensor_copy(to_row[u][:], d_sb[:, e * S2:(e + 1) * S2, D]).then_inc(ids_done, 1)
                dve.wait_ge(h_in_psum, e * 2 + 2)
                nc.vector.tensor_scalar(hT[u][:, FT // 2:, :].rearrange("p f s -> p (f s)"), psH[u][:, F:], 0.0, None,
                                        ALU.max).then_inc(h_dve, 1)
                dve.wait_ge(y_in_psum, e + 1)
                for s in range(S2):
                    nc.vector.tensor_scalar(y[u][:, s, :], psY[u][:, s * D:(s + 1) * D],
                                            d_sb[:, e * S2 + s, D + 1:D + 2], None, ALU.mult).then_inc(y_done, 1)

        @block.scalar
        def _(act):
            act.sem_inc(xsT_copied, 2)
            act.wait_ge(steps_done, 4)
            nc.scalar.activation(std[:], var[:], ACT.Sqrt).then_inc(std_done, 1)
            with act.Fori(0, NCH // 2) as it:
                for u in range(2):
                    ch = it * 2 + u
                    act.wait_ge(xs_in_psum, ch + 3)
                    act.wait_ge(logits_in_psum, ch + 1)
                    nc.scalar.activation(xsT[u][:], psH[u][:, 0:TC * P], ACT.Copy).then_inc(xsT_copied, 1)
            act.wait_ge(counts_in_psum, 2)
            nc.scalar.activation(totals[:].rearrange("p e j -> p j e"), psD[0][:].rearrange("p (j e) -> p j e", e=E_),
                                 ACT.Copy).then_inc(counted, 1)
            act.wait_ge(slots_ready, 1)
            act.wait_ge(steps_done, RANK_STEP)
            nc.scalar.activation(work[:], expd[:], ACT.Exp).then_inc(exp_done, 1)

            def copy_rows(e):
                act.wait_ge(d_in_psum, e + 1)
                if e >= 2:
                    act.wait_ge(h_in_psum, e * 2 - 2)
                nc.scalar.activation(dT[e % 2][:], psD[e % 2][:, 0:CAP], ACT.Copy).then_inc(d_copied, 1)

            copy_rows(0)
            copy_rows(1)
            for e in range(E_):
                act.wait_ge(h_in_psum, e * 2 + 1)
                if e >= 2:
                    act.wait_ge(y_in_psum, e - 1)
                nc.scalar.activation(hT[e % 2][:, 0:FT // 2, :].rearrange("p f s -> p (f s)"), psH[e % 2][:, 0:F], ACT.Relu)\
                  .then_inc(h_act, 1)
                if e + 2 < E_:
                    copy_rows(e + 2)

        @block.tensor
        def _(pe):
            pe.sem_inc(xs_in_psum, 2)
            pe.sem_inc(logits_in_psum, 2)
            pe.sem_inc(rows_copied, 2)
            pe.wait_ge(wg_loaded, 16)
            def turn_tokens(ch, u):
                pe.wait_ge(xs_ready, (ch + 1) * TC)
                pe.wait_ge(xsT_copied, ch + 1)
                for i in range(TC):
                    last = nc.tensor.transpose(psH[u][:, i * P:(i + 1) * P], xs[u][:, i, :], c.ident[:])
                last.then_inc(xs_in_psum, 1)

            def gate(ch, u):
                pe.wait_ge(xsT_copied, ch + 3)
                for i in range(TC):
                    last = nc.tensor.matmul(logits[:, bass.ds(ch * TC + i, 1), :].rearrange("p j e -> p (j e)"),
                                            xsT[u][:, i * P:(i + 1) * P], Wg_sb[:], start=True, stop=True)
                last.then_inc(logits_in_psum, 1)

            turn_tokens(0, 0)
            with pe.Fori(0, NCH // 2 - 1) as it:
                for u in range(2):
                    turn_tokens(it * 2 + u + 1, 1 - u)
                    gate(it * 2 + u, u)
            turn_tokens(NCH - 1, 1)
            for u in range(2):
                gate(NCH - 2 + u, u)
            pe.wait_ge(steps_done, ONEHOT_STEP)
            pe.wait_ge(made, 8)
            nc.tensor.matmul(psD[0][:], ones[:], onehot[:, 0:J, :].rearrange("p j e -> p (j e)"), start=True, stop=True)\
              .then_inc(counts_in_psum, 1)
            nc.tensor.matmul(psY[1][:], up_to[:], onehot[:, 1:, :].rearrange("p j e -> p (j e)"), start=True, stop=True)\
              .then_inc(counts_in_psum, 1)
            pe.wait_ge(steps_done, ONEHOT_STEP + 2)

            def turn(e):
                pe.wait_ge(d_loaded, (e // 2 + 1) * 16)
                if e >= 2:
                    pe.wait_ge(d_copied, e - 1)
                for s in range(S2):
                    last = nc.tensor.transpose(psD[e % 2][:, s * P:(s + 1) * P], d_sb[:, e * S2 + s, 0:D], c.ident[:])
                last.then_inc(d_in_psum, 1)

            def up(e):
                pe.wait_ge(d_copied, e + 1)
                if e >= 2:
                    pe.wait_ge(h_act, e - 1)
                    pe.wait_ge(h_dve, e - 1)
                for f in range(FT):
                    last = nc.tensor.matmul(psH[e % 2][:, f * CAP:(f + 1) * CAP], w1_sb[:, e, f * P:(f + 1) * P],
                                            dT[e % 2][:], start=True, stop=True)
                    if f % 2:
                        last.then_inc(h_in_psum, 1)

            def down(e):
                pe.wait_ge(h_act, e + 1)
                pe.wait_ge(h_dve, e + 1)
                if e >= 2:
                    pe.wait_ge(y_done, (e - 1) * S2)
                for s in range(S2):
                    for f in range(FT):
                        last = nc.tensor.matmul(psY[e % 2][:, s * D:(s + 1) * D], hT[e % 2][:, f, s * P:(s + 1) * P],
                                                w2_sb[:, e, f, :], start=f == 0, stop=f == FT - 1)
                last.then_inc(y_in_psum, 1)

            pe.wait_ge(w_loaded, 16 * E_)
            turn(0)
            turn(1)
            up(0)
            for e in range(E_):
                if e + 2 < E_:
                    turn(e + 2)
                if e + 1 < E_:
                    up(e + 1)
                down(e)


LANES = 4
W_LANE = D // LANES
SC = 4
CW = N // SC // P
SHIFTS = [1 << k for k in range(T.bit_length() - 1)]
PAD = SHIFTS[-1]
RMS_EPS = 1e-8


def scan_tensors(nc, cx, c):
    def sb(name, shape, dt=fp32):
        return cx.enter_context(nc.sbuf_tensor(name, shape, dt))
    c.X2 = c.X[:].rearrange("p (c j) d -> p c j d", c=SC)
    c.q = sb("q", [P, SC, CW, D])
    c.v2 = sb("v2", [P, SC, CW, D])
    c.Wproj_T = sb("Wproj_T", [P, D])
    c.L = [sb(f"L{ch}", [P, CW, D]) for ch in range(SC)]
    c.U = [sb(f"U{u}", [P, CW, D]) for u in range(2)]
    c.UT = [sb(f"UT{u}", [P, CW * P]) for u in range(2)]


def token_rows(t, ch):
    return t.rearrange("(c j p) d -> p c j d", c=SC, j=CW)[:, bass.ds(ch, 1), :, :].rearrange("p c j d -> p (c j) d")


def padded_rows(t, ch, shift=0):
    first = ch // (SC // B) * (PAD + T) + PAD + ch % (SC // B) * (CW * P) - shift
    return t[first:first + CW * P, :].rearrange("(j p) d -> p j d", j=CW)


def scan_inputs(nc, c, routed, W_up, W_v, W_proj, identity, scanned):
    with ExitStack() as cx:
        def sb(name, shape, dt=fp32):
            return cx.enter_context(nc.sbuf_tensor(name, shape, dt))

        def ps(name):
            return cx.enter_context(nc.psum_tensor(name, [P, CW * P], fp32))

        sem = stage_semaphores(nc, cx, "scan_inputs_")

        W_nat = sb("Wb_nat", [P, 3, D])
        W_T = sb("Wb_T", [P, 2, D])
        st = sb("st_b", [P, NT, 6])
        tmp = sb("tmp_b", [P, 4, NT])
        mean, var, std, rstd = (sb(n, [P, NT]) for n in ("mean_b", "var_b", "std_b", "rstd_b"))
        ident_row = sb("ident_row", [P, D])
        psT, psQ, psV = ps("psT_b"), ps("psQ_b"), ps("psV_b")

        loaded = [sem(f"loaded{ch}") for ch in range(SC)]
        w_loaded, identity_loaded, padded, q_stored = sem("w_loaded"), sem("identity_loaded"), sem("padded"), sem("q_stored")
        summed, stats, stat_steps, std_done, rstd_done = (
            sem(n) for n in ("summed", "stats", "stat_steps", "std_done", "rstd_done"))
        wT_in_psum, wT_copied = sem("wT_in_psum"), sem("wT_copied")
        xn_ready, xT_in_psum, xT_copied, q_in_psum, v_in_psum, q_copied, v_copied = (
            sem(n) for n in ("xn_ready", "xT_in_psum", "xT_copied", "q_in_psum", "v_in_psum", "q_copied", "v_copied"))
        block = cx.enter_context(nc.Block())

        @block.sync
        def _(sp):
            for ch in range(SC):
                sp.dma_start(c.L[ch][:], token_rows(routed, ch)).then_inc(loaded[ch], 16)
            for m, w in enumerate((W_up, W_v, W_proj)):
                sp.dma_start(W_nat[:, m, :], w).then_inc(w_loaded, 16)
            sp.dma_start(ident_row[:], identity.rearrange("(a d) -> a d", a=1).broadcast_to([P, D]))\
              .then_inc(identity_loaded, 16)
            sp.wait_ge(identity_loaded, 16)
            for t in scanned:
                for b in range(B):
                    pads = t[b * (PAD + T):b * (PAD + T) + PAD, :].rearrange("(p j) d -> p j d", j=PAD // P)
                    sp.dma_start(pads, ident_row[:].unsqueeze(1).broadcast_to([P, PAD // P, D])).then_inc(padded, 16)
            for ch in range(SC):
                sp.wait_ge(q_copied, ch + 1)
                sp.dma_start(padded_rows(scanned[0], ch), c.q[:, ch]).then_inc(q_stored, 16)
            sp.wait_ge(padded, 16 * B * len(scanned))
            sp.wait_ge(q_stored, 16 * SC)

        @block.gpsimd
        def _(pool):
            for ch in range(SC):
                pool.wait_ge(loaded[ch], 16)
                nc.gpsimd.tensor_tensor(c.X2[:, ch], c.X2[:, ch], c.L[ch][:], ALU.add).then_inc(summed, 1)

        @block.vector
        def _(dve):
            dve.wait_ge(wT_in_psum, 1)
            nc.vector.tensor_copy(W_T[:].rearrange("p m d -> p (m d)"), psT[:, 0:2 * D]).then_inc(wT_copied, 1)
            nc.vector.tensor_copy(c.Wproj_T[:], psT[:, 2 * D:3 * D]).then_inc(wT_copied, 1)
            tiles = c.X
            with dve.Fori(0, SC) as ch:
                dve.wait_ge(summed, ch + 1)
                for j in range(CW):
                    i = ch * CW + j
                    nc.vector.bn_stats(st[:, bass.ds(i, 1), :], tiles[:, bass.ds(i, 1), :]).then_inc(stats, 1)
            dve.wait_ge(stats, NT)
            finish_stats(nc, Steps(dve, stat_steps), st, tmp, mean[:], var[:])
            dve.wait_ge(std_done, 1)
            nc.vector.reciprocal(rstd[:], std[:]).then_inc(rstd_done, 1)
            dve.wait_ge(rstd_done, 1)
            for ch in range(SC + 1):
                if ch < SC:
                    if ch >= 2:
                        dve.wait_ge(xT_in_psum, ch - 1)
                    for j in range(CW):
                        i = ch * CW + j
                        last = nc.vector.tensor_scalar(c.U[ch % 2][:, j, :], c.X2[:, ch, j, :], mean[:, i:i + 1],
                                                       rstd[:, i:i + 1], ALU.subtract, ALU.mult)
                    last.then_inc(xn_ready, 1)
                if ch > 0:
                    dve.wait_ge(v_in_psum, ch)
                    nc.vector.tensor_copy(c.v2[:, ch - 1].rearrange("p j d -> p (j d)"), psV[:]).then_inc(v_copied, 1)
            dve.wait_ge(v_copied, SC)

        @block.scalar
        def _(act):
            act.wait_ge(stat_steps, 4)
            nc.scalar.activation(std[:], var[:], ACT.Sqrt).then_inc(std_done, 1)
            for ch in range(SC):
                act.wait_ge(xT_in_psum, ch + 1)
                if ch >= 2:
                    act.wait_ge(v_in_psum, ch - 1)
                nc.scalar.activation(c.UT[ch % 2][:], psT[:], ACT.Copy).then_inc(xT_copied, 1)
                act.wait_ge(q_in_psum, ch + 1)
                nc.scalar.activation(c.q[:, ch].rearrange("p j d -> p (j d)"), psQ[:], ACT.Copy).then_inc(q_copied, 1)

        @block.tensor
        def _(pe):
            pe.wait_ge(w_loaded, 48)
            for m in range(3):
                last = nc.tensor.transpose(psT[:, m * D:(m + 1) * D], W_nat[:, m, :], c.ident[:])
            last.then_inc(wT_in_psum, 1)
            pe.wait_ge(wT_copied, 2)
            for ch in range(SC):
                pe.wait_ge(xn_ready, ch + 1)
                if ch >= 1:
                    pe.wait_ge(xT_copied, ch)
                for j in range(CW):
                    last = nc.tensor.transpose(psT[:, j * P:(j + 1) * P], c.U[ch % 2][:, j, :], c.ident[:])
                last.then_inc(xT_in_psum, 1)
                pe.wait_ge(xT_copied, ch + 1)
                for m, (dst, read, ready) in enumerate(((psQ, q_copied, q_in_psum), (psV, v_copied, v_in_psum))):
                    if ch >= 1:
                        pe.wait_ge(read, ch)
                    for j in range(CW):
                        last = nc.tensor.matmul(dst[:, j * D:(j + 1) * D], c.UT[ch % 2][:, j * P:(j + 1) * P], W_T[:, m, :],
                                                start=True, stop=True)
                    last.then_inc(ready, 1)


def scan(nc, c, scanned):
    LA, LW, CE = LANES, W_LANE, CW * D
    NS = len(SHIFTS)
    G = NS * SC
    ROWS = CW * LA
    HEAD = 7
    with ExitStack() as cx:
        def sb(name, shape, dt=fp32):
            return cx.enter_context(nc.sbuf_tensor(name, shape, dt))

        def ps(name):
            return cx.enter_context(nc.psum_tensor(name, [P, CE], fp32))

        sem = stage_semaphores(nc, cx, "scan_")

        lane_products = [sb(f"lane_products{u}", [P, LA, ROWS, LW]) for u in range(2)]
        weighted = sb("weighted", [P, LA, ROWS, LW])
        v_sb = [sb(f"v_sb{u}", [P, CE]) for u in range(2)]
        z_normed = sb("z_normed", [P, CW, D])
        squares = sb("z_squares", [P, ROWS, LW])
        scores = sb("scores", [P, LA * CW, LA])
        best = sb("best_score", [P, LA * CW])
        shifted = sb("shifted_scores", [P, LA * CW, LA])
        expd = sb("exp_scores", [P, LA * CW, LA])
        total = sb("total", [P, LA * CW])
        share = sb("share", [P, LA * CW])
        att = [sb(f"att{u}", [P, LA, ROWS]) for u in range(2)]
        ss, log_ms, rs, rs_lane = (sb(n, [P, LA * CW]) for n in ("ss", "log_ms", "rs", "rs_lane"))
        lane_inv = sb("lane_inv", [P, LA, CW])
        eps = sb("rms_eps", [P, 1])
        psU, psZ = ps("psU"), ps("psZ")
        psV = [ps(f"psV_s{u}") for u in range(2)]

        l_loaded = [sem(f"l_loaded{ch}") for ch in range(SC)]
        x_stored = [sem(f"x_stored{ch}") for ch in range(SC)]
        made = sem("made_s")
        p1_pool, p2_pool, x_new = (sem(n) for n in ("p1_pool", "p2_pool", "x_new"))
        u_in_psum, uT_copied, v_in_psum, v_copied, z_in_psum = (
            sem(n) for n in ("u_in_psum", "uT_copied", "v_in_psum", "v_copied", "z_in_psum"))
        head_steps, p2_dve, ss_done, rs_steps, z_done = (
            sem(n) for n in ("head_steps", "p2_dve", "ss_done", "rs_steps", "z_done"))
        exp_done, squared, rs_log, rs_done = sem("exp_done"), sem("squared"), sem("rs_log"), sem("rs_done")
        block = cx.enter_context(nc.Block())

        def chunks(engine, section, lag):
            for ch in range(SC):
                section(ch, 0, ch, True)
            with engine.Fori(1, NS) as s:
                for ch in range(SC):
                    section(s * SC + ch, s, ch, True)
            for k in range(lag):
                section(G + k, NS, k, False)

        def wait(engine, semaphore, value):
            if not isinstance(value, int) or value > 0:
                engine.wait_ge(semaphore, value)

        def reached(g, lag):
            return not isinstance(g, int) or 0 <= g - lag < G

        @block.sync
        def _(sp):
            for ch in range(SC):
                sp.dma_start(c.L[ch][:], padded_rows(scanned[0], ch, SHIFTS[0])).then_inc(l_loaded[ch], 16)
            for s in range(NS - 1):
                for ch in range(SC):
                    sp.wait_ge(x_new, s * SC + ch + 1)
                    sp.dma_start(padded_rows(scanned[(s + 1) % 2], ch), c.q[:, ch]).then_inc(x_stored[ch], 16)
                    sp.wait_ge(x_stored[ch], 16 * (s + 1))
                    sp.dma_start(c.L[ch][:], padded_rows(scanned[(s + 1) % 2], ch, SHIFTS[s + 1]))\
                      .then_inc(l_loaded[ch], 16)

        def lane_product(engine, ch, l, out):
            return engine.tensor_tensor(
                out[:, l].rearrange("p (j m) d -> p j m d", m=LA),
                c.L[ch][:, :, l * LW:(l + 1) * LW].unsqueeze(2).broadcast_to([P, CW, LA, LW]),
                c.q[:, ch].rearrange("p j (m d) -> p j m d", m=LA), ALU.mult)

        @block.gpsimd
        def _(pool):
            for l in range(LA):
                nc.gpsimd.memset(lane_inv[:, l, :], 1.0 / (l + 1)).then_inc(made, 1)
            nc.gpsimd.memset(eps[:], RMS_EPS).then_inc(made, 1)

            def section(g, s, ch, head):
                u = ch % 2
                if head:
                    pool.wait_ge(l_loaded[ch], s * 16 + 16)
                    wait(pool, x_new, g - 3)
                    wait(pool, head_steps, (g - 2) * HEAD + 2)
                    lane_product(nc.gpsimd, ch, 1, lane_products[u])
                    lane_product(nc.gpsimd, ch, 2, lane_products[u])
                    lane_product(nc.gpsimd, ch, 3, lane_products[u]).then_inc(p1_pool, 1)
                if reached(g, 1):
                    pool.wait_ge(head_steps, (g - 1) * HEAD + HEAD)
                    pool.wait_ge(v_copied, g)
                    wait(pool, z_in_psum, g - 1)
                    nc.gpsimd.tensor_tensor(weighted[:, 3], att[1 - u][:, 3].unsqueeze(2).broadcast_to([P, ROWS, LW]),
                                            v_sb[1 - u][:].rearrange("p (r d) -> p r d", d=LW), ALU.mult)\
                      .then_inc(p2_pool, 1)
                if reached(g, 2):
                    pool.wait_ge(z_done, g - 1)
                    nc.gpsimd.tensor_tensor(c.q[:, (ch - 2) % SC], c.L[(ch - 2) % SC][:], z_normed[:], ALU.add)\
                      .then_inc(x_new, 1)

            chunks(pool, section, 2)
            pool.wait_ge(x_new, G)

        @block.vector
        def _(dve):
            dve.wait_ge(made, LA + 1)

            def section(g, s, ch, head):
                u = ch % 2
                if head:
                    dve.wait_ge(l_loaded[ch], s * 16 + 16)
                    wait(dve, x_new, g - 3)
                    steps = Steps(dve, head_steps, g * HEAD)
                    steps.then(lane_product(nc.vector, ch, 0, lane_products[u]))
                    dve.wait_ge(p1_pool, g + 1)
                    steps.then(nc.vector.tensor_reduce(scores[:].rearrange("p r m -> p (r m)"),
                                                       lane_products[u][:].rearrange("p l r d -> p (l r) d"),
                                                       axis=AX.X, op=ALU.add))
                    steps.then(nc.vector.tensor_reduce(best[:], scores[:], axis=AX.X, op=ALU.max))
                    steps.then(nc.vector.tensor_tensor(shifted[:], scores[:], best[:].unsqueeze(2)
                                                       .broadcast_to([P, LA * CW, LA]), ALU.subtract))
                if reached(g, 1):
                    dve.wait_ge(squared, g)
                    nc.vector.tensor_reduce(ss[:], squares[:], axis=AX.X, op=ALU.add).then_inc(ss_done, 1)
                if head:
                    dve.wait_ge(exp_done, g + 1)
                    steps.then(nc.vector.tensor_reduce(total[:], expd[:], axis=AX.X, op=ALU.add))
                    steps.then(nc.vector.reciprocal(share[:], total[:]))
                    steps.then(nc.vector.tensor_tensor(att[u][:].rearrange("p l (j m) -> p (l j) m", m=LA), expd[:],
                                                       share[:].unsqueeze(2).broadcast_to([P, LA * CW, LA]), ALU.mult))
                    assert steps.n == HEAD
                if reached(g, 1):
                    dve.wait_ge(rs_done, g)
                    nc.vector.tensor_tensor(rs_lane[:], rs[:], lane_inv[:].rearrange("p l j -> p (l j)"), ALU.mult)\
                      .then_inc(rs_steps, 1)
                    dve.wait_ge(rs_steps, g)
                    wait(dve, x_new, g - 1)
                    nc.vector.tensor_tensor(z_normed[:].rearrange("p j (l d) -> p l j d", l=LA),
                                            psZ[:].rearrange("p (l j d) -> p l j d", l=LA, d=LW),
                                            rs_lane[:].rearrange("p (l j) -> p l j", l=LA).unsqueeze(3)
                                            .broadcast_to([P, LA, CW, LW]), ALU.mult).then_inc(z_done, 1)
                if head:
                    dve.wait_ge(v_in_psum, g + 1)
                    dve.wait_ge(v_copied, g + 1)
                    wait(dve, z_in_psum, g)
                    for l in range(LA - 1):
                        nc.vector.tensor_tensor(weighted[:, l], att[u][:, l].unsqueeze(2).broadcast_to([P, ROWS, LW]),
                                                psV[u][:].rearrange("p (r d) -> p r d", d=LW), ALU.mult)\
                          .then_inc(p2_dve, 1)

            chunks(dve, section, 1)

        @block.scalar
        def _(act):
            act.preload_act_table_set("natural_log_exp_and_others")
            act.wait_ge(made, LA + 1)

            def section(g, s, ch, head):
                u = ch % 2
                if reached(g, 2):
                    act.wait_ge(z_in_psum, g - 1)
                    wait(act, ss_done, g - 2)
                    nc.scalar.activation(squares[:].rearrange("p r d -> p (r d)"), psZ[:], ACT.Square).then_inc(squared, 1)
                if reached(g, 1):
                    act.wait_ge(head_steps, (g - 1) * HEAD + 4)
                    nc.scalar.activation(expd[:], shifted[:], ACT.Exp, scale=W_LANE ** -0.5).then_inc(exp_done, 1)
                if head:
                    act.wait_ge(u_in_psum, g + 1)
                    wait(act, v_in_psum, g - 1)
                    nc.scalar.activation(c.UT[u][:], psU[:], ACT.Copy).then_inc(uT_copied, 1)
                if reached(g, 2):
                    act.wait_ge(ss_done, g - 1)
                    nc.scalar.activation(log_ms[:], ss[:], ACT.Ln, bias=eps[:], scale=1.0 / W_LANE).then_inc(rs_log, 1)
                    act.wait_ge(rs_log, g - 1)
                    nc.scalar.activation(rs[:], log_ms[:], ACT.Exp, scale=-0.5).then_inc(rs_done, 1)
                if head:
                    act.wait_ge(v_in_psum, g + 1)
                    wait(act, p2_pool, g - 1)
                    nc.scalar.activation(v_sb[u][:], psV[u][:], ACT.Copy).then_inc(v_copied, 1)

            chunks(act, section, 2)

        @block.tensor
        def _(pe):
            def section(g, s, ch, head):
                u = ch % 2
                if reached(g, 2):
                    pe.wait_ge(p2_pool, g - 1)
                    wait(pe, z_done, g - 2)
                    for l in (3, 0, 1, 2):
                        if l < 3:
                            pe.wait_ge(p2_dve, (g - 2) * 3 + (l + 1))
                        for m in range(LA):
                            last = nc.tensor.matmul(psZ[:, l * CW * LW:(l + 1) * CW * LW], c.ident[:],
                                                    weighted[:, l].rearrange("p (j m) d -> p j m d", m=LA)[:, :, m, :],
                                                    start=m == 0, stop=m == LA - 1)
                    last.then_inc(z_in_psum, 1)
                if head:
                    pe.wait_ge(l_loaded[ch], s * 16 + 16)
                    wait(pe, x_new, g - 3)
                    wait(pe, uT_copied, g)
                    for j in range(CW):
                        for k, t in enumerate((c.L[ch][:, j, :], c.q[:, ch, j, :])):
                            last = nc.tensor.matmul(psU[:, j * P:(j + 1) * P], t, c.ident[:], start=k == 0, stop=k == 1)
                    last.then_inc(u_in_psum, 1)
                    pe.wait_ge(uT_copied, g + 1)
                    wait(pe, p2_dve, (g - 1) * 3)
                    wait(pe, v_copied, g - 1)
                    for j in range(CW):
                        last = nc.tensor.matmul(psV[u][:, j * D:(j + 1) * D], c.UT[u][:, j * P:(j + 1) * P], c.S[:, 0, :],
                                                start=True, stop=True)
                    last.then_inc(v_in_psum, 1)

            chunks(pe, section, 2)


def scan_outputs(nc, c):
    with ExitStack() as cx:
        def ps(name):
            return cx.enter_context(nc.psum_tensor(name, [P, CW * P], fp32))

        sem = stage_semaphores(nc, cx, "scan_outputs_")

        psT = [ps(f"psT_o{u}") for u in range(2)]
        psY = [ps(f"psY_o{u}") for u in range(2)]
        gated, gT_in_psum, gT_copied, y_in_psum, y_done = (
            sem(n) for n in ("gated", "gT_in_psum", "gT_copied", "y_in_psum", "y_done"))
        block = cx.enter_context(nc.Block())

        @block.gpsimd
        def _(pool):
            for ch in range(SC):
                if ch >= 2:
                    pool.wait_ge(gT_in_psum, ch - 1)
                nc.gpsimd.tensor_tensor(c.U[ch % 2][:], c.q[:, ch], c.v2[:, ch], ALU.mult).then_inc(gated, 1)

        @block.tensor
        def _(pe):
            for ch in range(SC):
                pe.wait_ge(gated, ch + 1)
                if ch >= 2:
                    pe.wait_ge(gT_copied, ch - 1)
                for j in range(CW):
                    last = nc.tensor.transpose(psT[ch % 2][:, j * P:(j + 1) * P], c.U[ch % 2][:, j, :], c.ident[:])
                last.then_inc(gT_in_psum, 1)
                pe.wait_ge(gT_copied, ch + 1)
                if ch >= 2:
                    pe.wait_ge(y_done, ch - 1)
                for j in range(CW):
                    last = nc.tensor.matmul(psY[ch % 2][:, j * D:(j + 1) * D], c.UT[ch % 2][:, j * P:(j + 1) * P],
                                            c.Wproj_T[:], start=True, stop=True)
                last.then_inc(y_in_psum, 1)

        @block.scalar
        def _(act):
            for ch in range(SC):
                act.wait_ge(gT_in_psum, ch + 1)
                if ch >= 2:
                    act.wait_ge(y_in_psum, ch - 1)
                nc.scalar.activation(c.UT[ch % 2][:], psT[ch % 2][:], ACT.Copy).then_inc(gT_copied, 1)

        @block.vector
        def _(dve):
            for ch in range(SC):
                dve.wait_ge(y_in_psum, ch + 1)
                nc.vector.tensor_tensor(c.X2[:, ch].rearrange("p j d -> p (j d)"), psY[ch % 2][:],
                                        c.X2[:, ch].rearrange("p j d -> p (j d)"), ALU.add).then_inc(y_done, 1)
            dve.wait_ge(y_done, SC)


def final_sum(nc, c, routed, out):
    with ExitStack() as cx:
        r_sb = [cx.enter_context(nc.sbuf_tensor(f"r_last{ch}", [P, CW, D], fp32)) for ch in range(SC)]
        sem = stage_semaphores(nc, cx, "final_sum_")
        loaded = [sem(f"loaded_last{ch}") for ch in range(SC)]
        summed, stored = sem("summed_last"), sem("stored_last")
        block = cx.enter_context(nc.Block())

        @block.sync
        def _(sp):
            for ch in range(SC):
                sp.dma_start(r_sb[ch][:], token_rows(routed, ch)).then_inc(loaded[ch], 16)
            for ch in range(SC):
                sp.wait_ge(summed, ch + 1)
                sp.dma_start(token_rows(out, ch), r_sb[ch][:]).then_inc(stored, 16)
            sp.wait_ge(stored, 16 * SC)

        @block.vector
        def _(dve):
            for ch in range(SC):
                dve.wait_ge(loaded[ch], 16)
                nc.vector.tensor_tensor(r_sb[ch][:], c.X[:, ch * CW:(ch + 1) * CW, :], r_sb[ch][:], ALU.add)                  .then_inc(summed, 1)


def hybrid_layer(nc, x, Wq, bq, Wk, bk, Wv, bv, Wo, bo, W_up, W_v, W_proj, identity, W_scan_raw, Wg, w1, w2, out):
    q_parts = nc.dram_tensor("q_parts", [3, P, N], bf16).ap()
    k_parts = nc.dram_tensor("k_parts", [3, P, N], bf16).ap()
    max_dram = nc.dram_tensor("max_rows_dram", [2, NT // B, P], bf16).ap()
    dispatched = [nc.dram_tensor(f"dispatched{k}", [2 * N, ROW], fp32).ap() for k in range(2)]
    routed = [nc.dram_tensor(f"routed{k}", [2 * N, D], fp32).ap() for k in range(2)]
    scanned = [nc.dram_tensor(f"scanned{k}", [B * (PAD + T), D], fp32).ap() for k in range(2)]

    class Shared:
        pass

    c = Shared()
    with ExitStack() as cx:
        constants(nc, cx, c)
        with ExitStack() as cx_attention:
            attention_tensors(nc, cx_attention, c)
            project(nc, c, x, Wq, bq, Wk, bk, Wv, bv, Wo, bo, W_scan_raw, q_parts, k_parts)
            attend(nc, c, q_parts, k_parts, max_dram)
            project_out(nc, c)
        moe(nc, c, "m0", Wg, w1, w2, dispatched[0], routed[0])
        with ExitStack() as cx_scan:
            scan_tensors(nc, cx_scan, c)
            scan_inputs(nc, c, routed[0][0:N, :], W_up, W_v, W_proj, identity, scanned)
            scan(nc, c, scanned)
            scan_outputs(nc, c)
        moe(nc, c, "m1", Wg, w1, w2, dispatched[1], routed[1])
        final_sum(nc, c, routed[1][0:N, :], out)


_INS = ["L0_attn_a_x", "L0_attn_a_Wq", "L0_attn_a_bq", "L0_attn_a_Wk", "L0_attn_a_bk", "L0_attn_a_Wv", "L0_attn_a_bv",
        "L0_attn_a_Wo", "L0_attn_a_bo", "L0_attn_b_W_up", "L0_attn_b_W_v", "L0_attn_b_W_proj", "L0_attn_b_identity",
        "L0_attn_b_W_scan_raw", "L0_ffn_Wg", "L0_ffn_w1", "L0_ffn_w2"]


def kernel(**inputs):
    import numpy as _np
    import concourse.bacc as _bacc
    from concourse import mybir as _mybir
    from concourse.bass_utils import run_bass_kernel_spmd as _run

    nc = _bacc.Bacc("TRN2", target_bir_lowering=False, num_devices=1)
    arrays, args = {}, []
    for name in _INS:
        a = _np.ascontiguousarray(inputs[name])
        if name == "L0_attn_a_x":
            a = a.reshape(N, D)
        arrays[f"in_{name}_dram"] = a
        args.append(nc.dram_tensor(f"in_{name}_dram", a.shape, _mybir.dt.from_np(a.dtype), kind="ExternalInput").ap())
    out = nc.dram_tensor("out_0_dram", (N, D), fp32, kind="ExternalOutput").ap()
    hybrid_layer(nc, *args, out)
    r = _run(nc, [arrays], core_ids=[0])
    return r.results[0]["out_0_dram"].reshape(B, T, D)
```

```python
import concourse.bass as bass
from concourse import mybir
from contextlib import ExitStack

fp32 = mybir.dt.float32
bf16 = mybir.dt.bfloat16
i32 = mybir.dt.int32
ALU = mybir.AluOpType
ACT = mybir.ActivationFunctionType
AX = mybir.AxisListType

P = 128
B, T, D = 2, 2048, 128
N = B * T
H = 16
HD = D // H
NT = N // P
EPS = 1e-5
MASKED = -1e30
LEAST = -3e38
NEWTON = (15 / 8, -10 / 8, 3 / 8)


class Steps:

    def __init__(self, engine, semaphore, base=0):
        self.engine, self.semaphore, self.base, self.n = engine, semaphore, base, 0

    def then(self, instruction):
        self.n += 1
        instruction.then_inc(self.semaphore, 1)
        self.engine.wait_ge(self.semaphore, self.base + self.n)


def stage_semaphores(nc, cx, prefix):
    taken = []
    cx.callback(nc.all_engine_barrier)
    cx.callback(nc.clear_and_free_semaphores, taken)

    def take(name):
        taken.append(nc.alloc_semaphore(name=prefix + name))
        return taken[-1]

    return take


def finish_stats(nc, steps, st, tmp, mean, var):
    mean_a, m2_a, mean_b, m2_b = st[:, :, 1], st[:, :, 2], st[:, :, 4], st[:, :, 5]
    s, d, m2, dd = (tmp[:, k, :] for k in range(4))
    nc.vector.tensor_tensor(s, mean_a, mean_b, ALU.add)
    nc.vector.tensor_tensor(m2, m2_a, m2_b, ALU.add)
    steps.then(nc.vector.tensor_tensor(d, mean_a, mean_b, ALU.subtract))
    steps.then(nc.vector.tensor_tensor(dd, d, d, ALU.mult))
    nc.vector.tensor_scalar(mean, s, 0.5, None, ALU.mult)
    steps.then(nc.vector.tensor_scalar(m2, m2, 1.0 / D, EPS, ALU.mult, ALU.add))
    steps.then(nc.vector.scalar_tensor_tensor(out=var, in0=dd, scalar=0.25, in1=m2, op0=ALU.mult, op1=ALU.add))


def project(nc, c, x, Wq, bq, Wk, bk, Wv, bv, Wo, bo, Wscan, q_parts, k_parts):
    CH = 512
    NCH = N // CH
    TC = CH // P
    NB = NT // B
    with ExitStack() as cx:
        def sb(name, shape, dt=fp32):
            return cx.enter_context(nc.sbuf_tensor(name, shape, dt))

        def ps(name, shape=(P, CH)):
            return cx.enter_context(nc.psum_tensor(name, list(shape), fp32))

        sem = stage_semaphores(nc, cx, "project_")

        W_nat = sb("W_nat", [P, 4, D])
        W_T = sb("W_T", [P, 3, D])
        bias_cols = sb("bias_cols", [P, 2])
        bv_rows = sb("bv_rows", [P, D])
        st = sb("st", [P, NT, 6])
        tmp = sb("tmp", [P, 4, NT])
        mean, var, std, rstd = (sb(n, [P, NT]) for n in ("mean", "var", "std", "rstd"))
        centred = [sb(f"centred{u}", [P, TC, D]) for u in range(2)]
        xn = [sb(f"xn{u}", [P, TC, D]) for u in range(2)]
        xnT = [sb(f"xnT{u}", [P, CH]) for u in range(2)]
        full = [sb(f"full{u}", [P, 2, CH]) for u in range(2)]
        rest = [sb(f"rest{u}", [P, 2, CH]) for u in range(2)]
        parts = [sb(f"parts{k}", [P, 2, 3, CH], bf16) for k in range(4)]
        squares = sb("squares", [P, D])
        norm = sb("norm", [P, 3])
        ones = sb("ones_f", [P, P])
        psT = [ps(f"psT{u}") for u in range(2)]
        psQK = [[ps(f"psQK{u}{a}") for a in range(2)] for u in range(2)]
        psV = [ps(f"psV{u}") for u in range(2)]

        x_loaded = [sem(f"x_loaded{b}") for b in range(B)]
        w_loaded, b_loaded, made = sem("w_loaded"), sem("b_loaded"), sem("made")
        wT_in_psum, wT_copied = sem("wT_in_psum"), sem("wT_copied")
        stats, stat_steps, std_done, rstd_done = sem("stats"), sem("stat_steps"), sem("std_done"), sem("rstd_done")
        centred_done, xn_ready = sem("centred_done"), sem("xn_ready")
        xT_in_psum, xT_copied, v_in_psum, v_done, full_done = (
            sem(n) for n in ("xT_in_psum", "xT_copied", "v_in_psum", "v_done", "full_done"))
        stored = [sem(f"stored{k}") for k in range(4)]
        qk_in_psum, rest_done, mid_done, lo_dve, lo_pool = (
            sem(n) for n in ("qk_in_psum", "rest_done", "mid_done", "lo_dve", "lo_pool"))
        norm_act, norm_pe, norm_dve = sem("norm_act"), sem("norm_pe"), sem("norm_dve")
        block = cx.enter_context(nc.Block())

        x_t = x.rearrange("(i p) d -> p i d", p=P)

        @block.sync
        def _(sp):
            for ch in range(NCH):
                sp.dma_start(c.X[:, ch * TC:(ch + 1) * TC, :], x_t[:, ch * TC:(ch + 1) * TC, :])\
                  .then_inc(x_loaded[ch // (NCH // B)], 16)
            for m, w in enumerate((Wq, Wk, Wv, Wo)):
                sp.dma_start(W_nat[:, m, :], w).then_inc(w_loaded, 16)
            sp.dma_start(c.S_nat[:], Wscan).then_inc(w_loaded, 16)
            for a, bias in enumerate((bq, bk)):
                sp.dma_start(bias_cols[:, a:a + 1], bias.rearrange("(p a) -> p a", a=1)).then_inc(b_loaded, 16)
            sp.dma_start(bv_rows[:], bv.rearrange("(a d) -> a d", a=1).broadcast_to([P, D])).then_inc(b_loaded, 16)
            sp.dma_start(c.bo_rows[:], bo.rearrange("(a d) -> a d", a=1).broadcast_to([P, D])).then_inc(b_loaded, 16)
            for ch in range(NCH):
                k = ch % 4
                sp.wait_ge(lo_dve, ch + 1)
                sp.wait_ge(lo_pool, ch + 3)
                for a, dst in enumerate((q_parts, k_parts)):
                    sp.dma_start(dst.rearrange("a p t -> p a t")[:, :, ch * CH:(ch + 1) * CH], parts[k][:, a, :, :])\
                      .then_inc(stored[k], 16)
            for k in range(4):
                sp.wait_ge(stored[k], 32 + 32 * (NCH // 4))

        @block.gpsimd
        def _(pool):
            for t, value in ((c.ident, 0.0), (c.ident_b, 0.0), (c.mask_b, 0.0), (c.mask, 0.0), (c.select, 0.0),
                             (ones, 1.0)):
                nc.gpsimd.memset(t[:], value).then_inc(made, 1)
            pool.wait_ge(made, 6)
            for m in (c.ident, c.ident_b):
                nc.gpsimd.affine_select(out=m[:], in_=m[:], compare_op=ALU.not_equal, fill=1.0, base=0,
                                        pattern=[[-1, P]], channel_multiplier=1).then_inc(made, 1)
            nc.gpsimd.affine_select(out=c.mask_b[:], in_=c.mask_b[:], compare_op=ALU.is_ge, fill=MASKED, base=0,
                                    pattern=[[-1, P]], channel_multiplier=1).then_inc(made, 1)
            nc.gpsimd.affine_select(out=c.mask[:, 3 * P:], in_=c.mask[:, 3 * P:], compare_op=ALU.is_ge,
                                    fill=MASKED, base=0, pattern=[[-1, P]], channel_multiplier=1).then_inc(made, 1)
            for g in range(4):
                pool.wait_ge(made, 10 + g)
                nc.gpsimd.affine_select(out=c.select[:], in_=c.select[:], compare_op=ALU.not_equal, fill=1.0,
                                        base=-32 * g, pattern=[[-1, HD + 1]], channel_multiplier=1).then_inc(made, 1)

            def normalise(ch, u):
                pool.wait_ge(rstd_done, ch // (NCH // B) + 1)
                sl = (slice(None), bass.ds(ch * TC, TC))
                pool.wait_ge(xT_in_psum, ch + 1)
                nc.gpsimd.tensor_tensor(centred[u][:], c.X[sl], mean[sl].unsqueeze(2).broadcast_to([P, TC, D]),
                                        ALU.subtract).then_inc(centred_done, 1)
                pool.wait_ge(centred_done, ch + 1)
                nc.gpsimd.tensor_tensor(xn[u][:], centred[u][:], rstd[sl].unsqueeze(2).broadcast_to([P, TC, D]),
                                        ALU.mult).then_inc(xn_ready, 1)

            def last_part(ch, k):
                pool.wait_ge(mid_done, ch * 2 + 2)
                nc.gpsimd.tensor_tensor(parts[k][:, 1, 2, :], rest[k % 2][:, 1, :], parts[k][:, 1, 1, :], ALU.subtract)\
                  .then_inc(lo_pool, 1)

            normalise(0, 0)
            normalise(1, 1)
            for ch in range(NCH):
                if ch + 2 < NCH:
                    normalise(ch + 2, ch % 2)
                last_part(ch, ch % 4)

        @block.vector
        def _(dve):
            dve.sem_inc(v_done, 2)
            steps = Steps(dve, stat_steps)
            for b in range(B):
                half = slice(b * NB, (b + 1) * NB)
                dve.wait_ge(x_loaded[b], 16 * NCH // B)
                with dve.Fori(b * NB // 8, (b + 1) * NB // 8) as k:
                    for i in range(8):
                        nc.vector.bn_stats(st[:, bass.ds(k * 8 + i, 1), :], c.X[:, bass.ds(k * 8 + i, 1), :])\
                          .then_inc(stats, 1)
                dve.wait_ge(stats, (b + 1) * NB)
                finish_stats(nc, steps, st[:, half, :], tmp[:, :, half], mean[:, half], var[:, half])
                dve.wait_ge(std_done, b + 1)
                nc.vector.reciprocal(rstd[:, half], std[:, half]).then_inc(rstd_done, 1)
                if b == 0:
                    dve.wait_ge(wT_in_psum, 1)
                    nc.vector.tensor_copy(W_T[:].rearrange("p m d -> p (m d)"), psT[0][:, 0:3 * D]).then_inc(wT_copied, 1)
                    nc.vector.tensor_copy(c.Wo_T[:], psT[0][:, 3 * D:]).then_inc(wT_copied, 1)
            dve.wait_ge(b_loaded, 64)
            with dve.Fori(0, NCH // 4) as it:
                for k in range(4):
                    ch, u = it * 4 + k, k % 2
                    dve.wait_ge(lo_pool, ch + 1)
                    for a in range(2):
                        dve.wait_ge(full_done, ch * 2 + a + 5)
                        nc.vector.tensor_tensor(rest[u][:, a, :], full[u][:, a, :], parts[k][:, a, 0, :], ALU.subtract)\
                          .then_inc(rest_done, 1)
                        dve.wait_ge(rest_done, ch * 2 + a + 5)
                        nc.vector.tensor_copy(parts[k][:, a, 1, :], rest[u][:, a, :]).then_inc(mid_done, 1)
                        if a == 0:
                            dve.wait_ge(mid_done, ch * 2 + 1)
                            nc.vector.tensor_tensor(parts[k][:, a, 2, :], rest[u][:, a, :], parts[k][:, a, 1, :],
                                                    ALU.subtract).then_inc(lo_dve, 1)
                    dve.wait_ge(v_in_psum, ch + 3)
                    nc.vector.tensor_tensor(c.V[:, :, bass.ds(ch, 1), :, :].rearrange("p h c i d -> p (c i) h d"),
                                            psV[u][:].rearrange("p (i h d) -> p i h d", i=TC, h=H),
                                            bv_rows[:].rearrange("p (h d) -> p h d", h=H).unsqueeze(1)
                                            .broadcast_to([P, TC, H, HD]), ALU.add).then_inc(v_done, 1)
            dve.wait_ge(norm_act, 2)
            nc.vector.reciprocal(norm[:, 2:3], norm[:, 1:2]).then_inc(norm_dve, 1)
            dve.wait_ge(norm_dve, 1)
            nc.vector.tensor_scalar(c.S[:, 0, :], c.S_nat[:], norm[:, 2:3], None, ALU.mult).then_inc(norm_dve, 1)
            dve.wait_ge(norm_pe, 2)
            nc.vector.tensor_copy(c.S[:, 1, :], psT[0][:, 0:D]).then_inc(norm_dve, 1)
            dve.wait_ge(norm_dve, 3)

        @block.scalar
        def _(act):
            act.sem_inc(xT_copied, 2)
            act.sem_inc(full_done, 4)
            act.sem_inc(rest_done, 4)
            act.wait_ge(w_loaded, 80)
            nc.scalar.activation(squares[:], c.S_nat[:], ACT.Square, accum_out=norm[:, 0:1]).then_inc(norm_act, 1)
            act.wait_ge(norm_pe, 1)
            nc.scalar.activation(norm[:, 1:2], psQK[0][0][:, 0:1], ACT.Sqrt).then_inc(norm_act, 1)
            for b in range(B):
                half = slice(b * NB, (b + 1) * NB)
                act.wait_ge(stat_steps, 4 * (b + 1))
                nc.scalar.activation(std[:, half], var[:, half], ACT.Sqrt).then_inc(std_done, 1)
            act.wait_ge(b_loaded, 64)
            with act.Fori(0, NCH // 4) as it:
                for k in range(4):
                    ch, u = it * 4 + k, k % 2
                    act.wait_ge(xT_in_psum, ch + 3)
                    act.wait_ge(v_in_psum, ch + 1)
                    nc.scalar.activation(xnT[u][:], psT[u][:], ACT.Copy).then_inc(xT_copied, 1)
                    act.wait_ge(stored[k], it * 32 + 32)
                    act.wait_ge(rest_done, ch * 2 + 2)
                    for a in range(2):
                        act.wait_ge(qk_in_psum, ch * 2 + a + 1)
                        nc.scalar.activation(parts[k][:, a, 0, :], psQK[u][a][:], ACT.Identity,
                                             bias=bias_cols[:, a:a + 1])
                        nc.scalar.activation(full[u][:, a, :], psQK[u][a][:], ACT.Identity,
                                             bias=bias_cols[:, a:a + 1]).then_inc(full_done, 1)

        @block.tensor
        def _(pe):
            pe.sem_inc(xT_in_psum, 2)
            pe.sem_inc(v_in_psum, 2)
            pe.sem_inc(lo_pool, 2)
            for k in range(4):
                pe.sem_inc(stored[k], 32)
            pe.wait_ge(made, 8)
            pe.wait_ge(w_loaded, 80)
            for m in range(4):
                last = nc.tensor.transpose(psT[0][:, m * D:(m + 1) * D], W_nat[:, m, :], c.ident[:])
            last.then_inc(wT_in_psum, 1)
            pe.wait_ge(norm_act, 1)
            nc.tensor.matmul(psQK[0][0][:, 0:1], ones[:], norm[:, 0:1], start=True, stop=True).then_inc(norm_pe, 1)
            pe.wait_ge(norm_act, 2)
            pe.wait_ge(wT_copied, 2)
            with pe.Fori(0, NCH // 4) as it:
                for k in range(4):
                    ch, u = it * 4 + k, k % 2
                    pe.wait_ge(xn_ready, ch + 1)
                    pe.wait_ge(xT_copied, ch + 1)
                    for i in range(TC):
                        last = nc.tensor.transpose(psT[u][:, i * P:(i + 1) * P], xn[u][:, i, :], c.ident[:])
                    last.then_inc(xT_in_psum, 1)
                    pe.wait_ge(xT_copied, ch + 3)
                    pe.wait_ge(full_done, ch * 2 + 2)
                    for a in range(2):
                        nc.tensor.matmul(psQK[u][a][:], W_T[:, a, :], xnT[u][:], start=True, stop=True)\
                          .then_inc(qk_in_psum, 1)
                    pe.wait_ge(v_done, ch + 1)
                    for i in range(TC):
                        last = nc.tensor.matmul(psV[u][:, i * D:(i + 1) * D], xnT[u][:, i * P:(i + 1) * P],
                                                W_T[:, 2, :], start=True, stop=True)
                    last.then_inc(v_in_psum, 1)
            pe.wait_ge(norm_dve, 2)
            pe.wait_ge(xT_copied, NCH + 2)
            nc.tensor.transpose(psT[0][:, 0:D], c.S[:, 0, :], c.ident[:]).then_inc(norm_pe, 1)


def constants(nc, cx, c):
    def sb(name, shape, dt=fp32):
        return cx.enter_context(nc.sbuf_tensor(name, shape, dt))
    c.ident = sb("ident", [P, P])
    c.ident_b = sb("ident_b", [P, P], bf16)
    c.X = sb("X", [P, NT, D])
    c.S = sb("S_pair", [P, 2, D])


def attention_tensors(nc, cx, c):
    def sb(name, shape, dt=fp32):
        return cx.enter_context(nc.sbuf_tensor(name, shape, dt))
    c.mask_b = sb("mask_b", [P, P], bf16)
    c.mask = sb("mask", [P, 4 * P])
    c.select = sb("select", [P, HD + 1])
    c.V = sb("V", [P, H, 8, 4, HD])
    c.Wo_T = sb("Wo_T", [P, D])
    c.bo_rows = sb("bo_rows", [P, D])
    c.A_out = sb("A_out", [P, NT // B, B * H, HD])
    c.S_nat = sb("S_nat", [P, D])


def attend(nc, c, q_parts, k_parts, max_dram):
    NH = B * H
    NQ = T // P
    G = 4
    QW = T // G
    SCALE = HD ** -0.5
    R = 3
    ROWS = P
    MROW = P - 2
    STEPS = [(g, kt) for g in range(G) for kt in range(4 * g + 4)]
    NS = len(STEPS)
    NBATCH = NS // 4
    MIDDLE = 2
    GROUP_END = {g: sum(4 * f + 4 for f in range(g + 1)) // 4 - 1 for g in range(G)}
    MAXES = [(i, ck) for a in range(4) for i, ck in ((a + 4, 0), (a, 0))]
    MAXES += [(i, 1) for i in range(7, 3, -1)]
    MAXES += [(i, ck) for i in range(NQ - 1, 7, -1) for ck in range(i // 4 + 1)]
    FILLED, MADE = 2 * R + 2, 3 * R + 3
    FIRST_MAXES = 12
    assert len(set(MAXES)) == NS and all(i < NQ // 2 for i, ck in MAXES[:FIRST_MAXES])

    with ExitStack() as cx:
        def sb(name, shape, dt=fp32):
            return cx.enter_context(nc.sbuf_tensor(name, shape, dt))

        def ps(name, shape=(P, 512), dt=fp32):
            return cx.enter_context(nc.psum_tensor(name, list(shape), dt))

        sem = stage_semaphores(nc, cx, "attend_")

        Q = [sb(f"Qs{r}", [ROWS, T], bf16) for r in range(R)]
        K = [sb(f"Ks{r}", [ROWS, T], bf16) for r in range(R)]
        Vp = [sb(f"Vp{r}", [P, NQ, 32]) for r in range(R)]
        probs = sb("probs", [P, 12, QW])
        probs0 = sb("probs0", [P, 4, QW])
        chunk_max = [sb(f"chunk_max{r}", [P, NQ, 4]) for r in range(R)]
        neg_max = [sb(f"neg_max{r}", [P, 2, NQ // 2]) for r in range(R)]
        neg_max_b = [sb(f"neg_max_b{r}", [P, 2, 2, NQ // 2], bf16) for r in range(R)]
        max_rows = [sb(f"max_rows{f}", [NQ, P], bf16) for f in range(2)]
        O_sb = [sb(f"O_sb{u}", [P, QW]) for u in range(2)]
        inv = sb("inv", [P, NQ])
        ones_row = sb("ones_row", [2, T], bf16)
        A = sb("A_newton", [P, D])
        A_b = sb("A_b", [P, D])
        Z = sb("Z_newton", [P, D])
        Y = sb("Y_newton", [P, D])
        a_ident = sb("a_ident", [P, D])
        b_tile = sb("b_tile", [P, D])
        ps_max = [ps(f"ps_max{u}") for u in range(R)]
        ps_s = [ps(f"ps_s{u}") for u in range(R)]
        ps_o = ps("ps_o")
        ps_misc = ps("ps_misc")
        comb3 = ps_misc[:, 0:16 * NQ].rearrange("p (i w) -> p i w", w=16)
        newton_ps = ps_misc[:, 256:512]
        rows_ps = ps_misc[0:NQ, 256:256 + P // 2].bitcast(bf16)

        stacks_loaded = [sem(f"stacks_loaded{r}") for r in range(R)]
        max_rows_loaded = [[sem(f"max_rows_loaded{r}{f}") for f in range(2)] for r in range(R)]
        max_rows_stored = [sem(f"max_rows_stored{f}") for f in range(2)]
        ones_loaded, made, zeroed, v_staged = sem("ones_loaded"), sem("made"), sem("zeroed"), sem("v_staged")
        max_scored, max_reduced = sem("max_scored"), sem("max_reduced")
        neg_max_steps = sem("neg_max_steps")
        rows_in_psum = sem("rows_in_psum")
        scored, exp_done, pv_done, o_copied = sem("scored"), sem("exp_done"), sem("pv_done"), sem("o_copied")
        combined, inv_done, diagonals = sem("combined"), sem("inv_done"), sem("diagonals")
        misc_read = sem("misc_read")
        newton_mm, newton_pool = sem("newton_mm"), sem("newton_pool")
        block = cx.enter_context(nc.Block())

        def sections(engine, section):
            section(-1, -1, 2, False, True)
            section(0, 0, 0, True, True)
            with engine.Fori(0, (NH - 2) // R) as it:
                for u in range(R):
                    section(it * R + (u + 1), it + (u + 1) // R, (u + 1) % R, True, True)
            section(NH - 1, (NH - 1) // R, (NH - 1) % R, True, False)

        def following(j, r):
            return (j + 1, 0) if r == R - 1 else (j, r + 1)

        def preceding(j, r):
            return (j - 1, R - 1) if r == 0 else (j, r - 1)

        def wait(engine, semaphore, value):
            if not isinstance(value, int) or value > 0:
                engine.wait_ge(semaphore, value)

        def reads(s, name, nxt=True):
            if not isinstance(s, int) or s > 0:
                order = ["rows1", "A", "comb", "Y", "rows0", "X", "end"]
                if not nxt:
                    order.remove("rows0")
                return s * 6 + order.index(name)
            return ["rows0 of head 0", "rows1", "A", "Y", "rows0", "X", "end"].index(name) if s == 0 else 0

        @block.sync
        def _(sp):
            def load(s, j, r):
                rows, cols = bass.ds(s % H * HD, HD), bass.ds(s // H * T, T)
                for stack, parts, order in ((Q[r], q_parts, (0, 0, 0, 1, 1, 2)), (K[r], k_parts, (0, 1, 2, 0, 1, 0))):
                    for row, a in enumerate(order):
                        sp.dma_start(stack[row * HD:(row + 1) * HD, :], parts[a, rows, cols])\
                          .then_inc(stacks_loaded[r], 16)

            def place_max_rows(s, j, r, f):
                if f:
                    sp.wait_ge(misc_read, reads(s, "rows1") + 1)
                else:
                    sp.wait_ge(misc_read, reads(s - 1, "rows0") + 1)
                sp.dma_start(max_dram[f], max_rows[f][:])\
                  .then_inc(max_rows_stored[f], 16)
                sp.wait_ge(max_rows_stored[f], s * 16 + 16)
                sp.dma_start(Q[r][MROW:, f * T // 2:(f + 1) * T // 2],
                             max_dram[f].rearrange("(a i) q -> a (i q)", a=2)).then_inc(max_rows_loaded[r][f], 16)

            def section(s, j, r):
                place_max_rows(s, j, r, 1)
                if not isinstance(s, int) or s < NH - 2:
                    sp.wait_ge(scored, s * NS)
                    load(s + 2, *following(*following(j, r)))
                if not isinstance(s, int) or s < NH - 1:
                    place_max_rows(s + 1, *following(j, r), 0)

            sp.wait_ge(zeroed, 2)
            load(0, 0, 0)
            sp.wait_ge(zeroed, 4)
            load(1, 0, 1)
            sp.wait_ge(zeroed, 6)
            sp.wait_ge(made, FILLED)
            for r in range(R):
                sp.dma_start(K[r][MROW:, :], ones_row[:]).then_inc(ones_loaded, 16)
            place_max_rows(0, 0, 0, 0)
            place_max_rows(0, 0, 0, 1)
            load(2, 0, 2)
            place_max_rows(1, 0, 1, 0)
            with sp.Fori(0, (NH - 2) // R - 1) as it:
                for u in range(R):
                    section(it * R + (u + 1), it + (u + 1) // R, (u + 1) % R)
            for s in range(NH - 1 - R, NH):
                section(s, s // R, s % R)

        @block.gpsimd
        def _(pool):
            n = 0
            for t, value in [(t, 0.0) for t in Vp] + [(t, LEAST) for t in chunk_max] + [(probs0, 0.0), (ones_row, 1.0)]:
                nc.gpsimd.memset(t[:], value).then_inc(made, 1)
                n += 1
            pool.wait_ge(made, n)
            for t in Vp:
                nc.gpsimd.memset(t[:, :, HD:HD + 1], 1.0).then_inc(made, 1)
            nc.gpsimd.memset(b_tile[:], NEWTON[1])
            nc.gpsimd.tensor_scalar(a_ident[:], c.ident[:], NEWTON[0], None, ALU.mult).then_inc(made, 1)
            pool.wait_ge(made, n + R + 1)
            assert (n, n + R + 1) == (FILLED, MADE)
            nc.gpsimd.tensor_tensor(c.X[:], c.X[:], c.bo_rows[:].unsqueeze(1).broadcast_to([P, NT, D]), ALU.add)

            def section(s, j, r, exp, nxt):
                if nxt:
                    h, b = (s + 1) % H, (s + 1) // H
                    wait(pool, pv_done, (s - 1) * NBATCH + 1)
                    nc.gpsimd.tensor_copy(Vp[(r + 1) % R][:, :, 0:HD], c.V[:, bass.ds(h, 1), bass.ds(b * 4, 4), :, :]
                                          .rearrange("p h c i d -> p (h c i) d")).then_inc(v_staged, 1)
                if exp:
                    pool.wait_ge(misc_read, reads(s, "A") + 1)
                    nc.gpsimd.tensor_tensor(A_b[:], A[:], b_tile[:], ALU.mult).then_inc(newton_pool, 1)
                    pool.wait_ge(newton_pool, s * 2 + 1)
                    nc.gpsimd.tensor_tensor(Z[:], A_b[:], a_ident[:], ALU.add).then_inc(newton_pool, 1)

            sections(pool, section)

        @block.vector
        def _(dve):
            for r in range(R):
                for t in (Q[r], K[r]):
                    nc.vector.memset(t[:].bitcast(fp32), 0.0).then_inc(zeroed, 1)
            dve.wait_ge(made, MADE)

            def negate_maxima(s, r, f):
                half = neg_max_b[r][:, f]
                nc.vector.tensor_reduce(neg_max[r][:, f, :], chunk_max[r][:, f * NQ // 2:(f + 1) * NQ // 2, :],
                                        axis=AX.X, op=ALU.max, negate=True).then_inc(neg_max_steps, 1)
                dve.wait_ge(neg_max_steps, s * 6 + (3 * f + 1))
                nc.vector.tensor_copy(half[:, 0, :], neg_max[r][:, f, :]).then_inc(neg_max_steps, 1)
                dve.wait_ge(neg_max_steps, s * 6 + (3 * f + 2))
                nc.vector.tensor_tensor(half[:, 1, :], neg_max[r][:, f, :], half[:, 0, :], ALU.subtract)\
                  .then_inc(neg_max_steps, 1)

            def normalise(s):
                dve.wait_ge(combined, s * G)
                nc.vector.reciprocal(inv[:], comb3[:, :, HD]).then_inc(inv_done, 1)
                dve.wait_ge(inv_done, s)
                nc.vector.tensor_tensor(c.A_out[:, :, bass.ds(s - 1, 1), :].rearrange("p i s d -> p i (s d)"),
                                        comb3[:, :, 0:HD], inv[:].unsqueeze(2).broadcast_to([P, NQ, HD]), ALU.mult)\
                  .then_inc(misc_read, 1)

            def newton(s):
                dve.wait_ge(newton_mm, s * 3 + 2)
                dve.wait_ge(newton_pool, s * 2 + 2)
                nc.vector.scalar_tensor_tensor(out=Y[:], in0=newton_ps[:, 0:D], scalar=NEWTON[2], in1=Z[:],
                                               op0=ALU.mult, op1=ALU.add).then_inc(misc_read, 1)

            def section(s, j, r, exp, nxt):
                first = isinstance(s, int) and s <= 0
                r1 = (r + 1) % R
                for k, (i, ck) in enumerate(MAXES if nxt else []):
                    dve.wait_ge(max_scored, (s + 1) * NS + (k + 1))
                    scores, out = ps_max[(k + r1) % R], chunk_max[r1][:, i, ck:ck + 1]
                    if ck < i // 4:
                        nc.vector.tensor_reduce(out, scores[:], axis=AX.X, op=ALU.max).then_inc(max_reduced, 1)
                    else:
                        w = (i % 4 + 1) * P
                        dve.sem_inc(diagonals, 1)
                        nc.vector.tensor_tensor_reduce(out=scores[:, 0:w], in0=scores[:, 0:w], in1=c.mask[:, 4 * P - w:],
                                                       scale=1.0, scalar=LEAST, op0=ALU.add, op1=ALU.max,
                                                       accum_out=out).then_inc(max_reduced, 1)
                    if k == FIRST_MAXES - 1:
                        dve.wait_ge(max_reduced, (s + 1) * NS + (k + 1))
                        negate_maxima(s + 1, r1, 0)
                        if exp and not first:
                            normalise(s)
                    if k == 15 and exp:
                        newton(s)
                if nxt:
                    dve.wait_ge(max_reduced, (s + 1) * NS + NS)
                    negate_maxima(s + 1, r1, 1)
                else:
                    normalise(s)
                    newton(s)

            sections(dve, section)
            normalise(NH)
            dve.wait_ge(misc_read, reads(NH - 1, "end", False) + 1)

        @block.scalar
        def _(act):
            act.wait_ge(made, FILLED)

            def copy_rows(s, j, r, f):
                act.wait_ge(rows_in_psum, s * 2 + (f + 1))
                wait(act, max_rows_stored[f], s * 16)
                nc.scalar.activation(max_rows[f][:], rows_ps, ACT.Copy).then_inc(misc_read, 1)

            def copy_group(s, g):
                batches = s * NBATCH + (GROUP_END[g] + 1)
                act.wait_ge(pv_done, batches)
                wait(act, combined, s * G + (g - 1))
                nc.scalar.activation(O_sb[g % 2][:], ps_o[:], ACT.Copy).then_inc(o_copied, 1)

            def section(s, j, r, exp, nxt):
                if not exp:
                    copy_rows(0, 0, 0, 0)
                    return
                first = isinstance(s, int) and s == 0
                for n in range(NBATCH):
                    wait(act, pv_done, s * NBATCH + (1 - NBATCH if n == 0 else n - 3 if n <= 3 else n - 2))
                    for q in range(4):
                        k = 4 * n + q
                        g, kt = STEPS[k]
                        q0 = max(0, kt - 4 * g) * P
                        dst = (probs0[:, q, q0:] if n == 0 else probs[:, n % 3 * 4 + q, q0:])
                        act.wait_ge(scored, s * NS + (k + 1))
                        nc.scalar.activation(dst, ps_s[(k + r) % R][:, q0:], ACT.Exp, scale=SCALE).then_inc(exp_done, 1)
                    if n == 0:
                        copy_rows(s, j, r, 1)
                        if not first:
                            copy_group(s - 1, G - 1)
                    if n == 1:
                        act.wait_ge(newton_mm, s * 3 + 1)
                        nc.scalar.activation(A[:], newton_ps[:, 0:D], ACT.Copy).then_inc(misc_read, 1)
                    for g in range(G - 1):
                        if n == GROUP_END[g] + 1:
                            copy_group(s, g)
                    if n == 4 and nxt:
                        copy_rows(s + 1, *following(j, r), 0)
                    if n == 6:
                        act.wait_ge(newton_mm, s * 3 + 3)
                        nc.scalar.activation(c.S[:].rearrange("p a d -> p (a d)"), newton_ps, ACT.Copy)\
                          .then_inc(misc_read, 1)

            sections(act, section)
            copy_group(NH - 1, G - 1)

        @block.tensor
        def _(pe):
            pe.wait_ge(made, MADE)

            def score(s, j, r, k):
                g, kt = STEPS[k]
                q0 = max(0, kt - 4 * g) * P
                if k == 0:
                    if isinstance(s, int) and s == 0:
                        pe.wait_ge(ones_loaded, 16 * R)
                    pe.wait_ge(max_rows_loaded[r][0], j * 16 + 16)
                if k == 12:
                    pe.wait_ge(max_rows_loaded[r][1], j * 16 + 16)
                wait(pe, exp_done, s * NS + (k - 2))
                diagonal = kt >= 4 * g
                last = nc.tensor.matmul(ps_s[(k + r) % R][:, q0:], K[r][:, kt * P:(kt + 1) * P],
                                        Q[r][:, g * QW + q0:(g + 1) * QW], start=True, stop=not diagonal)
                if diagonal:
                    last = nc.tensor.matmul(ps_s[(k + r) % R][:, q0:q0 + P], c.mask_b[:], c.ident_b[:], start=False,
                                            stop=True)
                last.then_inc(scored, 1)

            def score_for_max(s, j, r, k):
                i, ck = MAXES[k]
                w = QW if ck < i // 4 else (i % 4 + 1) * P
                if k == 0:
                    pe.wait_ge(stacks_loaded[r], j * 192 + 192)
                wait(pe, max_reduced, s * NS + (k - 2))
                nc.tensor.matmul(ps_max[(k + r) % R][:, 0:w], Q[r][0:MROW, i * P:(i + 1) * P],
                                 K[r][0:MROW, ck * QW:ck * QW + w], start=True, stop=True).then_inc(max_scored, 1)

            def products(s, r, n):
                pe.wait_ge(exp_done, s * NS + 4 * (n + 1))
                if n == 0:
                    pe.wait_ge(v_staged, s + 1)
                g = STEPS[4 * n][0]
                if STEPS[4 * n][1] == 0:
                    wait(pe, o_copied, s * G + g)
                for q in range(4):
                    kt = STEPS[4 * n + q][1]
                    q0 = max(0, kt - 4 * g) * P if n else 0
                    src = probs[:, n % 3 * 4 + q, q0:] if n else probs0[:, q, :]
                    last = nc.tensor.matmul(ps_o[32 * q:32 * q + 32, q0:], Vp[r][:, kt, :], src,
                                            start=kt < 4, stop=kt >= 4 * g)
                last.then_inc(pv_done, 1)

            def combine(s, g):
                pe.wait_ge(o_copied, s * G + (g + 1))
                for t in range(4):
                    last = nc.tensor.matmul(comb3[:, 4 * g + t, 0:HD + 1], O_sb[g % 2][:, t * P:(t + 1) * P], c.select[:],
                                            start=True, stop=True)
                last.then_inc(combined, 1)

            def turn_rows(s, r, f):
                pe.wait_ge(neg_max_steps, s * 6 + 3 * (f + 1))
                nc.tensor.transpose(rows_ps, neg_max_b[r][:, f].rearrange("p a i -> p (a i)"), c.ident_b[:])\
                  .then_inc(rows_in_psum, 1)

            def between(s, j, r, n, exp, nxt):
                first = isinstance(s, int) and s == 0
                j1, r1 = following(j, r)

                def misc(name):
                    wait(pe, misc_read, reads(s, name, nxt))

                if not exp:
                    if n == 4:
                        turn_rows(0, 0, 0)
                    return
                if n == 0:
                    misc("rows1")
                    turn_rows(s, r, 1)
                    if not first:
                        products(s - 1, (r - 1) % R, NBATCH - 1)
                else:
                    products(s, r, n - 1)
                if n == 1:
                    misc("A")
                    nc.tensor.matmul(newton_ps[:, 0:D], c.S[:, 0, :], c.S[:, 0, :], start=True, stop=True)\
                      .then_inc(newton_mm, 1)
                if n == 2 and not first:
                    misc("comb")
                    combine(s - 1, G - 1)
                if n == 3:
                    misc("Y")
                    combine(s, 0)
                    nc.tensor.matmul(newton_ps[:, 0:D], A[:], A[:], start=True, stop=True).then_inc(newton_mm, 1)
                if n == 4 and nxt:
                    misc("rows0")
                    turn_rows(s + 1, r1, 0)
                if n == 5:
                    misc("X")
                    combine(s, 1)
                if n == 6:
                    nc.tensor.matmul(newton_ps[:, 0:D], c.S[:, 1, :], Y[:], start=True, stop=True)
                    nc.tensor.matmul(newton_ps[:, D:], Y[:], c.S[:, 1, :], start=True, stop=True).then_inc(newton_mm, 1)
                if n == 8:
                    misc("end")
                    combine(s, 2)

            def section(s, j, r, exp, nxt):
                j1, r1 = following(j, r)
                for n in range(NBATCH):
                    for k in range(4 * n, 4 * n + 4):
                        if exp:
                            score(s, j, r, k)
                        if nxt:
                            score_for_max(s + 1, j1, r1, k)
                        if k == 4 * n + MIDDLE:
                            between(s, j, r, n, exp, nxt)

            sections(pe, section)
            products(NH - 1, (NH - 1) % R, NBATCH - 1)
            combine(NH - 1, G - 1)


def project_out(nc, c):
    TC = 4
    NCH = NT // TC
    with ExitStack() as cx:
        sem = stage_semaphores(nc, cx, "project_out_")

        aT = [cx.enter_context(nc.sbuf_tensor(f"aT{u}", [P, TC * P], fp32)) for u in range(2)]
        psT = [cx.enter_context(nc.psum_tensor(f"ps_aT{u}", [P, TC * P], fp32)) for u in range(2)]
        psY = [cx.enter_context(nc.psum_tensor(f"ps_y{u}", [P, TC * D], fp32)) for u in range(2)]
        aT_in_psum, aT_copied, y_in_psum, y_done = (sem(n) for n in ("aT_in_psum", "aT_copied", "y_in_psum", "y_done"))
        block = cx.enter_context(nc.Block())

        @block.tensor
        def _(pe):
            def turn(ch):
                if ch >= 2:
                    pe.wait_ge(aT_copied, ch - 1)
                for t in range(ch * TC, (ch + 1) * TC):
                    b, i = divmod(t, NT // B)
                    last = nc.tensor.transpose(psT[ch % 2][:, t % TC * P:(t % TC + 1) * P],
                                               c.A_out[:, i, b * H:(b + 1) * H, :].rearrange("p h d -> p (h d)"),
                                               c.ident[:])
                last.then_inc(aT_in_psum, 1)

            turn(0)
            for ch in range(NCH):
                if ch + 1 < NCH:
                    turn(ch + 1)
                pe.wait_ge(aT_copied, ch + 1)
                if ch >= 2:
                    pe.wait_ge(y_done, ch - 1)
                for i in range(TC):
                    last = nc.tensor.matmul(psY[ch % 2][:, i * D:(i + 1) * D], aT[ch % 2][:, i * P:(i + 1) * P], c.Wo_T[:],
                                            start=True, stop=True)
                last.then_inc(y_in_psum, 1)

        @block.scalar
        def _(act):
            for ch in range(NCH):
                act.wait_ge(aT_in_psum, ch + 1)
                if ch >= 2:
                    act.wait_ge(y_in_psum, ch - 1)
                nc.scalar.activation(aT[ch % 2][:], psT[ch % 2][:], ACT.Copy).then_inc(aT_copied, 1)

        @block.vector
        def _(dve):
            for ch in range(NCH):
                dve.wait_ge(y_in_psum, ch + 1)
                x = c.X[:, ch * TC:(ch + 1) * TC, :].rearrange("p i d -> p (i d)")
                nc.vector.tensor_tensor(x, psY[ch % 2][:], x, ALU.add).then_inc(y_done, 1)
            dve.wait_ge(y_done, NCH)


E_ = 16
F = 512
CAP = (N + E_ - 1) // E_
ROW = D + 2


def moe(nc, c, name, Wg, w1, w2, dispatched, routed):
    J = NT
    TC = 4
    NCH = J // TC
    S2 = CAP // P
    FT = F // P
    JH = J // 2
    HALF_STEPS = 15
    with ExitStack() as cx:
        def sb(n, shape, dt=fp32):
            return cx.enter_context(nc.sbuf_tensor(f"{name}_{n}", shape, dt))

        def ps(n, shape):
            return cx.enter_context(nc.psum_tensor(f"{name}_{n}", shape, fp32))

        sem = stage_semaphores(nc, cx, f"{name}_")

        X = c.X
        Wg_sb = sb("Wg", [P, E_])
        st = sb("st", [P, J, 6])
        tmp = sb("tmp", [P, 4, J])
        mean, var, std, rstd = (sb(n, [P, J]) for n in ("mean", "var", "std", "rstd"))
        xs = [sb(f"xs{k}", [P, TC, D]) for k in range(4)]
        xsT = [sb(f"xsT{u}", [P, TC * P]) for u in range(2)]
        rows = sb("rows", [P, J, ROW])
        best = sb("best", [P, J])
        work = sb("work", [P, J, E_])
        expd = sb("expd", [P, J, E_])
        weight = sb("weight", [P, J, E_])
        rank = sb("rank", [P, J])
        onehot = sb("onehot", [P, J + 1, E_])
        restart = [sb(f"restart{h}", [P, E_, (h + 1) * JH]) for h in range(2)]
        totals = [sb(f"totals{h}", [P, E_, (h + 1) * JH]) for h in range(2)]
        earlier = [sb(f"earlier{h}", [P, E_, (h + 1) * JH]) for h in range(2)]
        place = sb("place", [P, J, E_])
        token = sb("token", [P, J])
        small = sb("small", [P, 8, J])
        slot_i = sb("slot_i", [P, J], i32)
        up_to = sb("up_to", [P, P])
        ones = sb("ones", [P, P])
        blank = sb("blank", [P, J, ROW])
        w1_sb = sb("w1", [P, E_, F])
        w2_sb = sb("w2", [P, E_, FT, D])
        d_sb = blank
        dT = [sb(f"dT{u}", [P, CAP]) for u in range(2)]
        hT = [sb(f"hT{u}", [P, FT, CAP]) for u in range(2)]
        y = [sb(f"y{u}", [P, S2, D]) for u in range(2)]
        to_row = [sb(f"to_row{u}", [P, S2], i32) for u in range(2)]
        psD = [ps(f"psD{u}", [P, 512]) for u in range(2)]
        psH = [ps(f"psH{u}", [P, 1024]) for u in range(2)]
        psY = [ps(f"psY{u}", [P, 512]) for u in range(2)]
        logits = [t[:, 0:JH * E_].rearrange("p (j e) -> p j e", e=E_) for t in psY]
        counts = psD[1][:].rearrange("p (j e) -> p j e", e=E_)

        wg_loaded, made, blanked, blank_made = (sem(n) for n in ("wg_loaded", "made", "blanked", "blank_made"))
        stats, steps_done, std_done = sem("stats"), sem("steps"), sem("std_done")
        xs_in_psum, xsT_copied, logits_in_psum = (sem(n) for n in ("xs_in_psum", "xsT_copied", "logits_in_psum"))
        xs_ready, rows_copied, exp_done, counts_in_psum, counted = (
            sem(n) for n in ("xs_ready", "rows_copied", "exp_done", "counts_in_psum", "counted"))
        slots_ready, scattered = sem("slots_ready"), sem("scattered")
        w_loaded, d_loaded = sem("w_loaded"), sem("d_loaded")
        d_in_psum, d_copied, h_in_psum, h_act, h_dve, y_in_psum, y_done, ids_done = (
            sem(n) for n in ("d_in_psum", "d_copied", "h_in_psum", "h_act", "h_dve", "y_in_psum", "y_done", "ids_done"))
        y_sent = [sem(f"y_sent{u}") for u in range(2)]
        block = cx.enter_context(nc.Block())

        @block.sync
        def _(sp):
            sp.dma_start(Wg_sb[:], Wg).then_inc(wg_loaded, 16)
            for e in range(0, E_, 2):
                sp.dma_start(w1_sb[:, e:e + 2, :], w1[e:e + 2, :, :].rearrange("e m f -> m e f")).then_inc(w_loaded, 16)
                sp.dma_start(w2_sb[:, e:e + 2, :, :].rearrange("p e f m -> p (e f) m"),
                             w2[e:e + 2, :, :].rearrange("e (f p) m -> p (e f) m", p=P)).then_inc(w_loaded, 16)
                if e == 0:
                    sp.wait_ge(blank_made, 2)
                    sp.dma_start(dispatched[0:N, :].rearrange("(p j) w -> p j w", j=J), blank[:]).then_inc(blanked, 16)
                    sp.dma_start(routed[0:N, :].rearrange("(p j) w -> p j w", j=J), blank[:, :, 0:D])\
                      .then_inc(blanked, 16)
            sp.wait_ge(scattered, 16 * J)
            for e in range(0, E_, 2):
                if e:
                    sp.wait_ge(d_loaded, e // 2 * 16)
                sp.dma_start(d_sb[:, e * S2:(e + 2) * S2, :],
                             dispatched[e * CAP:(e + 2) * CAP, :].rearrange("(s p) w -> p s w", p=P)).then_inc(d_loaded, 16)

        @block.gpsimd
        def _(pool):
            nc.gpsimd.memset(blank[:], 0.0).then_inc(blank_made, 1)
            for t in restart:
                nc.gpsimd.memset(t[:], 1.0).then_inc(made, 1)
            nc.gpsimd.memset(up_to[:], 1.0).then_inc(made, 1)
            nc.gpsimd.memset(ones[:], 1.0).then_inc(made, 1)
            nc.gpsimd.memset(onehot[:, 0, :], 0.0).then_inc(made, 1)
            nc.gpsimd.iota(weight[:], pattern=[[0, J], [-1, E_]], base=E_, channel_multiplier=0,
                           allow_small_or_imprecise_dtypes=True).then_inc(made, 1)
            nc.gpsimd.iota(token[:], pattern=[[P, J]], base=0, channel_multiplier=1,
                           allow_small_or_imprecise_dtypes=True).then_inc(made, 1)
            pool.wait_ge(blank_made, 1)
            pool.wait_ge(made, 7)
            nc.gpsimd.iota(blank[:, :, D:D + 1], pattern=[[1, J]], base=N, channel_multiplier=J,
                           allow_small_or_imprecise_dtypes=True).then_inc(blank_made, 1)
            for t in restart:
                nc.gpsimd.memset(t[:, :, 0:1], 0.0).then_inc(made, 1)
            nc.gpsimd.affine_select(out=up_to[:], in_=up_to[:], compare_op=ALU.is_ge, fill=0.0, base=0,
                                    pattern=[[1, P]], channel_multiplier=-1).then_inc(made, 1)
            pool.wait_ge(blanked, 32)
            for half in range(2):
                pool.wait_ge(rows_copied, (half + 1) * NCH // 2)
                pool.wait_ge(slots_ready, 3 * (half + 1))
                for j in range(half * JH, (half + 1) * JH):
                    pool.indirect_dma_start(dispatched, bass.IndirectOffsetOnAxis(ap=slot_i[:, j:j + 1], axis=0),
                                            rows[:, j, :], None).then_inc(scattered, 16)

            for e in range(E_):
                pool.wait_ge(ids_done, e + 1)
                for s in range(S2):
                    pool.wait_ge(y_done, e * S2 + s + 1)
                    pool.indirect_dma_start(routed, bass.IndirectOffsetOnAxis(ap=to_row[e % 2][:, s:s + 1], axis=0),
                                            y[e % 2][:, s, :], None).then_inc(y_sent[e % 2], 16)
            for u in range(2):
                pool.wait_ge(y_sent[u], E_ // 2 * S2 * 16)

        @block.vector
        def _(dve):
            steps = Steps(dve, steps_done)
            for j in range(J):
                nc.vector.bn_stats(st[:, j:j + 1, :], X[:, j:j + 1, :]).then_inc(stats, 1)
            dve.wait_ge(stats, J)
            finish_stats(nc, steps, st, tmp, mean[:], var[:])
            dve.wait_ge(std_done, 1)
            steps.then(nc.vector.reciprocal(rstd[:], std[:]))

            def normalise(half):
                for ch in range(half * NCH // 2, (half + 1) * NCH // 2):
                    if ch >= 4:
                        dve.wait_ge(xs_in_psum, ch - 3)
                        dve.wait_ge(rows_copied, ch - 3)
                    for i in range(TC):
                        j = ch * TC + i
                        nc.vector.tensor_scalar(xs[ch % 4][:, i, :], X[:, j, :], mean[:, j:j + 1], rstd[:, j:j + 1],
                                                ALU.subtract, ALU.mult).then_inc(xs_ready, 1)

            def route(half):
                tiles = slice(half * JH, (half + 1) * JH)
                per_token = [P, JH, E_]
                dve.wait_ge(logits_in_psum, (half + 1) * NCH // 2)
                steps.then(nc.vector.tensor_reduce(best[:, tiles], logits[half], axis=AX.X, op=ALU.max))
                best_b = best[:, tiles].unsqueeze(2).broadcast_to(per_token)
                steps.then(nc.vector.tensor_tensor(work[:, tiles], logits[half], best_b, ALU.is_equal))
                nc.vector.tensor_tensor(expd[:, tiles], logits[half], best_b, ALU.subtract).then_inc(slots_ready, 1)
                steps.then(nc.vector.tensor_tensor(work[:, tiles], work[:, tiles], weight[:, tiles], ALU.mult))
                steps.then(nc.vector.tensor_reduce(rank[:, tiles], work[:, tiles], axis=AX.X, op=ALU.max))
                mine = onehot[:, 1 + half * JH:1 + (half + 1) * JH, :]
                steps.then(nc.vector.tensor_tensor(mine, weight[:, tiles],
                                                   rank[:, tiles].unsqueeze(2).broadcast_to(per_token), ALU.is_equal))
                dve.wait_ge(counted, half + 1)
                steps.then(nc.vector.tensor_tensor_scan(out=earlier[half][:].rearrange("p e j -> p (e j)"),
                                                        data0=restart[half][:].rearrange("p e j -> p (e j)"),
                                                        data1=totals[half][:].rearrange("p e j -> p (e j)"), initial=0.0,
                                                        op0=ALU.mult, op1=ALU.add))
                steps.then(nc.vector.tensor_tensor(place[:, tiles], counts[:, tiles],
                                                   earlier[half][:, :, tiles].rearrange("p e j -> p j e"), ALU.add))
                steps.then(nc.vector.tensor_tensor(place[:, tiles], place[:, tiles], mine, ALU.mult))
                loc1, valid, first_slot, slot, trash, diff, dest, total = (small[:, k, tiles] for k in range(8))
                steps.then(nc.vector.tensor_reduce(loc1, place[:, tiles], axis=AX.X, op=ALU.add))
                nc.vector.tensor_scalar(valid, loc1, float(CAP), None, ALU.is_le)
                nc.vector.tensor_scalar(trash, token[:, tiles], float(N), None, ALU.add)
                steps.then(nc.vector.tensor_scalar(first_slot, rank[:, tiles], -float(CAP), float(E_ * CAP - 1), ALU.mult,
                                                   ALU.add))
                steps.then(nc.vector.tensor_tensor(slot, first_slot, loc1, ALU.add))
                steps.then(nc.vector.tensor_tensor(diff, slot, trash, ALU.subtract))
                steps.then(nc.vector.tensor_tensor(slot, diff, valid, ALU.mult))
                steps.then(nc.vector.tensor_tensor(dest, slot, trash, ALU.add))
                nc.vector.tensor_copy(slot_i[:, tiles], dest).then_inc(slots_ready, 1)
                nc.vector.tensor_copy(rows[:, tiles, D], token[:, tiles])
                dve.wait_ge(exp_done, half + 1)
                steps.then(nc.vector.tensor_reduce(total, work[:, tiles], axis=AX.X, op=ALU.add))
                nc.vector.reciprocal(rows[:, tiles, D + 1], total).then_inc(slots_ready, 1)
                assert steps.n == 5 + (half + 1) * HALF_STEPS

            dve.wait_ge(made, 10)
            normalise(0)
            normalise(1)
            route(0)
            route(1)

            for e in range(E_):
                u = e % 2
                dve.wait_ge(d_loaded, (e // 2 + 1) * 16)
                if e >= 2:
                    dve.wait_ge(y_sent[u], e // 2 * 32)
                nc.vector.tensor_copy(to_row[u][:], d_sb[:, e * S2:(e + 1) * S2, D]).then_inc(ids_done, 1)
                dve.wait_ge(h_in_psum, e * 2 + 2)
                nc.vector.tensor_scalar(hT[u][:, FT // 2:, :].rearrange("p f s -> p (f s)"), psH[u][:, F:], 0.0, None,
                                        ALU.max).then_inc(h_dve, 1)
                dve.wait_ge(y_in_psum, e + 1)
                for s in range(S2):
                    nc.vector.tensor_scalar(y[u][:, s, :], psY[u][:, s * D:(s + 1) * D],
                                            d_sb[:, e * S2 + s, D + 1:D + 2], None, ALU.mult).then_inc(y_done, 1)

        @block.scalar
        def _(act):
            act.wait_ge(steps_done, 4)
            nc.scalar.activation(std[:], var[:], ACT.Sqrt).then_inc(std_done, 1)
            def copy_tokens(ch):
                act.wait_ge(xs_in_psum, ch + 1)
                if ch >= 2:
                    act.wait_ge(logits_in_psum, ch - 1)
                nc.scalar.activation(xsT[ch % 2][:], psH[ch % 2][:, 0:TC * P], ACT.Copy).then_inc(xsT_copied, 1)
                nc.scalar.activation(rows[:, ch * TC:(ch + 1) * TC, 0:D], xs[ch % 4][:], ACT.Copy)\
                  .then_inc(rows_copied, 1)

            def copy_totals(half):
                tiles = slice(half * JH, (half + 1) * JH)
                act.wait_ge(counts_in_psum, 2 * (half + 1))
                nc.scalar.activation(totals[half][:].rearrange("p e j -> p j e"),
                                     psD[0][:, 0:(half + 1) * JH * E_].rearrange("p (j e) -> p j e", e=E_),
                                     ACT.Copy).then_inc(counted, 1)
                act.wait_ge(slots_ready, 3 * half + 1)
                act.wait_ge(steps_done, 5 + half * HALF_STEPS + 4)
                nc.scalar.activation(work[:, tiles], expd[:, tiles], ACT.Exp).then_inc(exp_done, 1)

            for ch in range(NCH):
                copy_tokens(ch)
                if ch == NCH - 2:
                    copy_totals(0)
            copy_totals(1)

            def copy_rows(e):
                act.wait_ge(d_in_psum, e + 1)
                if e >= 2:
                    act.wait_ge(h_in_psum, e * 2 - 2)
                nc.scalar.activation(dT[e % 2][:], psD[e % 2][:, 0:CAP], ACT.Copy).then_inc(d_copied, 1)

            copy_rows(0)
            copy_rows(1)
            for e in range(E_):
                act.wait_ge(h_in_psum, e * 2 + 1)
                if e >= 2:
                    act.wait_ge(y_in_psum, e - 1)
                nc.scalar.activation(hT[e % 2][:, 0:FT // 2, :].rearrange("p f s -> p (f s)"), psH[e % 2][:, 0:F],
                                     ACT.Relu)\
                  .then_inc(h_act, 1)
                if e + 2 < E_:
                    copy_rows(e + 2)

        @block.tensor
        def _(pe):
            pe.wait_ge(wg_loaded, 16)
            def turn_tokens(ch):
                pe.wait_ge(xs_ready, (ch + 1) * TC)
                if ch >= 2:
                    pe.wait_ge(xsT_copied, ch - 1)
                for i in range(TC):
                    last = nc.tensor.transpose(psH[ch % 2][:, i * P:(i + 1) * P], xs[ch % 4][:, i, :], c.ident[:])
                last.then_inc(xs_in_psum, 1)

            def gate(ch):
                pe.wait_ge(xsT_copied, ch + 1)
                half, first = ch // (NCH // 2), ch % (NCH // 2) * TC
                for i in range(TC):
                    last = nc.tensor.matmul(logits[half][:, first + i, :], xsT[ch % 2][:, i * P:(i + 1) * P], Wg_sb[:],
                                            start=True, stop=True)
                last.then_inc(logits_in_psum, 1)

            def count(half):
                mine = slice(half * JH * E_, (half + 1) * JH * E_)
                pe.wait_ge(steps_done, 5 + half * HALF_STEPS + 5)
                nc.tensor.matmul(psD[0][:, 0:mine.stop], ones[:], onehot[:, 0:(half + 1) * JH, :]
                                 .rearrange("p j e -> p (j e)"), start=True, stop=True).then_inc(counts_in_psum, 1)
                nc.tensor.matmul(psD[1][:, mine], up_to[:], onehot[:, 1 + half * JH:1 + (half + 1) * JH, :]
                                 .rearrange("p j e -> p (j e)"), start=True, stop=True).then_inc(counts_in_psum, 1)

            pe.wait_ge(made, 10)
            turn_tokens(0)
            for ch in range(NCH):
                if ch + 1 < NCH:
                    turn_tokens(ch + 1)
                gate(ch)
                if ch == NCH - 3:
                    count(0)
            count(1)
            pe.wait_ge(steps_done, 5 + HALF_STEPS + 7)

            def turn(e):
                pe.wait_ge(d_loaded, (e // 2 + 1) * 16)
                if e >= 2:
                    pe.wait_ge(d_copied, e - 1)
                for s in range(S2):
                    last = nc.tensor.transpose(psD[e % 2][:, s * P:(s + 1) * P], d_sb[:, e * S2 + s, 0:D], c.ident[:])
                last.then_inc(d_in_psum, 1)

            def up(e):
                pe.wait_ge(d_copied, e + 1)
                if e >= 2:
                    pe.wait_ge(h_act, e - 1)
                    pe.wait_ge(h_dve, e - 1)
                for f in range(FT):
                    last = nc.tensor.matmul(psH[e % 2][:, f * CAP:(f + 1) * CAP], w1_sb[:, e, f * P:(f + 1) * P],
                                            dT[e % 2][:], start=True, stop=True)
                    if f % 2:
                        last.then_inc(h_in_psum, 1)

            def down(e):
                pe.wait_ge(h_act, e + 1)
                pe.wait_ge(h_dve, e + 1)
                if e >= 2:
                    pe.wait_ge(y_done, (e - 1) * S2)
                for s in range(S2):
                    for f in range(FT):
                        last = nc.tensor.matmul(psY[e % 2][:, s * D:(s + 1) * D], hT[e % 2][:, f, s * P:(s + 1) * P],
                                                w2_sb[:, e, f, :], start=f == 0, stop=f == FT - 1)
                last.then_inc(y_in_psum, 1)

            pe.wait_ge(w_loaded, 16 * E_)
            turn(0)
            turn(1)
            up(0)
            for e in range(E_):
                if e + 2 < E_:
                    turn(e + 2)
                if e + 1 < E_:
                    up(e + 1)
                down(e)


LANES = 4
W_LANE = D // LANES
SC = 4
CW = N // SC // P
SHIFTS = [1 << k for k in range(T.bit_length() - 1)]
PAD = SHIFTS[-1]
RMS_EPS = 1e-8


def scan_tensors(nc, cx, c):
    def sb(name, shape, dt=fp32):
        return cx.enter_context(nc.sbuf_tensor(name, shape, dt))
    c.X2 = c.X[:].rearrange("p (c j) d -> p c j d", c=SC)
    c.q = sb("q", [P, SC, CW, D])
    c.v2 = sb("v2", [P, SC, CW, D])
    c.Wproj_T = sb("Wproj_T", [P, D])
    c.L = [sb(f"L{ch}", [P, CW, D]) for ch in range(SC)]
    c.U = [sb(f"U{u}", [P, CW, D]) for u in range(2)]
    c.UT = [sb(f"UT{u}", [P, CW * P]) for u in range(2)]


def token_rows(t, ch):
    return t.rearrange("(c j p) d -> p c j d", c=SC, j=CW)[:, bass.ds(ch, 1), :, :].rearrange("p c j d -> p (c j) d")


def padded_rows(t, ch, shift=0):
    first = ch // (SC // B) * (PAD + T) + PAD + ch % (SC // B) * (CW * P) - shift
    return t[first:first + CW * P, :].rearrange("(j p) d -> p j d", j=CW)


def scan_inputs(nc, c, routed, W_up, W_v, W_proj, identity, scanned):
    with ExitStack() as cx:
        def sb(name, shape, dt=fp32):
            return cx.enter_context(nc.sbuf_tensor(name, shape, dt))

        def ps(name):
            return cx.enter_context(nc.psum_tensor(name, [P, CW * P], fp32))

        sem = stage_semaphores(nc, cx, "scan_inputs_")

        W_nat = sb("Wb_nat", [P, 3, D])
        W_T = sb("Wb_T", [P, 2, D])
        st = sb("st_b", [P, NT, 6])
        tmp = sb("tmp_b", [P, 4, NT])
        mean, var, std, rstd = (sb(n, [P, NT]) for n in ("mean_b", "var_b", "std_b", "rstd_b"))
        ident_row = sb("ident_row", [P, D])
        psT = [ps(f"psT_b{u}") for u in range(2)]
        psQ, psV = ps("psQ_b"), ps("psV_b")

        loaded = [sem(f"loaded{ch}") for ch in range(SC)]
        w_loaded, identity_loaded, padded, q_stored = (
            sem(n) for n in ("w_loaded", "identity_loaded", "padded", "q_stored"))
        summed, stats, stat_steps, std_done, rstd_done = (
            sem(n) for n in ("summed", "stats", "stat_steps", "std_done", "rstd_done"))
        wT_in_psum, wT_copied = sem("wT_in_psum"), sem("wT_copied")
        xn_ready, xT_in_psum, xT_copied, q_in_psum, v_in_psum, q_copied, v_copied = (
            sem(n) for n in ("xn_ready", "xT_in_psum", "xT_copied", "q_in_psum", "v_in_psum", "q_copied", "v_copied"))
        block = cx.enter_context(nc.Block())

        @block.sync
        def _(sp):
            for ch in range(SC):
                sp.dma_start(c.L[ch][:], token_rows(routed, ch)).then_inc(loaded[ch], 16)
            for m, w in enumerate((W_up, W_v, W_proj)):
                sp.dma_start(W_nat[:, m, :], w).then_inc(w_loaded, 16)
            sp.dma_start(ident_row[:], identity.rearrange("(a d) -> a d", a=1).broadcast_to([P, D]))\
              .then_inc(identity_loaded, 16)
            sp.wait_ge(identity_loaded, 16)
            for t in scanned:
                for b in range(B):
                    pads = t[b * (PAD + T):b * (PAD + T) + PAD, :].rearrange("(p j) d -> p j d", j=PAD // P)
                    sp.dma_start(pads, ident_row[:].unsqueeze(1).broadcast_to([P, PAD // P, D])).then_inc(padded, 16)
            for ch in range(SC):
                sp.wait_ge(q_copied, ch + 1)
                sp.dma_start(padded_rows(scanned[0], ch), c.q[:, ch]).then_inc(q_stored, 16)
            sp.wait_ge(padded, 16 * B * len(scanned))
            sp.wait_ge(q_stored, 16 * SC)

        @block.gpsimd
        def _(pool):
            for ch in range(SC):
                pool.wait_ge(loaded[ch], 16)
                nc.gpsimd.tensor_tensor(c.X2[:, ch], c.X2[:, ch], c.L[ch][:], ALU.add).then_inc(summed, 1)

        @block.vector
        def _(dve):
            dve.wait_ge(wT_in_psum, 1)
            nc.vector.tensor_copy(W_T[:].rearrange("p m d -> p (m d)"), psT[1][:, 0:2 * D]).then_inc(wT_copied, 1)
            nc.vector.tensor_copy(c.Wproj_T[:], psT[1][:, 2 * D:3 * D]).then_inc(wT_copied, 1)
            tiles = c.X
            for ch in range(SC):
                dve.wait_ge(summed, ch + 1)
                for j in range(CW):
                    i = ch * CW + j
                    nc.vector.bn_stats(st[:, i:i + 1, :], tiles[:, i:i + 1, :]).then_inc(stats, 1)
            dve.wait_ge(stats, NT)
            finish_stats(nc, Steps(dve, stat_steps), st, tmp, mean[:], var[:])
            dve.wait_ge(std_done, 1)
            nc.vector.reciprocal(rstd[:], std[:]).then_inc(rstd_done, 1)
            dve.wait_ge(rstd_done, 1)

            def normalise(ch):
                if ch >= 2:
                    dve.wait_ge(xT_in_psum, ch - 1)
                for j in range(CW):
                    i = ch * CW + j
                    last = nc.vector.tensor_scalar(c.U[ch % 2][:, j, :], c.X2[:, ch, j, :], mean[:, i:i + 1],
                                                   rstd[:, i:i + 1], ALU.subtract, ALU.mult)
                last.then_inc(xn_ready, 1)

            normalise(0)
            normalise(1)
            for ch in range(SC):
                if ch + 2 < SC:
                    normalise(ch + 2)
                dve.wait_ge(v_in_psum, ch + 1)
                nc.vector.tensor_copy(c.v2[:, ch].rearrange("p j d -> p (j d)"), psV[:]).then_inc(v_copied, 1)
            dve.wait_ge(v_copied, SC)

        @block.scalar
        def _(act):
            act.wait_ge(stat_steps, 4)
            nc.scalar.activation(std[:], var[:], ACT.Sqrt).then_inc(std_done, 1)

            def copy_tokens(ch):
                act.wait_ge(xT_in_psum, ch + 1)
                if ch >= 2:
                    act.wait_ge(v_in_psum, ch - 1)
                nc.scalar.activation(c.UT[ch % 2][:], psT[ch % 2][:], ACT.Copy).then_inc(xT_copied, 1)

            copy_tokens(0)
            for ch in range(SC):
                if ch + 1 < SC:
                    copy_tokens(ch + 1)
                act.wait_ge(q_in_psum, ch + 1)
                nc.scalar.activation(c.q[:, ch].rearrange("p j d -> p (j d)"), psQ[:], ACT.Copy).then_inc(q_copied, 1)

        @block.tensor
        def _(pe):
            pe.wait_ge(w_loaded, 48)
            for m in range(3):
                last = nc.tensor.transpose(psT[1][:, m * D:(m + 1) * D], W_nat[:, m, :], c.ident[:])
            last.then_inc(wT_in_psum, 1)
            pe.wait_ge(wT_copied, 2)

            def turn(ch):
                pe.wait_ge(xn_ready, ch + 1)
                if ch >= 2:
                    pe.wait_ge(xT_copied, ch - 1)
                for j in range(CW):
                    last = nc.tensor.transpose(psT[ch % 2][:, j * P:(j + 1) * P], c.U[ch % 2][:, j, :], c.ident[:])
                last.then_inc(xT_in_psum, 1)

            turn(0)
            for ch in range(SC):
                if ch + 1 < SC:
                    turn(ch + 1)
                pe.wait_ge(xT_copied, ch + 1)
                for m, (dst, read, ready) in enumerate(((psQ, q_copied, q_in_psum), (psV, v_copied, v_in_psum))):
                    if ch >= 1:
                        pe.wait_ge(read, ch)
                    for j in range(CW):
                        last = nc.tensor.matmul(dst[:, j * D:(j + 1) * D], c.UT[ch % 2][:, j * P:(j + 1) * P],
                                                W_T[:, m, :], start=True, stop=True)
                    last.then_inc(ready, 1)


def scan(nc, c, scanned):
    LA, LW, CE = LANES, W_LANE, CW * D
    NS = len(SHIFTS)
    G = NS * SC
    ROWS = CW * LA
    HEAD = 6
    with ExitStack() as cx:
        def sb(name, shape, dt=fp32):
            return cx.enter_context(nc.sbuf_tensor(name, shape, dt))

        def ps(name):
            return cx.enter_context(nc.psum_tensor(name, [P, CE], fp32))

        sem = stage_semaphores(nc, cx, "scan_")

        lane_products = [sb(f"lane_products{u}", [P, LA, ROWS, LW]) for u in range(2)]
        weighted = sb("weighted", [P, LA, ROWS, LW])
        v_sb = [sb(f"v_sb{u}", [P, CE]) for u in range(2)]
        z_normed = sb("z_normed", [P, CW, D])
        squares = sb("z_squares", [P, ROWS, LW])
        scores = sb("scores", [P, LA * CW, LA])
        best = sb("best_score", [P, LA * CW])
        shifted = sb("shifted_scores", [P, LA * CW, LA])
        expd = sb("exp_scores", [P, LA * CW, LA])
        total = sb("total", [P, LA * CW])
        share = sb("share", [P, LA * CW])
        att = [sb(f"att{u}", [P, LA, ROWS]) for u in range(2)]
        ss, log_ms, rs, rs_lane = (sb(n, [P, LA * CW]) for n in ("ss", "log_ms", "rs", "rs_lane"))
        lane_inv = sb("lane_inv", [P, LA, CW])
        eps = sb("rms_eps", [P, 1])
        psU, psZ = ps("psU"), ps("psZ")
        psV = [ps(f"psV_s{u}") for u in range(2)]

        l_loaded = [sem(f"l_loaded{ch}") for ch in range(SC)]
        x_stored = [sem(f"x_stored{ch}") for ch in range(SC)]
        made = sem("made_s")
        p1_pool, p2_pool, x_new = (sem(n) for n in ("p1_pool", "p2_pool", "x_new"))
        u_in_psum, uT_copied, v_in_psum, v_copied, z_in_psum = (
            sem(n) for n in ("u_in_psum", "uT_copied", "v_in_psum", "v_copied", "z_in_psum"))
        p1_dve, head_steps, p2_dve, ss_done, rs_steps, z_done = (
            sem(n) for n in ("p1_dve", "head_steps", "p2_dve", "ss_done", "rs_steps", "z_done"))
        exp_done, squared, rs_log, rs_done = sem("exp_done"), sem("squared"), sem("rs_log"), sem("rs_done")
        block = cx.enter_context(nc.Block())

        def chunks(engine, section, lag):
            for ch in range(SC):
                section(ch, 0, ch, True)
            with engine.Fori(1, NS) as s:
                for ch in range(SC):
                    section(s * SC + ch, s, ch, True)
            for k in range(lag):
                section(G + k, NS, k, False)

        def wait(engine, semaphore, value):
            if not isinstance(value, int) or value > 0:
                engine.wait_ge(semaphore, value)

        def reached(g, lag):
            return not isinstance(g, int) or 0 <= g - lag < G

        @block.sync
        def _(sp):
            for ch in range(SC):
                sp.dma_start(c.L[ch][:], padded_rows(scanned[0], ch, SHIFTS[0])).then_inc(l_loaded[ch], 16)
            for s in range(NS - 1):
                for ch in range(SC):
                    sp.wait_ge(x_new, s * SC + ch + 1)
                    sp.dma_start(padded_rows(scanned[(s + 1) % 2], ch), c.q[:, ch]).then_inc(x_stored[ch], 16)
                    sp.wait_ge(x_stored[ch], 16 * (s + 1))
                    sp.dma_start(c.L[ch][:], padded_rows(scanned[(s + 1) % 2], ch, SHIFTS[s + 1]))\
                      .then_inc(l_loaded[ch], 16)

        def lane_product(engine, ch, l, out):
            return engine.tensor_tensor(
                out[:, l].rearrange("p (j m) d -> p j m d", m=LA),
                c.L[ch][:, :, l * LW:(l + 1) * LW].unsqueeze(2).broadcast_to([P, CW, LA, LW]),
                c.q[:, ch].rearrange("p j (m d) -> p j m d", m=LA), ALU.mult)

        @block.gpsimd
        def _(pool):
            for l in range(LA):
                nc.gpsimd.memset(lane_inv[:, l, :], 1.0 / (l + 1)).then_inc(made, 1)
            nc.gpsimd.memset(eps[:], RMS_EPS).then_inc(made, 1)

            def section(g, s, ch, head):
                u = ch % 2
                if head:
                    pool.wait_ge(l_loaded[ch], s * 16 + 16)
                    wait(pool, x_new, g - 3)
                    wait(pool, head_steps, (g - 2) * HEAD + 1)
                    lane_product(nc.gpsimd, ch, 1, lane_products[u])
                    lane_product(nc.gpsimd, ch, 2, lane_products[u])
                    lane_product(nc.gpsimd, ch, 3, lane_products[u]).then_inc(p1_pool, 1)
                if reached(g, 1):
                    pool.wait_ge(head_steps, (g - 1) * HEAD + HEAD)
                    pool.wait_ge(v_copied, g)
                    wait(pool, z_in_psum, (g - 1) * 2)
                    nc.gpsimd.tensor_tensor(weighted[:, 3], att[1 - u][:, 3].unsqueeze(2).broadcast_to([P, ROWS, LW]),
                                            v_sb[1 - u][:].rearrange("p (r d) -> p r d", d=LW), ALU.mult)\
                      .then_inc(p2_pool, 1)
                if reached(g, 2):
                    pool.wait_ge(z_done, g - 1)
                    nc.gpsimd.tensor_tensor(c.q[:, (ch - 2) % SC], c.L[(ch - 2) % SC][:], z_normed[:], ALU.add)\
                      .then_inc(x_new, 1)

            chunks(pool, section, 2)
            pool.wait_ge(x_new, G)

        @block.vector
        def _(dve):
            dve.wait_ge(made, LA + 1)

            def section(g, s, ch, head):
                u, v = ch % 2, 1 - ch % 2
                body, end = reached(g, 1), reached(g, 2)
                steps = Steps(dve, head_steps, (g - 1) * HEAD)

                def weigh(l):
                    nc.vector.tensor_tensor(weighted[:, l], att[v][:, l].unsqueeze(2).broadcast_to([P, ROWS, LW]),
                                            psV[v][:].rearrange("p (r d) -> p r d", d=LW), ALU.mult).then_inc(p2_dve, 1)

                if body:
                    dve.wait_ge(p1_pool, g)
                    dve.wait_ge(p1_dve, g)
                    steps.then(nc.vector.tensor_reduce(scores[:].rearrange("p r m -> p (r m)"),
                                                       lane_products[v][:].rearrange("p l r d -> p (l r) d"),
                                                       axis=AX.X, op=ALU.add))
                    steps.then(nc.vector.tensor_reduce(best[:], scores[:], axis=AX.X, op=ALU.max))
                    nc.vector.tensor_tensor(shifted[:], scores[:], best[:].unsqueeze(2)
                                            .broadcast_to([P, LA * CW, LA]), ALU.subtract).then_inc(head_steps, 1)
                    steps.n += 1
                if head:
                    dve.wait_ge(l_loaded[ch], s * 16 + 16)
                    wait(dve, x_new, g - 3)
                    lane_product(nc.vector, ch, 0, lane_products[u]).then_inc(p1_dve, 1)
                if end:
                    dve.wait_ge(squared, g - 1)
                    nc.vector.tensor_reduce(ss[:], squares[:], axis=AX.X, op=ALU.add).then_inc(ss_done, 1)
                if body:
                    dve.wait_ge(exp_done, g)
                    steps.then(nc.vector.tensor_reduce(total[:], expd[:], axis=AX.X, op=ALU.add))
                    steps.then(nc.vector.reciprocal(share[:], total[:]))
                    nc.vector.tensor_tensor(att[v][:].rearrange("p l (j m) -> p (l j) m", m=LA), expd[:],
                                            share[:].unsqueeze(2).broadcast_to([P, LA * CW, LA]), ALU.mult)\
                      .then_inc(head_steps, 1)
                    assert steps.n + 1 == HEAD
                if end:
                    dve.wait_ge(rs_done, g - 1)
                    nc.vector.tensor_tensor(rs_lane[:], rs[:], lane_inv[:].rearrange("p l j -> p (l j)"), ALU.mult)\
                      .then_inc(rs_steps, 1)
                    dve.wait_ge(rs_steps, g - 1)
                    wait(dve, x_new, g - 2)
                    nc.vector.tensor_tensor(z_normed[:].rearrange("p j (l d) -> p l j d", l=LA),
                                            psZ[:].rearrange("p (l j d) -> p l j d", l=LA, d=LW),
                                            rs_lane[:].rearrange("p (l j) -> p l j", l=LA).unsqueeze(3)
                                            .broadcast_to([P, LA, CW, LW]), ALU.mult).then_inc(z_done, 1)
                if body:
                    dve.wait_ge(head_steps, (g - 1) * HEAD + HEAD)
                    dve.wait_ge(v_in_psum, g)
                    dve.wait_ge(v_copied, g)
                    wait(dve, z_in_psum, (g - 1) * 2)
                    weigh(0)
                    weigh(1)
                    weigh(2)

            chunks(dve, section, 2)

        @block.scalar
        def _(act):
            act.preload_act_table_set("natural_log_exp_and_others")
            act.wait_ge(made, LA + 1)

            def section(g, s, ch, head):
                u = ch % 2
                if reached(g, 2):
                    wait(act, ss_done, g - 2)
                    for half in range(2):
                        act.wait_ge(z_in_psum, (g - 2) * 2 + (half + 1))
                        last = nc.scalar.activation(squares[:, half * ROWS // 2:(half + 1) * ROWS // 2]
                                                    .rearrange("p r d -> p (r d)"),
                                                    psZ[:, half * CE // 2:(half + 1) * CE // 2], ACT.Square)
                    last.then_inc(squared, 1)
                if reached(g, 1):
                    act.wait_ge(head_steps, (g - 1) * HEAD + 3)
                    nc.scalar.activation(expd[:], shifted[:], ACT.Exp, scale=W_LANE ** -0.5).then_inc(exp_done, 1)
                    act.wait_ge(v_in_psum, g)
                    wait(act, p2_pool, g - 2)
                    nc.scalar.activation(v_sb[1 - u][:], psV[1 - u][:], ACT.Copy).then_inc(v_copied, 1)
                if reached(g, 2):
                    act.wait_ge(ss_done, g - 1)
                    nc.scalar.activation(log_ms[:], ss[:], ACT.Ln, bias=eps[:], scale=1.0 / W_LANE).then_inc(rs_log, 1)
                    act.wait_ge(rs_log, g - 1)
                    nc.scalar.activation(rs[:], log_ms[:], ACT.Exp, scale=-0.5).then_inc(rs_done, 1)
                if head:
                    act.wait_ge(u_in_psum, g + 1)
                    wait(act, v_in_psum, g - 1)
                    nc.scalar.activation(c.UT[u][:], psU[:], ACT.Copy).then_inc(uT_copied, 1)

            chunks(act, section, 2)

        @block.tensor
        def _(pe):
            def section(g, s, ch, head):
                u = ch % 2
                if reached(g, 2):
                    wait(pe, z_done, g - 2)
                    for l in (0, 1, 3, 2):
                        if l < 3:
                            pe.wait_ge(p2_dve, (g - 2) * 3 + (l + 1))
                        else:
                            pe.wait_ge(p2_pool, g - 1)
                        for m in range(LA):
                            last = nc.tensor.matmul(psZ[:, l * CW * LW:(l + 1) * CW * LW], c.ident[:],
                                                    weighted[:, l].rearrange("p (j m) d -> p j m d", m=LA)[:, :, m, :],
                                                    start=m == 0, stop=m == LA - 1)
                        if l in (1, 2):
                            last.then_inc(z_in_psum, 1)
                if reached(g, 1):
                    pe.wait_ge(uT_copied, g)
                    wait(pe, p2_dve, (g - 2) * 3)
                    wait(pe, v_copied, g - 2)
                    for j in range(CW):
                        last = nc.tensor.matmul(psV[1 - u][:, j * D:(j + 1) * D], c.UT[1 - u][:, j * P:(j + 1) * P],
                                                c.S[:, 0, :], start=True, stop=True)
                    last.then_inc(v_in_psum, 1)
                if head:
                    pe.wait_ge(l_loaded[ch], s * 16 + 16)
                    wait(pe, x_new, g - 3)
                    wait(pe, uT_copied, g)
                    for j in range(CW):
                        for k, t in enumerate((c.L[ch][:, j, :], c.q[:, ch, j, :])):
                            last = nc.tensor.matmul(psU[:, j * P:(j + 1) * P], t, c.ident[:], start=k == 0, stop=k == 1)
                    last.then_inc(u_in_psum, 1)

            chunks(pe, section, 2)


def scan_outputs(nc, c):
    with ExitStack() as cx:
        def ps(name):
            return cx.enter_context(nc.psum_tensor(name, [P, CW * P], fp32))

        sem = stage_semaphores(nc, cx, "scan_outputs_")

        psT = [ps(f"psT_o{u}") for u in range(2)]
        psY = [ps(f"psY_o{u}") for u in range(2)]
        gated, gT_in_psum, gT_copied, y_in_psum, y_done = (
            sem(n) for n in ("gated", "gT_in_psum", "gT_copied", "y_in_psum", "y_done"))
        block = cx.enter_context(nc.Block())

        @block.gpsimd
        def _(pool):
            for ch in range(SC):
                if ch >= 2:
                    pool.wait_ge(gT_in_psum, ch - 1)
                nc.gpsimd.tensor_tensor(c.U[ch % 2][:], c.q[:, ch], c.v2[:, ch], ALU.mult).then_inc(gated, 1)

        @block.tensor
        def _(pe):
            for ch in range(SC):
                pe.wait_ge(gated, ch + 1)
                if ch >= 2:
                    pe.wait_ge(gT_copied, ch - 1)
                for j in range(CW):
                    last = nc.tensor.transpose(psT[ch % 2][:, j * P:(j + 1) * P], c.U[ch % 2][:, j, :], c.ident[:])
                last.then_inc(gT_in_psum, 1)
                pe.wait_ge(gT_copied, ch + 1)
                if ch >= 2:
                    pe.wait_ge(y_done, ch - 1)
                for j in range(CW):
                    last = nc.tensor.matmul(psY[ch % 2][:, j * D:(j + 1) * D], c.UT[ch % 2][:, j * P:(j + 1) * P],
                                            c.Wproj_T[:], start=True, stop=True)
                last.then_inc(y_in_psum, 1)

        @block.scalar
        def _(act):
            for ch in range(SC):
                act.wait_ge(gT_in_psum, ch + 1)
                if ch >= 2:
                    act.wait_ge(y_in_psum, ch - 1)
                nc.scalar.activation(c.UT[ch % 2][:], psT[ch % 2][:], ACT.Copy).then_inc(gT_copied, 1)

        @block.vector
        def _(dve):
            for ch in range(SC):
                dve.wait_ge(y_in_psum, ch + 1)
                nc.vector.tensor_tensor(c.X2[:, ch].rearrange("p j d -> p (j d)"), psY[ch % 2][:],
                                        c.X2[:, ch].rearrange("p j d -> p (j d)"), ALU.add).then_inc(y_done, 1)
            dve.wait_ge(y_done, SC)


def final_sum(nc, c, routed, out):
    with ExitStack() as cx:
        r_sb = [cx.enter_context(nc.sbuf_tensor(f"r_last{ch}", [P, CW, D], fp32)) for ch in range(SC)]
        sem = stage_semaphores(nc, cx, "final_sum_")
        loaded = [sem(f"loaded_last{ch}") for ch in range(SC)]
        summed, stored = sem("summed_last"), sem("stored_last")
        block = cx.enter_context(nc.Block())

        @block.sync
        def _(sp):
            for ch in range(SC):
                sp.dma_start(r_sb[ch][:], token_rows(routed, ch)).then_inc(loaded[ch], 16)
            for ch in range(SC):
                sp.wait_ge(summed, ch + 1)
                sp.dma_start(token_rows(out, ch), r_sb[ch][:]).then_inc(stored, 16)
            sp.wait_ge(stored, 16 * SC)

        @block.vector
        def _(dve):
            for ch in range(SC):
                dve.wait_ge(loaded[ch], 16)
                nc.vector.tensor_tensor(r_sb[ch][:], c.X[:, ch * CW:(ch + 1) * CW, :], r_sb[ch][:], ALU.add)\
                  .then_inc(summed, 1)


def hybrid_layer(nc, x, Wq, bq, Wk, bk, Wv, bv, Wo, bo, W_up, W_v, W_proj, identity, W_scan_raw, Wg, w1, w2, out):
    q_parts = nc.dram_tensor("q_parts", [3, P, N], bf16).ap()
    k_parts = nc.dram_tensor("k_parts", [3, P, N], bf16).ap()
    max_dram = nc.dram_tensor("max_rows_dram", [2, NT // B, P], bf16).ap()
    dispatched = [nc.dram_tensor(f"dispatched{k}", [2 * N, ROW], fp32).ap() for k in range(2)]
    routed = [nc.dram_tensor(f"routed{k}", [2 * N, D], fp32).ap() for k in range(2)]
    scanned = [nc.dram_tensor(f"scanned{k}", [B * (PAD + T), D], fp32).ap() for k in range(2)]

    class Shared:
        pass

    c = Shared()
    with ExitStack() as cx:
        constants(nc, cx, c)
        with ExitStack() as cx_attention:
            attention_tensors(nc, cx_attention, c)
            project(nc, c, x, Wq, bq, Wk, bk, Wv, bv, Wo, bo, W_scan_raw, q_parts, k_parts)
            attend(nc, c, q_parts, k_parts, max_dram)
            project_out(nc, c)
        moe(nc, c, "m0", Wg, w1, w2, dispatched[0], routed[0])
        with ExitStack() as cx_scan:
            scan_tensors(nc, cx_scan, c)
            scan_inputs(nc, c, routed[0][0:N, :], W_up, W_v, W_proj, identity, scanned)
            scan(nc, c, scanned)
            scan_outputs(nc, c)
        moe(nc, c, "m1", Wg, w1, w2, dispatched[1], routed[1])
        final_sum(nc, c, routed[1][0:N, :], out)


_INS = ["L0_attn_a_x", "L0_attn_a_Wq", "L0_attn_a_bq", "L0_attn_a_Wk", "L0_attn_a_bk", "L0_attn_a_Wv", "L0_attn_a_bv",
        "L0_attn_a_Wo", "L0_attn_a_bo", "L0_attn_b_W_up", "L0_attn_b_W_v", "L0_attn_b_W_proj", "L0_attn_b_identity",
        "L0_attn_b_W_scan_raw", "L0_ffn_Wg", "L0_ffn_w1", "L0_ffn_w2"]


def kernel(**inputs):
    import numpy as _np
    import concourse.bacc as _bacc
    from concourse import mybir as _mybir
    from concourse.bass_utils import run_bass_kernel_spmd as _run

    nc = _bacc.Bacc("TRN2", target_bir_lowering=False, num_devices=1)
    arrays, args = {}, []
    for name in _INS:
        a = _np.ascontiguousarray(inputs[name])
        if name == "L0_attn_a_x":
            a = a.reshape(N, D)
        arrays[f"in_{name}_dram"] = a
        args.append(nc.dram_tensor(f"in_{name}_dram", a.shape, _mybir.dt.from_np(a.dtype), kind="ExternalInput").ap())
    out = nc.dram_tensor("out_0_dram", (N, D), fp32, kind="ExternalOutput").ap()
    hybrid_layer(nc, *args, out)
    r = _run(nc, [arrays], core_ids=[0])
    return r.results[0]["out_0_dram"].reshape(B, T, D)
```
